# Optimizing a Trainium2 kernel written in Bass

```python
import numpy as np
import jax
import jax.numpy as jnp

def _softmax(x, axis=-1):
    return jax.nn.softmax(x, axis=axis)

def _gelu(x):
    return jax.nn.gelu(x, approximate=True)

def _silu(x):
    return jax.nn.silu(x)

def _sigmoid(x):
    return jax.nn.sigmoid(x)

def _layernorm(x, axis=-1, eps=1e-05):
    m = jnp.mean(x, axis=axis, keepdims=True)
    v = jnp.var(x, axis=axis, keepdims=True)
    return (x - m) / jnp.sqrt(v + eps)

def _scatter_add(tgt, idx, src, axis=0):
    return tgt.at[idx].add(src)

def _segment_sum(src, seg, n):
    return jax.ops.segment_sum(src, seg, n)
kernel_name = 'mk_gnn_ffn_d2_gnn_r32_fc61fc'

def setup_inputs(seed: int=0):
    np.random.seed(seed)
    _w = jnp.asarray

    def _rec_inputs():
        import jax
        import jax.numpy as jnp
        _gk = jax.random.key(seed)
        x = -0.0006008 + 1.001 * jax.random.normal(jax.random.fold_in(_gk, 1), (3125, 256), jnp.float32)
        src = jax.random.randint(jax.random.fold_in(_gk, 2), (50000,), 0, 3125, jnp.int32)
        dst = jnp.minimum((3125 * jax.random.uniform(jax.random.fold_in(_gk, 3), (50000,)) ** 2.0).astype(jnp.int32), 99999)
        _o = jnp.argsort(dst, stable=True)
        src = src[_o]
        dst = dst[_o]
        edge_weight = -0.00278149 + 0.998712 * jax.random.normal(jax.random.fold_in(_gk, 12), (50000,), jnp.float32)
        return (x, src, dst, edge_weight)
    x, src, dst, edge_weight = _rec_inputs()

    def _L0_gnn_setup():
        import jax, jax.numpy as jnp
        import numpy as np
        N = 10000
        E = 10000
        D = 256
        EPS = 1e-05

        def layer_norm(x, g, b):
            mu = jnp.mean(x, axis=-1, keepdims=True)
            var = jnp.mean(jnp.square(x - mu), axis=-1, keepdims=True)
            return (x - mu) * jax.lax.rsqrt(var + EPS) * g + b

        def linear(x, w, b):
            return x @ w + b
        key = jax.random.key(seed)
        ks = jax.random.split(key, 20)
        s = 1.0 / np.sqrt(D)
        inp = {'x': jax.random.normal(ks[0], (N, D), jnp.float32), 'edge_index': jax.random.randint(ks[1], (2, E), 0, N, jnp.int64), 'edge_weight': jax.random.normal(ks[2], (E,), jnp.float32), 'wq': jax.random.normal(ks[3], (D, D), jnp.float32) * s, 'bq': jnp.zeros((D,), jnp.float32), 'wk': jax.random.normal(ks[4], (D, D), jnp.float32) * s, 'bk': jnp.zeros((D,), jnp.float32), 'wv': jax.random.normal(ks[5], (D, D), jnp.float32) * s, 'bv': jnp.zeros((D,), jnp.float32), 'ws': jax.random.normal(ks[6], (D, D), jnp.float32) * s, 'bs': jnp.zeros((D,), jnp.float32), 'we': jax.random.normal(ks[7], (1, 1), jnp.float32), 'be': jnp.zeros((1,), jnp.float32), 'g1': jnp.ones((D,), jnp.float32), 'b1': jnp.zeros((D,), jnp.float32), 'g2': jnp.ones((D,), jnp.float32), 'b2': jnp.zeros((D,), jnp.float32), 'w_ff1': jax.random.normal(ks[8], (D, 2 * D), jnp.float32) * s, 'b_ff1': jnp.zeros((2 * D,), jnp.float32), 'w_ff2': jax.random.normal(ks[9], (2 * D, D), jnp.float32) * (1.0 / np.sqrt(2 * D)), 'b_ff2': jnp.zeros((D,), jnp.float32)}
        return inp
    _L0_gnn_all = _L0_gnn_setup()
    _L0_gnn_in = {k: v for k, v in _L0_gnn_all.items() if k in ('wq', 'bq', 'wk', 'bk', 'wv', 'bv', 'ws', 'bs', 'we', 'be', 'g1', 'b1', 'g2', 'b2', 'w_ff1', 'b_ff1', 'w_ff2', 'b_ff2')}
    del _L0_gnn_all

    def _L0_ffn_setup():
        import jax, jax.numpy as jnp
        import numpy as np
        C = 256
        HID = 1024
        E = 8
        TEMP = 1.0
        key = jax.random.key(seed)
        ks = jax.random.split(key, 7)
        x = jax.random.normal(ks[0], (8, 512, C), dtype=jnp.float32)
        W1 = jax.random.normal(ks[1], (C, HID), dtype=jnp.float32) * 0.02
        b1 = jnp.zeros((HID,), dtype=jnp.float32)
        Wg = jax.random.normal(ks[2], (HID, E), dtype=jnp.float32) * 0.02
        bg = jnp.zeros((E,), dtype=jnp.float32)
        Wd = jax.random.normal(ks[3], (E, HID, C), dtype=jnp.float32) * 0.02
        bd = jnp.zeros((E, C), dtype=jnp.float32)
        return {'x': x, 'W1': W1, 'b1': b1, 'Wg': Wg, 'bg': bg, 'Wd': Wd, 'bd': bd}
    _L0_ffn_all = _L0_ffn_setup()
    _L0_ffn_in = {k: v for k, v in _L0_ffn_all.items() if k in ('W1', 'b1', 'Wg', 'bg', 'Wd', 'bd')}
    del _L0_ffn_all

    def _L1_gnn_setup():
        import jax, jax.numpy as jnp
        import numpy as np
        NEG_SLOPE = 0.2

        def gatv2_layer(x, Wl, Wr, att, bias, src, dst, n_nodes, heads, ch, concat):
            xl = (x @ Wl).reshape(n_nodes, heads, ch)
            xr = (x @ Wr).reshape(n_nodes, heads, ch)
            m = xl[src] + xr[dst]
            e = jax.nn.leaky_relu(m, NEG_SLOPE)
            logits = jnp.einsum('ehc,hc->eh', e, att)
            mx = jax.ops.segment_max(logits, dst, num_segments=n_nodes)
            ex = jnp.exp(logits - mx[dst])
            denom = jax.ops.segment_sum(ex, dst, num_segments=n_nodes)
            alpha = ex / denom[dst]
            out = jax.ops.segment_sum(alpha[:, :, None] * xl[src], dst, num_segments=n_nodes)
            if concat:
                out = out.reshape(n_nodes, heads * ch)
            else:
                out = out.mean(axis=1)
            return out + bias
        N, E = (50000, 25000)
        IN, HID, OUT, H = (256, 64, 256, 4)
        key = jax.random.key(seed)
        ks = jax.random.split(key, 12)
        s = lambda fan_in: 1.0 / np.sqrt(fan_in)
        return {'x': jax.random.normal(ks[0], (N, IN), dtype=jnp.float32), 'edge_index': jax.random.randint(ks[1], (2, E), 0, N, dtype=jnp.int64), 'Wl1': jax.random.normal(ks[2], (IN, H * HID), jnp.float32) * s(IN), 'Wr1': jax.random.normal(ks[3], (IN, H * HID), jnp.float32) * s(IN), 'att1': jax.random.normal(ks[4], (H, HID), jnp.float32) * s(HID), 'b1': jnp.zeros((H * HID,), jnp.float32), 'Wl2': jax.random.normal(ks[5], (H * HID, OUT), jnp.float32) * s(H * HID), 'Wr2': jax.random.normal(ks[6], (H * HID, OUT), jnp.float32) * s(H * HID), 'att2': jax.random.normal(ks[7], (1, OUT), jnp.float32) * s(OUT), 'b2': jnp.zeros((OUT,), jnp.float32)}
    _L1_gnn_all = _L1_gnn_setup()
    _L1_gnn_in = {k: v for k, v in _L1_gnn_all.items() if k in ('Wl1', 'Wr1', 'att1', 'b1', 'Wl2', 'Wr2', 'att2', 'b2')}
    del _L1_gnn_all

    def _L1_ffn_setup():
        import jax, jax.numpy as jnp
        import numpy as np
        TOP_K = 2
        LN_EPS = 1e-05
        key = jax.random.key(seed)
        ks = jax.random.split(key, 8)
        B, S, D, E, H = (16, 1024, 256, 8, 1024)
        x = jax.random.normal(ks[0], (B, S, D), dtype=jnp.float32)
        Wr = jax.random.normal(ks[1], (D, E), dtype=jnp.float32) * 0.1
        br = jnp.zeros((E,), dtype=jnp.float32)
        ln_g = jnp.ones((E, D), dtype=jnp.float32)
        ln_b = jnp.zeros((E, D), dtype=jnp.float32)
        W1 = jax.random.normal(ks[2], (E, D, H), dtype=jnp.float32) * (1.0 / np.sqrt(D))
        b1 = jnp.zeros((E, H), dtype=jnp.float32)
        W2 = jax.random.normal(ks[3], (E, H, D), dtype=jnp.float32) * (1.0 / np.sqrt(H))
        b2 = jnp.zeros((E, D), dtype=jnp.float32)
        return {'x': x, 'Wr': Wr, 'br': br, 'ln_g': ln_g, 'ln_b': ln_b, 'W1': W1, 'b1': b1, 'W2': W2, 'b2': b2}
    _L1_ffn_all = _L1_ffn_setup()
    _L1_ffn_in = {k: v for k, v in _L1_ffn_all.items() if k in ('Wr', 'br', 'ln_g', 'ln_b', 'W1', 'b1', 'W2', 'b2')}
    del _L1_ffn_all
    return {'x': x, 'src': src, 'dst': dst, 'edge_weight': edge_weight, 'L0_gnn_wq': _L0_gnn_in['wq'], 'L0_gnn_bq': _L0_gnn_in['bq'], 'L0_gnn_wk': _L0_gnn_in['wk'], 'L0_gnn_bk': _L0_gnn_in['bk'], 'L0_gnn_wv': _L0_gnn_in['wv'], 'L0_gnn_bv': _L0_gnn_in['bv'], 'L0_gnn_ws': _L0_gnn_in['ws'], 'L0_gnn_bs': _L0_gnn_in['bs'], 'L0_gnn_we': _L0_gnn_in['we'], 'L0_gnn_be': _L0_gnn_in['be'], 'L0_gnn_g1': _L0_gnn_in['g1'], 'L0_gnn_b1': _L0_gnn_in['b1'], 'L0_gnn_g2': _L0_gnn_in['g2'], 'L0_gnn_b2': _L0_gnn_in['b2'], 'L0_gnn_w_ff1': _L0_gnn_in['w_ff1'], 'L0_gnn_b_ff1': _L0_gnn_in['b_ff1'], 'L0_gnn_w_ff2': _L0_gnn_in['w_ff2'], 'L0_gnn_b_ff2': _L0_gnn_in['b_ff2'], 'L0_ffn_W1': _L0_ffn_in['W1'], 'L0_ffn_b1': _L0_ffn_in['b1'], 'L0_ffn_Wg': _L0_ffn_in['Wg'], 'L0_ffn_bg': _L0_ffn_in['bg'], 'L0_ffn_Wd': _L0_ffn_in['Wd'], 'L0_ffn_bd': _L0_ffn_in['bd'], 'L1_gnn_Wl1': _L1_gnn_in['Wl1'], 'L1_gnn_Wr1': _L1_gnn_in['Wr1'], 'L1_gnn_att1': _L1_gnn_in['att1'], 'L1_gnn_b1': _L1_gnn_in['b1'], 'L1_gnn_Wl2': _L1_gnn_in['Wl2'], 'L1_gnn_Wr2': _L1_gnn_in['Wr2'], 'L1_gnn_att2': _L1_gnn_in['att2'], 'L1_gnn_b2': _L1_gnn_in['b2'], 'L1_ffn_Wr': _L1_ffn_in['Wr'], 'L1_ffn_br': _L1_ffn_in['br'], 'L1_ffn_ln_g': _L1_ffn_in['ln_g'], 'L1_ffn_ln_b': _L1_ffn_in['ln_b'], 'L1_ffn_W1': _L1_ffn_in['W1'], 'L1_ffn_b1': _L1_ffn_in['b1'], 'L1_ffn_W2': _L1_ffn_in['W2'], 'L1_ffn_b2': _L1_ffn_in['b2']}

def reference(x, src, dst, edge_weight, L0_gnn_wq, L0_gnn_bq, L0_gnn_wk, L0_gnn_bk, L0_gnn_wv, L0_gnn_bv, L0_gnn_ws, L0_gnn_bs, L0_gnn_we, L0_gnn_be, L0_gnn_g1, L0_gnn_b1, L0_gnn_g2, L0_gnn_b2, L0_gnn_w_ff1, L0_gnn_b_ff1, L0_gnn_w_ff2, L0_gnn_b_ff2, L0_ffn_W1, L0_ffn_b1, L0_ffn_Wg, L0_ffn_bg, L0_ffn_Wd, L0_ffn_bd, L1_gnn_Wl1, L1_gnn_Wr1, L1_gnn_att1, L1_gnn_b1, L1_gnn_Wl2, L1_gnn_Wr2, L1_gnn_att2, L1_gnn_b2, L1_ffn_Wr, L1_ffn_br, L1_ffn_ln_g, L1_ffn_ln_b, L1_ffn_W1, L1_ffn_b1, L1_ffn_W2, L1_ffn_b2):
    import jax
    import jax.numpy as jnp

    def _L0_gnn_ref(x, edge_index, edge_weight, wq, bq, wk, bk, wv, bv, ws, bs, we, be, g1, b1, g2, b2, w_ff1, b_ff1, w_ff2, b_ff2):
        import jax, jax.numpy as jnp
        import numpy as np
        N = 10000
        E = 10000
        D = 256
        EPS = 1e-05

        def layer_norm(x, g, b):
            mu = jnp.mean(x, axis=-1, keepdims=True)
            var = jnp.mean(jnp.square(x - mu), axis=-1, keepdims=True)
            return (x - mu) * jax.lax.rsqrt(var + EPS) * g + b

        def linear(x, w, b):
            return x @ w + b
        n = x.shape[0]
        scale = x.shape[-1] ** (-0.5)
        q = linear(x, wq, bq)
        k = linear(x, wk, bk)
        v = linear(x, wv, bv)
        src, dst = (edge_index[0], edge_index[1])
        scores = jnp.sum(q[dst] * k[src], axis=-1) * scale
        scores = scores + (edge_weight[:, None] @ we + be)[:, 0]
        seg_max = jax.ops.segment_max(scores, dst, num_segments=n)
        exp_s = jnp.exp(scores - seg_max[dst])
        denom = jax.ops.segment_sum(exp_s, dst, num_segments=n)
        attn = exp_s / jnp.maximum(denom[dst], 1e-12)
        message = v[src] * attn[:, None]
        out = jax.ops.segment_sum(message, dst, num_segments=n)
        x = layer_norm(x + out + linear(x, ws, bs), g1, b1)
        ffn = linear(jax.nn.gelu(linear(x, w_ff1, b_ff1)), w_ff2, b_ff2)
        x = layer_norm(x + ffn, g2, b2)
        return x

    def _L0_ffn_ref(x, W1, b1, Wg, bg, Wd, bd):
        import jax, jax.numpy as jnp
        import numpy as np
        C = 256
        HID = 1024
        E = 8
        TEMP = 1.0
        orig_shape = x.shape
        xf = x.reshape(-1, orig_shape[-1])
        H = jax.nn.gelu(xf @ W1 + b1, approximate=False)
        probs = jax.nn.softmax((H @ Wg + bg) / TEMP, axis=-1)
        assign = jnp.argmax(probs, axis=-1)
        out = jnp.zeros_like(xf)
        for e in range(Wd.shape[0]):
            y = H @ Wd[e] + bd[e]
            sel = (assign == e)[:, None]
            out = out + jnp.where(sel, probs[:, e:e + 1] * y, 0.0)
        return out.reshape(orig_shape)

    def _L1_gnn_ref(x, edge_index, Wl1, Wr1, att1, b1, Wl2, Wr2, att2, b2):
        import jax, jax.numpy as jnp
        import numpy as np
        NEG_SLOPE = 0.2

        def gatv2_layer(x, Wl, Wr, att, bias, src, dst, n_nodes, heads, ch, concat):
            xl = (x @ Wl).reshape(n_nodes, heads, ch)
            xr = (x @ Wr).reshape(n_nodes, heads, ch)
            m = xl[src] + xr[dst]
            e = jax.nn.leaky_relu(m, NEG_SLOPE)
            logits = jnp.einsum('ehc,hc->eh', e, att)
            mx = jax.ops.segment_max(logits, dst, num_segments=n_nodes)
            ex = jnp.exp(logits - mx[dst])
            denom = jax.ops.segment_sum(ex, dst, num_segments=n_nodes)
            alpha = ex / denom[dst]
            out = jax.ops.segment_sum(alpha[:, :, None] * xl[src], dst, num_segments=n_nodes)
            if concat:
                out = out.reshape(n_nodes, heads * ch)
            else:
                out = out.mean(axis=1)
            return out + bias
        N = x.shape[0]
        loops = jnp.arange(N, dtype=edge_index.dtype)
        src = jnp.concatenate([edge_index[0], loops])
        dst = jnp.concatenate([edge_index[1], loops])
        h = gatv2_layer(x, Wl1, Wr1, att1, b1, src, dst, N, 4, 64, concat=True)
        h = jax.nn.elu(h)
        out = gatv2_layer(h, Wl2, Wr2, att2, b2, src, dst, N, 1, 256, concat=False)
        return out

    def _L1_ffn_ref(x, Wr, br, ln_g, ln_b, W1, b1, W2, b2):
        import jax, jax.numpy as jnp
        import numpy as np
        TOP_K = 2
        LN_EPS = 1e-05
        B, S, D = x.shape
        N = B * S
        xt = x.reshape(N, D)
        logits = xt @ Wr + br
        probs = jax.nn.softmax(logits, axis=-1)
        top_p, top_idx = jax.lax.top_k(probs, TOP_K)
        weights = top_p / top_p.sum(axis=-1, keepdims=True)
        mu = xt.mean(axis=-1, keepdims=True)
        var = ((xt - mu) ** 2).mean(axis=-1, keepdims=True)
        xn = (xt - mu) * jax.lax.rsqrt(var + LN_EPS)
        xe = xn[None, :, :] * ln_g[:, None, :] + ln_b[:, None, :]
        h = jax.nn.gelu(jnp.einsum('end,edh->enh', xe, W1) + b1[:, None, :], approximate=False)
        y = jnp.einsum('enh,ehd->end', h, W2) + b2[:, None, :]
        y_tok = jnp.transpose(y, (1, 0, 2))
        sel = jnp.take_along_axis(y_tok, top_idx[:, :, None], axis=1)
        out = (weights[:, :, None] * sel).sum(axis=1)
        return out.reshape(B, S, D)
    edge_index = jnp.stack([src, dst])
    x = x + _L0_gnn_ref(_layernorm(x, axis=-1), edge_index, edge_weight, L0_gnn_wq, L0_gnn_bq, L0_gnn_wk, L0_gnn_bk, L0_gnn_wv, L0_gnn_bv, L0_gnn_ws, L0_gnn_bs, L0_gnn_we, L0_gnn_be, L0_gnn_g1, L0_gnn_b1, L0_gnn_g2, L0_gnn_b2, L0_gnn_w_ff1, L0_gnn_b_ff1, L0_gnn_w_ff2, L0_gnn_b_ff2)
    x = x + _L0_ffn_ref(_layernorm(x, axis=-1)[None], L0_ffn_W1, L0_ffn_b1, L0_ffn_Wg, L0_ffn_bg, L0_ffn_Wd, L0_ffn_bd)[0]
    x = x + _L1_gnn_ref(_layernorm(x, axis=-1), edge_index, L1_gnn_Wl1, L1_gnn_Wr1, L1_gnn_att1, L1_gnn_b1, L1_gnn_Wl2, L1_gnn_Wr2, L1_gnn_att2, L1_gnn_b2)
    x = x + _L1_ffn_ref(_layernorm(x, axis=-1)[None], L1_ffn_Wr, L1_ffn_br, L1_ffn_ln_g, L1_ffn_ln_b, L1_ffn_W1, L1_ffn_b1, L1_ffn_W2, L1_ffn_b2)[0]
    return x

_drawn_inputs = setup_inputs


def setup_inputs(seed=0):
    import zlib

    import numpy as np

    out = dict(_drawn_inputs(seed))
    spreads = {'L0_gnn_bq': (0.0, 0.334),
     'L0_gnn_bk': (0.0, 2.0),
     'L0_gnn_bv': (0.0, 0.1),
     'L0_gnn_bs': (0.0, 0.1),
     'L0_gnn_g1': (1.0, 0.2),
     'L0_gnn_b1': (0.0, 0.1),
     'L0_gnn_g2': (1.0, 0.2),
     'L0_gnn_b2': (0.0, 0.1),
     'L0_gnn_b_ff1': (0.0, 0.1),
     'L0_gnn_b_ff2': (0.0, 0.1),
     'L0_ffn_b1': (0.0, 0.532),
     'L0_ffn_bg': (0.0, 0.367),
     'L0_ffn_bd': (0.0, 0.438),
     'L1_gnn_b1': (0.0, 0.1),
     'L1_gnn_b2': (0.0, 0.1),
     'L1_ffn_br': (0.0, 0.1),
     'L1_ffn_ln_g': (1.0, 0.2),
     'L1_ffn_ln_b': (0.0, 0.282),
     'L1_ffn_b1': (0.0, 0.276),
     'L1_ffn_b2': (0.0, 0.1)}
    factors = {'edge_weight': 3.694,
     'L0_ffn_W1': 2.865,
     'L0_ffn_Wg': 2.941,
     'L0_ffn_Wd': 3.447,
     'L1_gnn_Wr1': 2.725,
     'L1_gnn_Wr2': 4.766,
     'L1_gnn_att2': 2.917}
    for name, (base, spread) in spreads.items():
        noise = np.random.default_rng([zlib.crc32(name.encode()), seed]).standard_normal(out[name].shape)
        drawn = base * np.exp(spread * noise) if base else spread * noise
        out[name] = jnp.asarray(drawn.astype(out[name].dtype))
    for name, factor in factors.items():
        out[name] = (out[name] * factor).astype(out[name].dtype)
    return out
```

```python
from contextlib import ExitStack, contextmanager

import numpy as np

import concourse.bass as bass
from concourse import mybir

ALU = mybir.AluOpType
ACT = mybir.ActivationFunctionType
AX = mybir.AxisListType
F32 = mybir.dt.float32
BF16 = mybir.dt.bfloat16
U32 = mybir.dt.uint32
I32 = mybir.dt.int32

P = 128
N = 3125
D = 256
KD = D // P
NT = -(-N // P)
NPAD = NT * P
LAST = N - (NT - 1) * P
E = 50000
EP, EJ = 125, 400
EB = 256
NB = -(-E // EB)
STEPS = NB + NT - 1
EPAD = NB * EB
HB = NB // 2
BIG = float(2 ** 100)
NOWHERE = float(2 ** 20)
TILE_BITS, FIELDS = 5, 6
UNROLL = 5
EPS = 1e-5
HID0, HID1, EXP = 1024, 1024, 8
TOP1_TILES = (N + EXP * (P - 1)) // P
TOP2_TILES = (2 * N + EXP * (P - 1)) // P


class Core:

    def __init__(self, nc):
        self.nc = nc
        self.keep = ExitStack()
        self.gp_dma = [self.keep.enter_context(nc.semaphore(f"gp_dma{k}")) for k in range(5)]

    @contextmanager
    def scope(self):
        outer, self.keep = self.keep, ExitStack()
        with self.keep:
            yield
        self.keep = outer

    def sbuf(self, name, shape, dt=F32):
        return self.keep.enter_context(self.nc.sbuf_tensor("kept_" + name, shape, dt))


@contextmanager
def phase(co, name):
    nc = co.nc
    sems, gp_dma = [], []
    with ExitStack() as ctx:
        class Ph:
            def sb(self, n, shape, dt=F32):
                return ctx.enter_context(nc.sbuf_tensor(f"{name}_{n}", shape, dt))

            def ps(self, n, shape, dt=F32):
                return ctx.enter_context(nc.psum_tensor(f"{name}_{n}", shape, dt))

            def sem(self, n):
                s = ctx.enter_context(nc.semaphore(f"{name}_{n}"))
                sems.append(s)
                return s

            def gp_dma_sem(self, k):
                gp_dma.append(co.gp_dma[k])
                return co.gp_dma[k]

        yield Ph()
        for s in sems:
            nc.sync.sem_clear(s)
        if gp_dma:
            nc.gpsimd.dma_reset()
        for s in gp_dma:
            nc.gpsimd.sem_clear(s)
        nc.all_engine_barrier()


def constants(nc, co):
    co.ident = co.sbuf("ident", [P, P])
    co.identb = co.sbuf("identb", [P, P], BF16)
    co.bigident = co.sbuf("bigident", [P, P], BF16)
    co.before = co.sbuf("before", [P, P])
    co.ones = co.sbuf("ones", [P, P])
    co.iota = co.sbuf("iota", [P, STEPS])
    co.iotab = co.sbuf("iotab", [P, P], BF16)
    co.rowno = co.sbuf("rowno", [P, 1])
    co.ones3 = co.sbuf("ones3", [3, P], BF16)
    with phase(co, "const") as ph:
        done = ph.sem("done")
        base = ph.sem("base")
        with nc.Block() as block:
            @block.gpsimd
            def _(gp):
                gp.memset(co.ident[:, :], 0.0).then_inc(base, 1)
                gp.memset(co.ones[:, :], 1.0).then_inc(base, 1)
                gp.iota(co.iota[:, :], pattern=[[1, STEPS]], base=0, channel_multiplier=0,
                        allow_small_or_imprecise_dtypes=True).then_inc(base, 1)
                gp.iota(co.rowno[:, :], pattern=[[0, 1]], base=0, channel_multiplier=1,
                        allow_small_or_imprecise_dtypes=True).then_inc(base, 1)
                gp.wait_ge(base, 4)
                gp.affine_select(out=co.before[:, :], in_=co.ones[:, :], compare_op=ALU.is_gt, fill=0.0,
                                 base=0, pattern=[[1, P]], channel_multiplier=-1).then_inc(base, 1)
                gp.affine_select(out=co.ident[:, :], in_=co.ident[:, :], compare_op=ALU.not_equal, fill=1.0,
                                 base=0, pattern=[[-1, P]], channel_multiplier=1).then_inc(base, 1)

            @block.vector
            def _(dve):
                dve.wait_ge(base, 6)
                dve.tensor_copy(co.identb[:, :], co.ident[:, :]).then_inc(done, 1)
                dve.tensor_scalar(co.bigident[:, :], co.ident[:, :], BIG, None, ALU.mult).then_inc(done, 1)
                dve.tensor_copy(co.iotab[:, :], co.iota[:, 0:P]).then_inc(done, 1)
                dve.memset(co.ones3[:, :], 1.0).then_inc(done, 1)
                dve.wait_ge(done, 4)


def sort_edges(nc, co, dst, src, weight, sdst, ssrc, sweight):
    co.count = co.sbuf("count", [NT, 1])
    co.first = co.sbuf("first", [NT, 1])
    with phase(co, "sort") as ph:
        d = ph.sb("d", [EP, EJ], I32)
        s = ph.sb("s", [EP, EJ], U32)
        w = ph.sb("w", [EP, EJ])
        bucket_i = ph.sb("bucket_i", [EP, EJ], I32)
        bucket = ph.sb("bucket", [EP, EJ + 1])
        next_i = ph.sb("next_i", [EP, 2], I32)
        member = ph.sb("member", [EP, EJ])
        rank = ph.sb("rank", [EP, EJ])
        slot = ph.sb("slot", [EP, EJ])
        slot_u = ph.sb("slot_u", [EP, EJ], U32)
        cnt = ph.sb("cnt", [EP, NT])
        excl = ph.sb("excl", [EP, NT])
        zero = ph.sb("zero", [EP, NT])
        offset = ph.sb("offset", [EP, NT])
        falls = ph.sb("falls", [EP, EJ])
        bad = ph.sb("bad", [EP, 1])
        flag = ph.sb("flag", [1, 1], I32)
        stage_i = ph.sb("stage_i", [EP, 1], U32)
        stage_d = ph.sb("stage_d", [EP, 1], I32)
        stage_s = ph.sb("stage_s", [EP, 1], U32)
        stage_w = ph.sb("stage_w", [EP, 1])
        pad = ph.sb("pad", [1, EPAD - E], I32)
        padz = ph.sb("padz", [1, EPAD - E], I32)
        psum = ph.ps("psum", [P, 512])
        loaded, chain, mm, copied, flagged = (ph.sem(n) for n in ("loaded", "chain", "mm", "copied", "flagged"))
        slots, staged, tick, padded = (ph.sem(n) for n in ("slots", "staged", "tick", "padded"))
        placed = ph.gp_dma_sem(0)
        with nc.Block() as block:
            @block.sync
            def _(sp):
                sp.dma_start(d[:, :], dst.rearrange("(p j) -> p j", j=EJ)).then_inc(loaded, 16)
                with nc.allow_non_contiguous_dma(reason="one edge of each row"):
                    sp.dma_start(next_i[0:EP - 1, 0:1], dst[EJ:E].rearrange("(p j) -> p j", j=EJ)[:, 0:1]).then_inc(loaded, 16)
                    sp.dma_start(next_i[EP - 1:EP, 0:1], dst[E - 1:E].rearrange("(p j) -> p j", j=1)).then_inc(loaded, 16)
                sp.dma_start(s[:, :], src.rearrange("(p j) -> p j", j=EJ)).then_inc(loaded, 16)
                sp.dma_start(w[:, :], weight.rearrange("(p j) -> p j", j=EJ)).then_inc(loaded, 16)
                sp.wait_ge(copied, 2)
                sp.dma_start(sdst[E:EPAD].rearrange("(a b) -> a b", a=1), pad[:, :]).then_inc(padded, 16)
                sp.dma_start(ssrc[E:EPAD].rearrange("(a b) -> a b", a=1), padz[:, :].bitcast(U32)).then_inc(padded, 16)
                sp.dma_start(sweight[E:EPAD].rearrange("(a b) -> a b", a=1), padz[:, :].bitcast(F32)).then_inc(padded, 16)
                sp.wait_ge(padded, 48)

            @block.vector
            def _(dve):
                dve.memset(pad[:, :], int(NOWHERE)).then_inc(copied, 1)
                dve.memset(padz[:, :], 0).then_inc(copied, 1)
                dve.memset(zero[:, :], 0.0).then_inc(chain, 1)
                dve.wait_ge(loaded, 80)
                dve.tensor_scalar(bucket_i[:, :], d[:, :], 7, None, ALU.arith_shift_right).then_inc(chain, 1)
                dve.tensor_scalar(next_i[:, 1:2], next_i[:, 0:1], 7, None, ALU.arith_shift_right).then_inc(chain, 1)
                dve.wait_ge(chain, 3)
                dve.tensor_copy(bucket[:, 0:EJ], bucket_i[:, :]).then_inc(chain, 1)
                dve.tensor_copy(bucket[:, EJ:EJ + 1], next_i[:, 1:2]).then_inc(chain, 1)
                dve.wait_ge(chain, 5)
                dve.tensor_tensor(falls[:, :], bucket[:, 0:EJ], bucket[:, 1:EJ + 1], ALU.is_gt).then_inc(chain, 1)
                for b in range(NT):
                    dve.wait_ge(chain, 6 + b)
                    dve.tensor_scalar(member[:, :], bucket[:, 0:EJ], float(b), None, ALU.is_equal, ALU.add,
                                      accum_out=cnt[:, b:b + 1]).then_inc(chain, 1)
                dve.wait_ge(chain, 6 + NT)
                dve.reduce_max(bad[:, :], falls[:, :], AX.X).then_inc(chain, 1)
                dve.tensor_tensor_scan(excl[:, :], cnt[:, :], zero[:, :], 0.0, ALU.add, ALU.add).then_inc(chain, 1)
                dve.wait_ge(chain, 8 + NT)
                dve.tensor_tensor(excl[:, :], excl[:, :], cnt[:, :], ALU.subtract).then_inc(chain, 1)
                dve.wait_ge(mm, 1)
                dve.tensor_copy(co.count[:, :], psum[0:NT, 0:1]).then_inc(copied, 1)
                dve.wait_ge(mm, 2)
                dve.tensor_copy(offset[:, :], psum[0:EP, 64:64 + NT]).then_inc(copied, 1)
                dve.tensor_copy(co.first[:, :], psum[0:NT, 128:129]).then_inc(copied, 1)
                dve.tensor_copy(flag[:, :], psum[0:1, 192:193]).then_inc(flagged, 1)
                dve.wait_ge(flagged, 1)
                unsorted = dve.value_load(flag[0:1, 0:1], min_val=0, max_val=EP)
                with dve.If(unsorted > 0):
                    dve.memset(slot[:, :], 0.0).then_inc(slots, 1)
                    dve.wait_ge(copied, 5)
                    for b in range(NT):
                        dve.tensor_scalar(member[:, :], bucket[:, 0:EJ], float(b), None, ALU.is_equal).then_inc(slots, 1)
                        dve.wait_ge(slots, 4 * b + 2)
                        dve.tensor_tensor_scan(rank[:, :], member[:, :], member[:, :], 0.0, ALU.add, ALU.bypass).then_inc(slots, 1)
                        dve.wait_ge(slots, 4 * b + 3)
                        dve.scalar_tensor_tensor(out=rank[:, :], in0=rank[:, :], scalar=offset[:, b:b + 1],
                                                 in1=member[:, :], op0=ALU.add, op1=ALU.mult).then_inc(slots, 1)
                        dve.wait_ge(slots, 4 * b + 4)
                        dve.tensor_tensor(slot[:, :], slot[:, :], rank[:, :], ALU.add).then_inc(slots, 1)
                        dve.wait_ge(slots, 4 * b + 5)
                    dve.tensor_scalar(slot_u[:, :], slot[:, :], -1.0, None, ALU.add).then_inc(slots, 1)
                with dve.Else():
                    dve.memset(slot[:, 0:1], 0.0).then_inc(slots, 1)

            @block.tensor
            def _(pe):
                pe.wait_ge(chain, 6 + NT)
                pe.matmul(psum[0:NT, 0:1], cnt[:, :], co.ones[0:EP, 0:1], start=True, stop=True).then_inc(mm, 1)
                pe.wait_ge(chain, 9 + NT)
                pe.wait_ge(copied, 3)
                pe.matmul(psum[0:EP, 64:64 + NT], co.before[0:EP, 0:EP], cnt[:, :], start=True, stop=False)
                pe.matmul(psum[0:EP, 64:64 + NT], co.ones[0:EP, 0:EP], excl[:, :], start=False, stop=True)
                pe.matmul(psum[0:NT, 128:129], co.before[0:NT, 0:NT], co.count[:, :], start=True, stop=True)
                pe.matmul(psum[0:1, 192:193], bad[:, :], co.ones[0:EP, 0:1], start=True, stop=True).then_inc(mm, 1)

            @block.gpsimd
            def _(gp):
                gp.wait_ge(flagged, 1)
                unsorted = gp.value_load(flag[0:1, 0:1], min_val=0, max_val=EP)
                with gp.If(unsorted > 0):
                    gp.wait_ge(slots, 4 * NT + 2)
                    gp.sem_inc(tick, 1)
                    with gp.Fori(0, EJ) as j:
                        gp.tensor_copy(stage_i[:, :], slot_u[:, bass.ds(j, 1)]).then_inc(staged, 1)
                        gp.tensor_copy(stage_d[:, :], d[:, bass.ds(j, 1)]).then_inc(staged, 1)
                        gp.tensor_copy(stage_s[:, :], s[:, bass.ds(j, 1)]).then_inc(staged, 1)
                        gp.tensor_copy(stage_w[:, :], w[:, bass.ds(j, 1)]).then_inc(staged, 1)
                        gp.wait_ge(staged, 4 * j + 4)
                        gp.sem_inc(tick, 1)
                        for there, value in ((sdst, stage_d), (ssrc, stage_s), (sweight, stage_w)):
                            gp.indirect_dma_start(there[0:E].rearrange("(a b) -> a b", b=1),
                                                  bass.IndirectOffsetOnAxis(ap=stage_i[:, 0:1], axis=0),
                                                  value[:, :], None).then_inc(placed, 16)
                        gp.wait_ge(placed, 48 * j + 48)
                        gp.sem_inc(tick, 1)
                with gp.Else():
                    for there, value in ((sdst, d), (ssrc, s), (sweight, w)):
                        gp.dma_start(there[0:E].rearrange("(p j) -> p j", j=EJ), value[:, :]).then_inc(placed, 16)
                    gp.wait_ge(placed, 48)


def plan_steps(nc, co, sdst, ssrc, sweight, we, be):
    co.tiles = co.sbuf("tiles", [1, STEPS + UNROLL], I32)
    co.local = co.sbuf("local", [P, 2, STEPS])
    co.edge_src = co.sbuf("edge_src", [P, 2, STEPS], U32)
    co.edge_term = co.sbuf("edge_term", [P, 2, STEPS])
    with phase(co, "plan") as ph:
        raw = [ph.sb(f"raw{i}", [HB, 2, EB], I32) for i in range(3)]
        val = [ph.sb(f"val{i}", [HB, 2, EB]) for i in range(2)]
        wev = ph.sb("wev", [P, 2])
        lim_i, lim = ph.sb("lim_i", [NT, 4], I32), ph.sb("lim", [NT, 9])
        meets = ph.sb("meets", [NT, STEPS])
        row = ph.sb("row", [1, 5, STEPS])
        tile_of, moved = ph.sb("tile_of", [1, STEPS], I32), ph.sb("moved", [1, STEPS], I32)
        number = ph.sb("number", [HB, 2])
        chosen = ph.sb("chosen", [HB, 2, STEPS])
        shift = ph.sb("shift", [P, 1, STEPS])
        psum, psum2, psum3, psum4 = (ph.ps(f"psum{i}", [P, 512]) for i in range(4))
        psb = [ph.ps(f"psb{i}", [P, 2, 256]) for i in range(3)]
        loaded, chain, mm, brought, conv = (ph.sem(n) for n in ("loaded", "chain", "mm", "brought", "conv"))
        with nc.Block() as block:
            @block.sync
            def _(sp):
                for i, a in enumerate((sdst, ssrc, sweight)):
                    a = a if i == 0 else a.bitcast(I32)
                    sp.dma_start(raw[i][:, :, :], a[0:NB * EB].rearrange("(h t e) -> t h e", h=2, e=EB)).then_inc(loaded, 16)
                sp.dma_start(wev[:, 0:1], we.to_broadcast([P, 1])).then_inc(loaded, 16)
                sp.dma_start(wev[:, 1:2], be.rearrange("(a b) -> a b", b=1).to_broadcast([P, 1])).then_inc(loaded, 16)

            @block.vector
            def _(dve):
                n = [0]

                def step(ins):
                    n[0] += 1
                    ins.then_inc(chain, 1)
                    dve.wait_ge(chain, n[0])

                c = lambda k: lim[:, k:k + 1]
                step(dve.tensor_copy(lim_i[:, 0:1], co.first[:, :]))
                step(dve.scalar_tensor_tensor(out=c(0), in0=co.first[:, :], scalar=-1.0, in1=co.count[:, :],
                                              op0=ALU.add, op1=ALU.add))
                step(dve.tensor_copy(lim_i[:, 1:2], c(0)))
                step(dve.tensor_scalar(lim_i[:, 2:4], lim_i[:, 0:2], 8, None, ALU.arith_shift_right))
                step(dve.tensor_copy(lim[:, 1:3], lim_i[:, 2:4]))
                step(dve.scalar_tensor_tensor(out=c(3), in0=c(2), scalar=1.0, in1=c(1), op0=ALU.add, op1=ALU.subtract))
                step(dve.tensor_scalar(c(4), co.count[:, :], 0.5, None, ALU.is_gt))
                step(dve.tensor_tensor(c(5), c(3), c(4), ALU.mult))
                dve.wait_ge(mm, 1)
                step(dve.tensor_copy(c(6), psum[0:NT, 0:1]))
                step(dve.tensor_tensor(c(7), c(6), c(5), ALU.add))
                step(dve.scalar_tensor_tensor(out=c(8), in0=c(1), scalar=-float(NB), in1=c(6), op0=ALU.add, op1=ALU.subtract))
                step(dve.tensor_scalar(meets[:, :], co.iota[0:NT, :], c(6), None, ALU.is_ge))
                step(dve.scalar_tensor_tensor(out=meets[:, :], in0=co.iota[0:NT, :], scalar=c(7), in1=meets[:, :],
                                              op0=ALU.is_lt, op1=ALU.mult))
                dve.wait_ge(mm, 2)
                step(dve.tensor_copy(row[:, 0, :], psum[0:1, 16:16 + STEPS]))
                step(dve.tensor_copy(row[:, 1, :], psum[0:1, 256:256 + STEPS]))
                step(dve.tensor_tensor(row[:, 2, :], co.iota[0:1, :], psum2[0:1, 0:STEPS], ALU.mult))
                step(dve.scalar_tensor_tensor(out=row[:, 3, :], in0=row[:, 1, :], scalar=float(NB), in1=row[:, 2, :],
                                              op0=ALU.add, op1=ALU.add))
                step(dve.tensor_scalar(row[:, 4, :], psum2[0:1, 0:STEPS], -NOWHERE, NOWHERE, ALU.mult, ALU.add))
                step(dve.scalar_tensor_tensor(out=row[:, 4, :], in0=row[:, 0, :], scalar=-float(P), in1=row[:, 4, :],
                                              op0=ALU.mult, op1=ALU.add))
                dve.tensor_scalar(number[:, 0:1], co.rowno[0:HB, :], 0.0, None, ALU.add)
                step(dve.tensor_scalar(number[:, 1:2], co.rowno[0:HB, :], float(HB), None, ALU.add))
                dve.wait_ge(mm, 3)
                dve.tensor_copy(shift[:, 0, :], psum3[:, 0:STEPS])
                for h in range(2):
                    last = dve.tensor_scalar(chosen[:, h, :], psum4[0:HB, 0:STEPS], number[:, h:h + 1], None, ALU.is_equal)
                step(last)
                dve.wait_ge(loaded, 80)
                for i in range(2):
                    dve.tensor_copy(val[i][:, :, :], raw[i][:, :, :]).then_inc(conv, 1)
                step(dve.tensor_copy(tile_of[:, :], row[:, 0, :]))
                step(dve.memset(co.tiles[:, :], 0))
                for i in range(FIELDS):
                    lo, hi = max(UNROLL - i, 0), STEPS + UNROLL - i
                    step(dve.tensor_scalar(moved[:, :], tile_of[:, :], TILE_BITS * i, None, ALU.logical_shift_left))
                    step(dve.tensor_tensor(co.tiles[:, lo:hi], co.tiles[:, lo:hi], moved[:, lo + i - UNROLL:STEPS], ALU.bitwise_or))
                dve.wait_ge(brought, 1)
                dve.tensor_tensor(co.local[:, :, :], psb[0][:, :, 0:STEPS], shift[:, :, :].to_broadcast([P, 2, STEPS]), ALU.add)
                dve.wait_ge(brought, 2)
                dve.tensor_copy(co.edge_src[:, :, :], psb[1][:, :, 0:STEPS])

            @block.tensor
            def _(pe):
                pe.wait_ge(chain, 8)
                pe.matmul(psum[0:NT, 0:1], co.before[0:NT, 0:NT], lim[:, 5:6], start=True, stop=True).then_inc(mm, 1)
                pe.wait_ge(chain, 13)
                pe.matmul(psum[0:1, 16:16 + STEPS], co.rowno[0:NT, :], meets[:, :], start=True, stop=True)
                pe.matmul(psum[0:1, 256:256 + STEPS], lim[:, 8:9], meets[:, :], start=True, stop=True)
                pe.matmul(psum2[0:1, 0:STEPS], co.ones[0:NT, 0:1], meets[:, :], start=True, stop=True).then_inc(mm, 1)
                pe.wait_ge(chain, 19)
                pe.matmul(psum3[:, 0:STEPS], co.ones[0:1, :], row[:, 4, :], start=True, stop=True)
                pe.matmul(psum4[:, 0:STEPS], co.ones[0:1, :], row[:, 3, :], start=True, stop=True).then_inc(mm, 1)
                pe.wait_ge(conv, 2)
                pe.wait_ge(chain, 21)
                for i in range(3):
                    for j in range(2):
                        for h in range(2):
                            a = val[i][:, h, :] if i < 2 else raw[i][:, h, :].bitcast(F32)
                            last = pe.matmul(psb[i][:, j, 0:STEPS], a[:, j * P:(j + 1) * P], chosen[:, h, :],
                                             start=(h == 0), stop=(h == 1))
                    last.then_inc(brought, 1)

            @block.scalar
            def _(act):
                act.preload_act_table(ACT.Exp)
                act.wait_ge(brought, 3)
                act.activation(co.edge_term[:, :, :], psb[2][:, :, 0:STEPS], ACT.Identity, bias=wev[:, 1:2], scale=wev[:, 0:1])


def load_x(nc, co, x):
    co.x = co.sbuf("x", [P, NT, D])
    with phase(co, "loadx") as ph:
        cleared, loaded = ph.sem("cleared"), ph.sem("loaded")
        with nc.Block() as block:
            @block.vector
            def _(dve):
                dve.memset(co.x[:, NT - 1, :], 0.0).then_inc(cleared, 1)

            @block.sync
            def _(sp):
                sp.dma_start(co.x[:, 0:NT - 1, :], x[0:(NT - 1) * P, :].rearrange("(t p) d -> p t d", p=P)).then_inc(loaded, 16)
                sp.wait_ge(cleared, 1)
                sp.dma_start(co.x[0:LAST, NT - 1, :], x[(NT - 1) * P:N, :]).then_inc(loaded, 16)
                sp.wait_ge(loaded, 32)


def layer_norm(nc, co, name, src, dst):
    with phase(co, name) as ph:
        stats = ph.sb("stats", [P, NT, 6])
        mv = ph.sb("mv", [P, NT, 2])
        var = ph.sb("var", [P, NT])
        std = ph.sb("std", [P, NT])
        rstd = ph.sb("rstd", [P, NT])
        shift = ph.sb("shift", [P, NT])
        stat, agg, eps, root, inv, neg = (ph.sem(n) for n in ("stat", "agg", "eps", "root", "inv", "neg"))
        half = 15
        with nc.Block() as block:
            @block.vector
            def _(dve):
                with dve.Fori(0, NT) as t:
                    dve.bn_stats(stats[:, bass.ds(t, 1), :], src[:, bass.ds(t, 1), :]).then_inc(stat, 1)
                dve.wait_ge(stat, NT)
                for t in range(NT):
                    dve.bn_aggr(mv[:, t, :], stats[:, t, :]).then_inc(agg, 1)
                dve.wait_ge(agg, NT)
                dve.tensor_scalar(var[:, :], mv[:, :, 1], EPS, None, ALU.add).then_inc(eps, 1)
                dve.wait_ge(root, 1)
                dve.reciprocal(rstd[:, :], std[:, :]).then_inc(inv, 1)
                dve.wait_ge(inv, 1)
                dve.scalar_tensor_tensor(out=shift[:, :], in0=mv[:, :, 0], scalar=-1.0, in1=rstd[:, :],
                                         op0=ALU.mult, op1=ALU.mult).then_inc(neg, 1)
                dve.wait_ge(neg, 1)
                with dve.Fori(0, half) as t:
                    dve.tensor_scalar(dst[:, bass.ds(t, 1), :], src[:, bass.ds(t, 1), :], rstd[:, bass.ds(t, 1)],
                                      shift[:, bass.ds(t, 1)], ALU.mult, ALU.add)

            @block.scalar
            def _(act):
                act.wait_ge(eps, 1)
                act.activation(std[:, :], var[:, :], ACT.Sqrt).then_inc(root, 1)
                act.wait_ge(neg, 1)
                with act.Fori(half, NT) as t:
                    act.activation(dst[:, bass.ds(t, 1), :], src[:, bass.ds(t, 1), :], ACT.Identity,
                                   bias=shift[:, bass.ds(t, 1)], scale=rstd[:, bass.ds(t, 1)])


def at_least(eng, sem, value):
    if not isinstance(value, int) or value > 0:
        eng.wait_ge(sem, value)


def over_tiles(eng, n, stages, start=0):
    most = max(lag for lag, _ in stages)

    def round_(r, static):
        for lag, body in stages:
            if not static or 0 <= r - lag < n:
                body(r - lag)

    for r in range(most + 1):
        round_(r, True)
    with eng.Fori(most + 1, n) as r:
        round_(r, False)
    for r in range(n, n + most):
        round_(r, True)


def split3(dve, parts, t, rest, whole, sem, count):
    part = lambda i: parts[:, bass.ds(t, 1), i, :]
    dve.tensor_tensor(rest, whole, part(0), ALU.subtract).then_inc(sem, 1)
    dve.wait_ge(sem, count + 1)
    dve.tensor_scalar(part(1), rest, 1.0, None, ALU.mult).then_inc(sem, 1)
    dve.wait_ge(sem, count + 2)
    dve.tensor_tensor(part(2), rest, part(1), ALU.subtract).then_inc(sem, 1)


def attention_inputs(nc, co, xn, a, q_parts, base, table, acc, top):
    with phase(co, "attin") as ph:
        wq, wk, ws = ph.sb("wq", [P, KD, D]), ph.sb("wk", [P, KD, D + 1]), ph.sb("ws", [P, KD, D])
        bq, bs = ph.sb("bq", [P, KD]), ph.sb("bs", [P, 1, D])
        cur, xt, qt = ph.sb("cur", [P, D]), ph.sb("xt", [P, KD, P]), ph.sb("qt", [P, KD, P])
        qf, rest = ph.sb("qf", [P, 1, D + 1]), ph.sb("rest", [P, 1, D + 1])
        ps_x, ps_q, ps_k, ps_s = (ph.ps(n, [P, 512]) for n in ("ps_x", "ps_q", "ps_k", "ps_s"))
        loaded, tabled, biased, staged = (ph.sem(n) for n in ("loaded", "tabled", "biased", "staged"))
        x_turned, x_out, q_made, q_out, k_made, k_out, s_made, s_out, split = (ph.sem(n) for n in (
            "x_turned", "x_out", "q_made", "q_out", "k_made", "k_out", "s_made", "s_out", "split"))
        seen = ph.sem("seen")
        with nc.Block() as block:
            @block.sync
            def _(sp):
                for there, w in ((wq[:, :, :], "L0_gnn_wq"), (wk[:, :, 0:D], "L0_gnn_wk"), (ws[:, :, :], "L0_gnn_ws")):
                    sp.dma_start(there, a[w].rearrange("(k p) d -> p k d", p=P)).then_inc(loaded, 16)
                with nc.allow_non_contiguous_dma(reason="a bias with its features on partitions"):
                    sp.dma_start(bq[:, :], a["L0_gnn_bq"].rearrange("(k p) -> p k", p=P)).then_inc(loaded, 16)
                    sp.dma_start(wk[:, :, D:D + 1], a["L0_gnn_bk"].rearrange("(k p a) -> p k a", p=P, a=1)).then_inc(loaded, 16)
                sp.dma_start(bs[:, 0, :], a["L0_gnn_bs"].rearrange("(a d) -> a d", a=1).to_broadcast([P, D])).then_inc(loaded, 16)
                sp.dma_start(table.rearrange("(t p) d -> p t d", p=P), xn[:, :, :]).then_inc(tabled, 16)
                sp.wait_ge(tabled, 16)

            @block.gpsimd
            def _(gp):
                gp.wait_ge(loaded, 96)

                def stage(t):
                    gp.tensor_tensor(base[:, bass.ds(t, 1), :], xn[:, bass.ds(t, 1), :], bs[:, :, :], ALU.add).then_inc(biased, 1)
                    at_least(gp, x_turned, t)
                    gp.sem_inc(seen, 1)
                    gp.tensor_copy(cur[:, :].unsqueeze(1), xn[:, bass.ds(t, 1), :]).then_inc(staged, 1)

                over_tiles(gp, NT, [(0, stage)])

            @block.tensor
            def _(pe):
                pe.wait_ge(loaded, 96)

                def turn(t):
                    pe.wait_ge(staged, t + 1)
                    at_least(pe, x_out, t)
                    for k in range(KD):
                        last = pe.transpose(ps_x[:, k * P:(k + 1) * P], cur[:, k * P:(k + 1) * P], co.ident[:, :])
                    last.then_inc(x_turned, 1)

                def project(t):
                    pe.wait_ge(x_out, t + 1)
                    at_least(pe, q_out, t)
                    for m in range(KD):
                        for k in range(KD):
                            last = pe.matmul(ps_q[:, m * P:(m + 1) * P], wq[:, k, m * P:(m + 1) * P], xt[:, k, :],
                                             start=(k == 0), stop=(k == KD - 1))
                    last.then_inc(q_made, 1)
                    at_least(pe, s_out, t)
                    for k in range(KD):
                        last = pe.matmul(ps_s[:, 0:D], xt[:, k, :], ws[:, k, :], start=(k == 0), stop=(k == KD - 1))
                    last.then_inc(s_made, 1)

                def keys(t):
                    pe.wait_ge(q_out, t + 1)
                    at_least(pe, k_out, t)
                    for k in range(KD):
                        last = pe.matmul(ps_k[:, 0:D + 1], qt[:, k, :], wk[:, k, :], start=(k == 0), stop=(k == KD - 1))
                    last.then_inc(k_made, 1)

                over_tiles(pe, NT, [(0, turn), (2, keys), (1, project)])

            @block.scalar
            def _(act):
                act.preload_act_table(ACT.Exp)

                def turned(t):
                    act.wait_ge(x_turned, t + 1)
                    at_least(act, s_made, t)
                    act.copy(xt[:, :, :], ps_x[:, 0:D].rearrange("p (k c) -> p k c", k=KD)).then_inc(x_out, 1)

                def scaled(t):
                    act.wait_ge(k_made, t + 1)
                    at_least(act, split, 3 * t)
                    act.mul(qf[:, 0, :], ps_k[:, 0:D + 1], D ** -0.5)
                    act.mul(q_parts[:, bass.ds(t, 1), 0, :], ps_k[:, 0:D + 1].unsqueeze(1), D ** -0.5).then_inc(k_out, 1)

                over_tiles(act, NT, [(0, turned), (2, scaled)])

            @block.vector
            def _(dve):
                dve.memset(acc[:, :, :], 0.0)
                dve.memset(top[:, :, :], -BIG)
                dve.wait_ge(loaded, 96)

                def biases(t):
                    dve.wait_ge(q_made, t + 1)
                    at_least(dve, k_made, t)
                    for m in range(KD):
                        last = dve.tensor_scalar(qt[:, m, :], ps_q[:, m * P:(m + 1) * P], bq[:, m:m + 1], None, ALU.add)
                    last.then_inc(q_out, 1)
                    dve.wait_ge(s_made, t + 1)
                    dve.wait_ge(biased, t + 1)
                    dve.tensor_tensor(base[:, bass.ds(t, 1), :], ps_s[:, 0:D].unsqueeze(1), base[:, bass.ds(t, 1), :], ALU.add)\
                       .then_inc(s_out, 1)

                def parts(t):
                    dve.wait_ge(k_out, t + 1)
                    split3(dve, q_parts, t, rest[:, :, :], qf[:, :, :], split, 3 * t)

                over_tiles(dve, NT, [(1, biases), (3, parts)])


def tile_in(word, field):
    return ((word >> TILE_BITS * field) & (2 ** TILE_BITS - 1)).with_bounds(min_val=0, max_val=NT - 1)


def over_steps(eng, n, tiles, stages):
    most = max(lag for lag, *_ in stages)
    turns = n // UNROLL
    assert n % UNROLL == 0 and most <= UNROLL

    def turn(q, steps, static):
        words = {first: eng.value_load(tiles[0:1, bass.ds(UNROLL * q + first + UNROLL, 1)])
                 for first in sorted({first for _, _, first in stages if first is not None})}
        for r in steps:
            for lag, body, first in stages:
                if not static or 0 <= UNROLL * q + r - lag < n:
                    body(q + (r - lag) // UNROLL, (r - lag) % UNROLL,
                         None if first is None else tile_in(words[first], r - lag - first))

    turn(0, range(UNROLL), True)
    turn(1, range(UNROLL), True)
    with eng.Fori(2, turns) as q:
        turn(q, range(UNROLL), False)
    turn(turns, range(most), True)


def edge_pass(nc, co, name, table, acc, top, heads, q_parts=None, r_parts=None, att=None):
    gat = att is not None
    tw = table.shape[1]
    ch = D // heads
    one = tw if heads == 1 else None
    uw = tw + 1 if heads == 1 else heads * (ch + 1)
    gw = max(uw, tw)
    per = 1 if heads == 1 else 2
    steps = STEPS
    with phase(co, name) as ph:
        rows = [ph.sb(f"rows{k}", [P, 2, gw]) for k in range(UNROLL)]
        index = [ph.sb(f"index{k}", [P, 2], U32) for k in range(UNROLL)]
        memb = [ph.sb(f"memb{k}", [P, 2, P]) for k in range(UNROLL)]
        out_of = [ph.sb(f"out_of{k}", [P, 2, P], BF16) for k in range(UNROLL)]
        turned = [ph.sb(f"turned{k}", [P, 2, P], BF16) for k in range(UNROLL)]
        score = [ph.sb(f"score{k}", [P, 2, heads]) for k in range(UNROLL)]
        rough = [ph.sb(f"rough{k}", [P, 2, heads], BF16) for k in range(UNROLL)]
        old, gmax = ph.sb("old", [P, heads]), ph.sb("gmax", [P, heads])
        peak = [ph.sb(f"peak{k}", [P, heads + 1], BF16) for k in range(UNROLL)]
        fall = [ph.sb(f"fall{k}", [P, heads]) for k in range(UNROLL)]
        keep = [ph.sb(f"keep{k}", [P, heads]) for k in range(UNROLL)]
        less = ph.sb("less", [P, 2, heads])
        arg = [ph.sb(f"arg{k}", [P, 2, heads]) for k in range(UNROLL)]
        wt = [ph.sb(f"wt{k}", [P, 2, heads]) for k in range(UNROLL)]
        if heads == 1:
            lhs = [ph.sb(f"lhs{k}", [P, 2, P]) for k in range(UNROLL)]
        else:
            scaled = [ph.sb(f"scaled{k}", [P, 2, heads, ch + 1]) for k in range(UNROLL)]
        if gat:
            mag = [ph.sb(f"mag{k}", [P, KD, 2 * P]) for k in range(UNROLL)]
            ps_m = ph.ps("ps_m", [P, KD, 2 * P])
            ps_l = ph.ps("ps_l", [P, 512])
        else:
            dots, constant = ph.sb("dots", [P, 2, 1]), ph.sb("constant", [P, 2, 1])
            junk = ph.sb("junk", [P, 2, D])
            ps_q = ph.ps("ps_q", [P, 2, 512])
        ps_t = ph.ps("ps_t", [P, 1024], BF16)
        ps_x = ph.ps("ps_x", [P, 1 if heads == 1 else 2, 512])
        ps_e = ph.ps("ps_e", [P, 512])
        ps_u = ph.ps("ps_u", [P, 512])
        xview = (lambda: ps_x[:, 0, 0:2 * P].rearrange("p (j h e) -> p j h e", j=2, h=1)) if heads == 1 else \
                (lambda: ps_x[:, :, :].rearrange("p j (h e) -> p j h e", h=heads))
        pair_e = lambda: ps_e[:, 0:2 * (heads + 1)].rearrange("p (j h) -> p j h", j=2)
        got = [ph.gp_dma_sem(k) for k in range(UNROLL)]
        indexed, seen, primed = ph.sem("indexed"), ph.sem("seen"), ph.sem("primed")
        dotted, maxed, peaked, fell, lessed, summed = (ph.sem(n) for n in (
            "dotted", "maxed", "peaked", "fell", "lessed", "summed"))
        members, t_made, t_out, m_made, m_out, l_made, l_out, x_made, x_out = (ph.sem(n) for n in (
            "members", "t_made", "t_out", "m_made", "m_out", "l_made", "l_out", "x_made", "x_out"))
        kept, e_made, e_out, weighed, spread, spread2, u_made, u_out = (ph.sem(n) for n in (
            "kept", "e_made", "e_out", "weighed", "spread", "spread2", "u_made", "u_out"))
        num = lambda q, k: UNROLL * q + k

        with nc.Block() as block:
            @block.gpsimd
            def _(gp):
                gp.wait_ge(primed, 2 if heads > 1 else 2 + UNROLL)

                def gather(q, k, _):
                    g = num(q, k)
                    at_least(gp, u_made, g - (UNROLL - 1))
                    gp.sem_inc(seen, 1)
                    gp.tensor_copy(index[k][:, :].unsqueeze(2), co.edge_src[:, :, bass.ds(g, 1)]).then_inc(indexed, 1)
                    gp.wait_ge(indexed, g + 1)
                    gp.sem_inc(seen, 1)
                    for j in range(2):
                        gp.indirect_dma_start(rows[k][:, j, 0:tw], None, table,
                                              bass.IndirectOffsetOnAxis(ap=index[k][:, j:j + 1], axis=0)).then_inc(got[k], 16)

                over_steps(gp, steps, co.tiles, [(0, gather, None)])

            @block.vector
            def _(dve):
                for k in range(UNROLL):
                    if heads == 1:
                        dve.memset(rows[k][:, :, one:one + 1], 1.0).then_inc(primed, 1)
                    dve.memset(peak[k][:, heads:heads + 1], BIG)
                dve.memset(gmax[:, :], 0.0).then_inc(primed, 1)
                dve.memset(less[:, :, :], 0.0).then_inc(primed, 1)
                dve.wait_ge(primed, 2 if heads > 1 else 2 + UNROLL)

                def outsiders(q, k, _):
                    g = num(q, k)
                    for j in range(2):
                        dve.tensor_scalar(out_of[k][:, j, :], co.iotab[:, :], co.local[:, j, bass.ds(g, 1)], -1.0, ALU.is_equal, ALU.add)

                def members_of(q, k, _):
                    g = num(q, k)
                    for j in range(2):
                        last = dve.tensor_scalar(memb[k][:, j, :], co.iota[:, 0:P], co.local[:, j, bass.ds(g, 1)], None, ALU.is_equal)
                    last.then_inc(members, 1)

                def dot_products(q, k, _):
                    g = num(q, k)
                    dve.wait_ge(m_made, g + 1)
                    dve.tensor_tensor(constant[:, :, :], co.edge_term[:, :, bass.ds(g, 1)], ps_q[:, :, D:D + 1], ALU.add)
                    for j in range(2):
                        last = dve.tensor_tensor_reduce(junk[:, j, :], rows[k][:, j, 0:D], ps_q[:, j, 0:D], 1.0, 0.0, ALU.mult,
                                                        ALU.add, dots[:, j, :])
                    last.then_inc(dotted, 1)

                def scores(q, k, _):
                    g = num(q, k)
                    if gat:
                        dve.wait_ge(l_made, g + 1)
                        parts = ps_l[:, 0:2 * heads].rearrange("p (j h) -> p j h", j=2), rows[k][:, :, D:D + heads]
                    else:
                        dve.wait_ge(dotted, g + 1)
                        parts = dots[:, :, :], constant[:, :, :]
                    dve.tensor_tensor(score[k][:, :, :], *parts, ALU.add)
                    dve.tensor_tensor(rough[k][:, :, :], *parts, ALU.add).then_inc(l_out, 1)

                def old_tops(q, k, tile):
                    dve.tensor_copy(old[:, :].unsqueeze(1), top[:, bass.ds(tile, 1), :])

                def maxima(q, k, _):
                    g = num(q, k)
                    dve.wait_ge(x_made, g + 1)
                    dve.tensor_reduce(gmax[:, :], xview().rearrange("p j h e -> p h j e"), AX.XY, ALU.max).then_inc(maxed, 1)

                def peaks(q, k, _):
                    g = num(q, k)
                    dve.wait_ge(maxed, g + 1)
                    dve.tensor_tensor(peak[k][:, 0:heads], old[:, :], gmax[:, :], ALU.max).then_inc(peaked, 1)

                def new_tops(q, k, tile):
                    g = num(q, k)
                    dve.wait_ge(peaked, g + 1)
                    dve.tensor_tensor(fall[k][:, :], old[:, :], peak[k][:, 0:heads], ALU.subtract).then_inc(fell, 1)
                    dve.tensor_scalar(top[:, bass.ds(tile, 1), :], peak[k][:, 0:heads].unsqueeze(1), 1.0, None, ALU.mult)

                def differences(q, k, _):
                    g = num(q, k)
                    dve.wait_ge(e_made, g + 1)
                    dve.tensor_tensor(less[:, :, :], score[k][:, :, :], pair_e()[:, :, 0:heads], ALU.subtract).then_inc(lessed, 1)

                def arguments(q, k, _):
                    g = num(q, k)
                    dve.wait_ge(lessed, g + 1)
                    dve.scalar_tensor_tensor(out=arg[k][:, :, :], in0=pair_e()[:, :, heads:heads + 1].to_broadcast([P, 2, heads]),
                                             scalar=-BIG, in1=less[:, :, :], op0=ALU.add, op1=ALU.add).then_inc(e_out, 1)

                def weights(q, k, _):
                    dve.wait_ge(weighed, num(q, k) + 1)
                    dve.tensor_tensor(scaled[k][:, 0, :, 0:ch], rows[k][:, 0, 0:D].rearrange("p (h c) -> p h c", h=heads),
                                      wt[k][:, 0, :].unsqueeze(2).to_broadcast([P, heads, ch]), ALU.mult)
                    dve.tensor_copy(scaled[k][:, :, :, ch], wt[k][:, :, :]).then_inc(spread, 1)

                def sums(q, k, tile):
                    g = num(q, k)
                    dve.wait_ge(u_made, g + 1)
                    dve.wait_ge(kept, g + 1)
                    w = uw // heads
                    for h in range(heads):
                        mine = acc[:, bass.ds(tile, 1), h * w:(h + 1) * w]
                        last = dve.scalar_tensor_tensor(out=mine, in0=mine, scalar=keep[k][:, h:h + 1],
                                                        in1=ps_u[:, h * w:(h + 1) * w].unsqueeze(1), op0=ALU.mult, op1=ALU.add)
                    last.then_inc(summed, 1)

                if gat:
                    over_steps(dve, steps, co.tiles,
                               [(3, scores, None), (4, differences, None), (4, arguments, None), (5, sums, -5), (3, old_tops, -3),
                                (0, outsiders, None)] + ([] if heads == 1 else [(4, weights, None)]) +
                               [(3, maxima, None), (3, peaks, None), (0, members_of, None), (3, new_tops, -3)])
                else:
                    over_steps(dve, steps, co.tiles,
                               [(3, dot_products, None), (4, differences, None), (3, scores, None), (4, arguments, None),
                                (5, sums, -5), (3, old_tops, -3), (0, outsiders, None), (3, maxima, None), (3, peaks, None),
                                (0, members_of, None), (3, new_tops, -3)])

            @block.scalar
            def _(act):
                act.preload_act_table(ACT.Exp)

                def turn(q, k, _):
                    g = num(q, k)
                    act.wait_ge(t_made, g + 1)
                    act.activation(turned[k][:, :, :], ps_t[:, 0:2 * P].rearrange("p (j e) -> p j e", j=2), ACT.Identity,
                                   bias=co.ones[:, 0:1]).then_inc(t_out, 1)

                def magnitudes(q, k, _):
                    g = num(q, k)
                    act.wait_ge(m_made, g + 1)
                    act.activation(mag[k][:, :, :], ps_m[:, :, :], ACT.Abs).then_inc(m_out, 1)

                def keeps(q, k, _):
                    g = num(q, k)
                    act.wait_ge(fell, g + 1)
                    act.activation(keep[k][:, :], fall[k][:, :], ACT.Exp).then_inc(kept, 1)

                def exps(q, k, _):
                    g = num(q, k)
                    act.wait_ge(e_out, g + 1)
                    act.activation(wt[k][:, :, :], arg[k][:, :, :], ACT.Exp).then_inc(weighed, 1)

                def weights(q, k, _):
                    act.wait_ge(weighed, num(q, k) + 1)
                    if heads == 1:
                        for j in range(2):
                            last = act.activation(lhs[k][:, j, :], memb[k][:, j, :], ACT.Copy, scale=wt[k][:, j, :])
                    else:
                        for h in range(heads):
                            last = act.activation(scaled[k][:, 1, h, 0:ch], rows[k][:, 1, h * ch:(h + 1) * ch],
                                                  ACT.Copy, scale=wt[k][:, 1, h:h + 1])
                    last.then_inc(spread2, 1)

                over_steps(act, steps, co.tiles, [(4, exps, None), (4, weights, None)] + ([(2, magnitudes, None)] if gat else []) +
                           [(1, turn, None), (3, keeps, None)])

            @block.tensor
            def _(pe):
                pe.wait_ge(primed, 2 if heads > 1 else 2 + UNROLL)

                def turns(q, k, tile):
                    g = num(q, k)
                    pe.wait_ge(members, g + 1)
                    for j in range(2):
                        last = pe.transpose(ps_t[:, j * P:(j + 1) * P], out_of[k][:, j, :], co.identb[:, :])
                    last.then_inc(t_made, 1)

                def expand(q, k, tile):
                    g = num(q, k)
                    if not gat:
                        pe.wait_ge(t_out, g + 1)
                        pe.wait_ge(got[k], 32 * q + 32)
                        for j in range(2):
                            for i in range(3):
                                last = pe.matmul(ps_q[:, j, 0:D + 1], turned[k][:, j, :], q_parts[:, bass.ds(tile, 1), i, :],
                                                 start=(i == 0), stop=(i == 2))
                        last.then_inc(m_made, 1)
                        return
                    pe.wait_ge(t_out, g + 1)
                    pe.wait_ge(got[k], 32 * q + 32)
                    at_least(pe, m_out, g)
                    for c in range(KD):
                        for j in range(2):
                            pe.matmul(ps_m[:, c, j * P:(j + 1) * P], rows[k][:, j, c * P:(c + 1) * P], co.ident[:, :],
                                      is_transpose=True, start=(c == 0 and j == 0), stop=False, skip_group_check=True)
                        for i in range(3):
                            last = pe.matmul(ps_m[:, c, :], r_parts[:, bass.ds(tile, 1), i, c * P:(c + 1) * P],
                                             turned[k][:, :, :], start=False, stop=(c == KD - 1 and i == 2),
                                             skip_group_check=True)
                    last.then_inc(m_made, 1)

                def logits(q, k, tile):
                    g = num(q, k)
                    pe.wait_ge(m_out, g + 1)
                    for j in range(2):
                        for c in range(KD):
                            pe.matmul(ps_l[:, j * heads:(j + 1) * heads], mag[k][:, c, j * P:(j + 1) * P],
                                      att[:, c, :], start=(c == 0), stop=False)
                        for i in range(3):
                            last = pe.matmul(ps_l[:, j * heads:(j + 1) * heads], turned[k][:, j, :],
                                             r_parts[:, bass.ds(tile, 1), i, D:D + heads], start=False, stop=(i == 2))
                    last.then_inc(l_made, 1)

                def spread_scores(q, k, tile):
                    g = num(q, k)
                    pe.wait_ge(l_out, g + 1)
                    for j in range(2):
                        where = ps_x[:, 0, j * P:(j + 1) * P] if heads == 1 else ps_x[:, j, :]
                        pe.matmul(where, out_of[k][:, j, :], co.bigident[:, :] if heads == 1 else
                                  co.bigident[:, :].unsqueeze(1).to_broadcast([P, heads, P]), start=(heads > 1 or j == 0),
                                  stop=False, skip_group_check=True)
                        for h in range(heads):
                            last = pe.matmul(where[:, h * P:(h + 1) * P], rough[k][:, j, h:h + 1].to_broadcast([P, P]),
                                             co.identb[:, :], start=False, stop=(h == heads - 1), skip_group_check=True)
                    last.then_inc(x_made, 1)

                def tops_of(q, k, tile):
                    g = num(q, k)
                    pe.wait_ge(peaked, g + 1)
                    w = heads + 1
                    for j in range(2):
                        last = pe.matmul(ps_e[:, j * w:(j + 1) * w], turned[k][:, j, :], peak[k][:, :], start=True, stop=True)
                    last.then_inc(e_made, 1)

                def add_up(q, k, tile):
                    g = num(q, k)
                    pe.wait_ge(spread2, g + 1)
                    if heads > 1:
                        pe.wait_ge(spread, g + 1)
                    else:
                        at_least(pe, summed, g)
                    for j in range(2):
                        if heads == 1:
                            last = pe.matmul(ps_u[:, 0:uw], lhs[k][:, j, :], rows[k][:, j, 0:uw], start=(j == 0), stop=(j == 1))
                        else:
                            last = pe.matmul(ps_u[:, 0:uw], memb[k][:, j, :], scaled[k][:, j, :, :].rearrange("p h c -> p (h c)"),
                                             start=(j == 0), stop=(j == 1))
                    last.then_inc(u_made, 1)

                if gat:
                    over_steps(pe, steps, co.tiles, [(2, expand, -2), (3, spread_scores, None), (4, add_up, None), (2, logits, -2),
                                                     (1, turns, None), (3, tops_of, None)])
                else:
                    over_steps(pe, steps, co.tiles, [(3, spread_scores, None), (2, expand, -2), (3, tops_of, None),
                                                     (4, add_up, None), (1, turns, None)])


def row_on_all(ap, n):
    return ap.rearrange("(a n) -> a n", a=1).to_broadcast([P, n])


def attention_output(nc, co, acc, base, a):
    with phase(co, "attout") as ph:
        wv = ph.sb("wv", [P, KD, D])
        bv = ph.sb("bv", [P, 1, D])
        most, inv, share = ph.sb("most", [P, NT]), ph.sb("inv", [P, NT]), ph.sb("share", [P, NT])
        cur, xt, biased = ph.sb("cur", [P, 1, D]), ph.sb("xt", [P, KD, P]), ph.sb("biased", [P, 1, D])
        ps_x, ps_v = ph.ps("ps_x", [P, 512]), ph.ps("ps_v", [P, 512])
        loaded, chain, staged, turned, out, made, mixed, used = (ph.sem(n) for n in (
            "loaded", "chain", "staged", "turned", "out", "made", "mixed", "used"))
        with nc.Block() as block:
            @block.sync
            def _(sp):
                sp.dma_start(wv[:, :, :], a["L0_gnn_wv"].rearrange("(k p) d -> p k d", p=P)).then_inc(loaded, 16)
                sp.dma_start(bv[:, 0, :], row_on_all(a["L0_gnn_bv"], D)).then_inc(loaded, 16)

            @block.scalar
            def _(act):
                act.preload_act_table(ACT.Exp)
                act.wait_ge(chain, 3)

                def stage(t):
                    at_least(act, turned, t)
                    act.activation(cur[:, :, :], acc[:, bass.ds(t, 1), 0:D], ACT.Copy, scale=inv[:, bass.ds(t, 1)]).then_inc(staged, 1)

                def evacuate(t):
                    act.wait_ge(turned, t + 1)
                    at_least(act, made, t)
                    act.copy(xt[:, :, :], ps_x[:, 0:D].rearrange("p (k c) -> p k c", k=KD)).then_inc(out, 1)

                over_tiles(act, NT, [(1, evacuate), (0, stage)])

            @block.tensor
            def _(pe):
                pe.wait_ge(loaded, 32)

                def turn(t):
                    pe.wait_ge(staged, t + 1)
                    at_least(pe, out, t)
                    for k in range(KD):
                        last = pe.transpose(ps_x[:, k * P:(k + 1) * P], cur[:, 0, k * P:(k + 1) * P], co.ident[:, :])
                    last.then_inc(turned, 1)

                def project(t):
                    pe.wait_ge(out, t + 1)
                    at_least(pe, mixed, t)
                    for k in range(KD):
                        last = pe.matmul(ps_v[:, 0:D], xt[:, k, :], wv[:, k, :], start=(k == 0), stop=(k == KD - 1))
                    last.then_inc(made, 1)

                over_tiles(pe, NT, [(0, turn), (1, project)])

            @block.vector
            def _(dve):
                dve.tensor_scalar(most[:, :], acc[:, :, D], 1e-12, None, ALU.max).then_inc(chain, 1)
                dve.wait_ge(chain, 1)
                dve.reciprocal(inv[:, :], most[:, :]).then_inc(chain, 1)
                dve.wait_ge(chain, 2)
                dve.tensor_tensor(share[:, :], acc[:, :, D], inv[:, :], ALU.mult).then_inc(chain, 1)
                dve.wait_ge(chain, 3)
                dve.wait_ge(loaded, 32)

                def mix(t):
                    dve.wait_ge(made, t + 1)
                    at_least(dve, used, t)
                    dve.scalar_tensor_tensor(out=biased[:, :, :], in0=bv[:, :, :], scalar=share[:, bass.ds(t, 1)],
                                             in1=ps_v[:, 0:D].unsqueeze(1), op0=ALU.mult, op1=ALU.add).then_inc(mixed, 1)
                    dve.wait_ge(mixed, t + 1)
                    dve.tensor_tensor(base[:, bass.ds(t, 1), :], biased[:, :, :], base[:, bass.ds(t, 1), :], ALU.add).then_inc(used, 1)

                over_tiles(dve, NT, [(1, mix)])


def attention_ffn(nc, co, y, base, a):
    K2 = 2 * KD
    with phase(co, "attffn") as ph:
        w1, w2 = ph.sb("w1", [P, KD, 2 * D]), ph.sb("w2", [P, K2, D])
        b1 = ph.sb("b1", [P, K2])
        g, b, b2, both = (ph.sb(n, [P, 1, D]) for n in ("g", "b", "b2", "both"))
        cur, xt, ht = ph.sb("cur", [P, 1, D]), ph.sb("xt", [P, KD, P]), ph.sb("ht", [P, K2, P])
        ps_x, ps_h, ps_f = ph.ps("ps_x", [P, 512]), ph.ps("ps_h", [P, K2, P]), ph.ps("ps_f", [P, 512])
        loaded, added, scaled, staged, rested, turned, out, made, bent, mixed, done, seen = (ph.sem(n) for n in (
            "loaded", "added", "scaled", "staged", "rested", "turned", "out", "made", "bent", "mixed", "done", "seen"))
        with nc.Block() as block:
            @block.sync
            def _(sp):
                sp.dma_start(w1[:, :, :], a["L0_gnn_w_ff1"].rearrange("(k p) d -> p k d", p=P)).then_inc(loaded, 16)
                sp.dma_start(w2[:, :, :], a["L0_gnn_w_ff2"].rearrange("(k p) d -> p k d", p=P)).then_inc(loaded, 16)
                with nc.allow_non_contiguous_dma(reason="a bias with its features on partitions"):
                    sp.dma_start(b1[:, :], a["L0_gnn_b_ff1"].rearrange("(k p) -> p k", p=P)).then_inc(loaded, 16)
                for there, v in ((g, "L0_gnn_g1"), (b, "L0_gnn_b1"), (b2, "L0_gnn_b_ff2")):
                    sp.dma_start(there[:, 0, :], row_on_all(a[v], D)).then_inc(loaded, 16)

            @block.gpsimd
            def _(gp):
                gp.wait_ge(loaded, 96)
                gp.tensor_tensor(both[:, :, :], b[:, :, :], b2[:, :, :], ALU.add).then_inc(added, 1)
                gp.wait_ge(added, 1)

                def stage(t):
                    at = y[:, bass.ds(t, 1), :]
                    gp.tensor_tensor(at, at, g[:, :, :], ALU.mult).then_inc(scaled, 1)
                    gp.wait_ge(scaled, t + 1)
                    at_least(gp, turned, t)
                    gp.sem_inc(seen, 1)
                    gp.tensor_tensor(cur[:, :, :], at, b[:, :, :], ALU.add).then_inc(staged, 1)
                    gp.wait_ge(staged, t + 1)
                    gp.sem_inc(seen, 1)
                    gp.tensor_tensor(at, at, both[:, :, :], ALU.add).then_inc(rested, 1)

                over_tiles(gp, NT, [(0, stage)])

            @block.tensor
            def _(pe):
                pe.wait_ge(loaded, 96)

                def turn(t):
                    pe.wait_ge(staged, t + 1)
                    at_least(pe, out, t)
                    for k in range(KD):
                        last = pe.transpose(ps_x[:, k * P:(k + 1) * P], cur[:, 0, k * P:(k + 1) * P], co.ident[:, :])
                    last.then_inc(turned, 1)

                def up(t):
                    pe.wait_ge(out, t + 1)
                    at_least(pe, bent, t)
                    for m in range(K2):
                        for k in range(KD):
                            last = pe.matmul(ps_h[:, m, :], w1[:, k, m * P:(m + 1) * P], xt[:, k, :],
                                             start=(k == 0), stop=(k == KD - 1))
                    last.then_inc(made, 1)

                def down(t):
                    pe.wait_ge(bent, t + 1)
                    at_least(pe, done, t)
                    for k in range(K2):
                        last = pe.matmul(ps_f[:, 0:D], ht[:, k, :], w2[:, k, :], start=(k == 0), stop=(k == K2 - 1))
                    last.then_inc(mixed, 1)

                over_tiles(pe, NT, [(0, turn), (2, down), (1, up)])

            @block.scalar
            def _(act):
                act.preload_act_table(ACT.Gelu_apprx_tanh)
                act.wait_ge(loaded, 96)

                def bend(t):
                    act.wait_ge(made, t + 1)
                    at_least(act, mixed, t)
                    for m in range(K2):
                        last = act.activation(ht[:, m, :], ps_h[:, m, :], ACT.Gelu_apprx_tanh, bias=b1[:, m:m + 1])
                    last.then_inc(bent, 1)

                over_tiles(act, NT, [(1, bend)])

            @block.vector
            def _(dve):
                def evacuate(t):
                    dve.wait_ge(turned, t + 1)
                    at_least(dve, made, t)
                    dve.tensor_copy(xt[:, :, :], ps_x[:, 0:D].rearrange("p (k c) -> p k c", k=KD)).then_inc(out, 1)

                def rest(t):
                    dve.wait_ge(mixed, t + 1)
                    dve.wait_ge(rested, t + 1)
                    dve.tensor_tensor(base[:, bass.ds(t, 1), :], ps_f[:, 0:D].unsqueeze(1), y[:, bass.ds(t, 1), :], ALU.add)\
                       .then_inc(done, 1)

                over_tiles(dve, NT, [(0, evacuate), (2, rest)])


def add_affine(nc, co, z, g_ap, b_ap):
    half = 17
    with phase(co, "affine") as ph:
        g, b = ph.sb("g", [P, 1, D]), ph.sb("b", [P, 1, D])
        loaded, v, w = ph.sem("loaded"), ph.sem("v"), ph.sem("w")
        with nc.Block() as block:
            @block.sync
            def _(sp):
                sp.dma_start(g[:, 0, :], row_on_all(g_ap, D)).then_inc(loaded, 16)
                sp.dma_start(b[:, 0, :], row_on_all(b_ap, D)).then_inc(loaded, 16)

            def steps(eng, lo, hi, sem):
                eng.wait_ge(loaded, 32)
                n = hi - lo
                zz, xx = z[:, lo:hi, :], co.x[:, lo:hi, :]
                eng.tensor_tensor(zz, zz, g[:, :, :].to_broadcast([P, n, D]), ALU.mult).then_inc(sem, 1)
                eng.wait_ge(sem, 1)
                eng.tensor_tensor(xx, xx, zz, ALU.add).then_inc(sem, 1)
                eng.wait_ge(sem, 2)
                eng.tensor_tensor(xx, xx, b[:, :, :].to_broadcast([P, n, D]), ALU.add)

            @block.vector
            def _(dve):
                steps(dve, 0, half, v)

            @block.gpsimd
            def _(gp):
                steps(gp, half, NT, w)
def top1_logits(nc, co, h, a, logits, table):
    HK = HID0 // P
    H2 = HK // 2
    with phase(co, "top1") as ph:
        w1, wg = ph.sb("w1", [P, KD, HID0]), ph.sb("wg", [P, HK, EXP])
        b1, bg = ph.sb("b1", [P, HK]), ph.sb("bg", [P, 1, EXP])
        cur, xt, ht = ph.sb("cur", [P, 1, D]), ph.sb("xt", [P, KD, P]), ph.sb("ht", [P, HK, P])
        ps_x, ps_g = ph.ps("ps_x", [P, 512]), ph.ps("ps_g", [P, 512])
        ps_h = [ph.ps(f"ps_h{i}", [P, H2, P]) for i in range(2)]
        loaded, tabled, staged, turned, out, done, routed, seen = (ph.sem(n) for n in (
            "loaded", "tabled", "staged", "turned", "out", "done", "routed", "seen"))
        made, bent, used = ([ph.sem(f"{n}{i}") for i in range(2)] for n in ("made", "bent", "used"))
        with nc.Block() as block:
            @block.sync
            def _(sp):
                sp.dma_start(w1[:, :, :], a["L0_ffn_W1"].rearrange("(k p) d -> p k d", p=P)).then_inc(loaded, 16)
                sp.dma_start(wg[:, :, :], a["L0_ffn_Wg"].rearrange("(k p) e -> p k e", p=P)).then_inc(loaded, 16)
                with nc.allow_non_contiguous_dma(reason="a bias with its features on partitions"):
                    sp.dma_start(b1[:, :], a["L0_ffn_b1"].rearrange("(k p) -> p k", p=P)).then_inc(loaded, 16)
                sp.dma_start(bg[:, 0, :], row_on_all(a["L0_ffn_bg"], EXP)).then_inc(loaded, 16)
                sp.dma_start(table.rearrange("(t p) d -> p t d", p=P), h[:, :, :]).then_inc(tabled, 16)
                sp.wait_ge(tabled, 16)

            @block.gpsimd
            def _(gp):
                def stage(t):
                    at_least(gp, turned, t)
                    gp.sem_inc(seen, 1)
                    gp.tensor_copy(cur[:, :, :], h[:, bass.ds(t, 1), :]).then_inc(staged, 1)

                over_tiles(gp, NT, [(0, stage)])

            @block.tensor
            def _(pe):
                pe.wait_ge(loaded, 64)

                def turn(t):
                    pe.wait_ge(staged, t + 1)
                    at_least(pe, out, t)
                    for k in range(KD):
                        last = pe.transpose(ps_x[:, k * P:(k + 1) * P], cur[:, 0, k * P:(k + 1) * P], co.ident[:, :])
                    last.then_inc(turned, 1)

                def up(i):
                    def body(t):
                        pe.wait_ge(out, t + 1)
                        at_least(pe, bent[i], t)
                        for m in range(H2):
                            for k in range(KD):
                                last = pe.matmul(ps_h[i][:, m, :], w1[:, k, (i * H2 + m) * P:(i * H2 + m + 1) * P], xt[:, k, :],
                                                 start=(k == 0), stop=(k == KD - 1))
                        last.then_inc(made[i], 1)
                    return body

                def gate(i):
                    def body(t):
                        pe.wait_ge(bent[i], t + 1)
                        if i == 0:
                            at_least(pe, done, t)
                        for m in range(i * H2, (i + 1) * H2):
                            last = pe.matmul(ps_g[:, 0:EXP], ht[:, m, :], wg[:, m, :], start=(m == 0), stop=(m == HK - 1))
                        last.then_inc(used[i], 1)
                    return body

                over_tiles(pe, NT, [(1, up(0)), (2, gate(1)), (1, up(1)), (1, gate(0)), (0, turn)])

            @block.scalar
            def _(act):
                act.preload_act_table(ACT.Gelu)
                act.wait_ge(loaded, 64)

                def bend(i):
                    def body(t):
                        act.wait_ge(made[i], t + 1)
                        at_least(act, used[i], t)
                        for m in range(H2):
                            last = act.activation(ht[:, i * H2 + m, :], ps_h[i][:, m, :], ACT.Gelu, bias=b1[:, i * H2 + m:i * H2 + m + 1])
                        last.then_inc(bent[i], 1)
                    return body

                over_tiles(act, NT, [(1, bend(0)), (1, bend(1))])

            @block.vector
            def _(dve):
                dve.wait_ge(loaded, 64)

                def evacuate(t):
                    dve.wait_ge(turned, t + 1)
                    at_least(dve, made[1], t)
                    dve.tensor_copy(xt[:, :, :], ps_x[:, 0:D].rearrange("p (k c) -> p k c", k=KD)).then_inc(out, 1)

                def rest(t):
                    dve.wait_ge(used[1], t + 1)
                    dve.tensor_tensor(logits[:, bass.ds(t, 1), :], ps_g[:, 0:EXP].unsqueeze(1), bg[:, :, :], ALU.add)\
                       .then_inc(done, 1)

                over_tiles(dve, NT, [(2, rest), (0, evacuate)])


def top2_logits(nc, co, h, xn, a, logits, table):
    with phase(co, "top2") as ph:
        wr, br = ph.sb("wr", [P, KD, EXP]), ph.sb("br", [P, 1, EXP])
        cur, xt = ph.sb("cur", [P, 1, D]), ph.sb("xt", [P, KD, P])
        ps_x, ps_g = ph.ps("ps_x", [P, 512]), ph.ps("ps_g", [P, 512])
        loaded, tabled, staged, turned, out, made, done, seen = (ph.sem(n) for n in (
            "loaded", "tabled", "staged", "turned", "out", "made", "done", "seen"))
        with nc.Block() as block:
            @block.sync
            def _(sp):
                sp.dma_start(wr[:, :, :], a["L1_ffn_Wr"].rearrange("(k p) e -> p k e", p=P)).then_inc(loaded, 16)
                sp.dma_start(br[:, 0, :], row_on_all(a["L1_ffn_br"], EXP)).then_inc(loaded, 16)
                sp.dma_start(table.rearrange("(t p) d -> p t d", p=P), xn[:, :, :]).then_inc(tabled, 16)
                sp.wait_ge(tabled, 16)

            @block.gpsimd
            def _(gp):
                def stage(t):
                    at_least(gp, turned, t)
                    gp.sem_inc(seen, 1)
                    gp.tensor_copy(cur[:, :, :], h[:, bass.ds(t, 1), :]).then_inc(staged, 1)

                over_tiles(gp, NT, [(0, stage)])

            @block.tensor
            def _(pe):
                pe.wait_ge(loaded, 32)

                def turn(t):
                    pe.wait_ge(staged, t + 1)
                    at_least(pe, out, t)
                    for k in range(KD):
                        last = pe.transpose(ps_x[:, k * P:(k + 1) * P], cur[:, 0, k * P:(k + 1) * P], co.ident[:, :])
                    last.then_inc(turned, 1)

                def gate(t):
                    pe.wait_ge(out, t + 1)
                    at_least(pe, done, t)
                    for k in range(KD):
                        last = pe.matmul(ps_g[:, 0:EXP], xt[:, k, :], wr[:, k, :], start=(k == 0), stop=(k == KD - 1))
                    last.then_inc(made, 1)

                over_tiles(pe, NT, [(0, turn), (1, gate)])

            @block.scalar
            def _(act):
                act.preload_act_table(ACT.Exp)

                def evacuate(t):
                    act.wait_ge(turned, t + 1)
                    at_least(act, made, t)
                    act.copy(xt[:, :, :], ps_x[:, 0:D].rearrange("p (k c) -> p k c", k=KD)).then_inc(out, 1)

                over_tiles(act, NT, [(0, evacuate)])

            @block.vector
            def _(dve):
                dve.wait_ge(loaded, 32)

                def rest(t):
                    dve.wait_ge(made, t + 1)
                    dve.tensor_tensor(logits[:, bass.ds(t, 1), :], ps_g[:, 0:EXP].unsqueeze(1), br[:, :, :], ALU.add)\
                       .then_inc(done, 1)

                over_tiles(dve, NT, [(1, rest)])


def route(nc, co, name, logits, picks, tiles, ids, weight, slot_of, token_of, expert_of):
    with phase(co, name) as ph:
        left = ph.sb("left", [P, NT, EXP])
        best = ph.sb("best", [P, picks, NT])
        pick = [ph.sb(f"pick{i}", [P, NT, EXP]) for i in range(picks)]
        member = ph.sb("member", [P, EXP, NT])
        rank, slot, tmp = ph.sb("rank", [P, EXP, NT]), ph.sb("slot", [P, NT, EXP]), ph.sb("tmp", [P, NT, EXP])
        order = ph.sb("order", [P, 1, EXP])
        col = ph.sb("col", [P, NT])
        valid, missing = ph.sb("valid", [P, NT]), ph.sb("missing", [P, NT])
        token = ph.sb("token", [P, NT])
        count, total, ntile, end = (ph.sb(n, [P, EXP]) for n in ("count", "total", "ntile", "end"))
        total_i = ph.sb("total_i", [P, EXP], I32)
        begin = ph.sb("begin", [P, 1, EXP])
        zeros = ph.sb("zeros", [P, NT])
        slots, slot_i = ph.sb("slots", [P, picks, NT]), ph.sb("slot_i", [P, picks, NT], U32)
        ring_i, ring_t = ph.sb("ring_i", [P, 5], U32), ph.sb("ring_t", [P, 5])
        past = ph.sb("past", [1, tiles, EXP])
        exp_f = ph.sb("exp_f", [1, tiles])
        back = ph.sb("back", [tiles, P])
        ps_c, ps_b = ph.ps("ps_c", [P, 512]), ph.ps("ps_b", [P, 512])
        iot, chain, mm, zeroed, exps, sloted, cols, loaded, seen, conv = (ph.sem(n) for n in (
            "iot", "chain", "mm", "zeroed", "exps", "sloted", "cols", "loaded", "seen", "conv"))
        placed = ph.gp_dma_sem(0)
        bcast = lambda ap: ap.to_broadcast([P, NT, EXP])
        with nc.Block() as block:
            @block.vector
            def _(dve):
                n = [0]

                def step(ins):
                    n[0] += 1
                    ins.then_inc(chain, 1)
                    dve.wait_ge(chain, n[0])

                dve.memset(zeros[:, :], 0.0)
                step(dve.memset(valid[:, :], 1.0))
                step(dve.tensor_scalar(valid[:, NT - 1:NT], co.rowno[:, :], float(LAST), None, ALU.is_lt))
                step(dve.tensor_scalar(missing[:, :], valid[:, :], -1e5, 1e5, ALU.mult, ALU.add))
                step(dve.tensor_scalar(order[:, 0, :], co.iota[:, 0:EXP], -1.0, float(EXP), ALU.mult, ALU.add))
                dve.wait_ge(iot, 1)
                source = logits
                for i in range(picks):
                    step(dve.tensor_reduce(best[:, i, :], source[:, :, :], AX.X, ALU.max))
                    step(dve.tensor_tensor(tmp[:, :, :], source[:, :, :], bcast(best[:, i, :].unsqueeze(2)), ALU.is_equal))
                    step(dve.tensor_tensor(tmp[:, :, :], tmp[:, :, :], bcast(order[:, :, :]), ALU.mult))
                    step(dve.tensor_reduce(col[:, :], tmp[:, :, :], AX.X, ALU.max))
                    step(dve.tensor_tensor(pick[i][:, :, :], tmp[:, :, :], bcast(col[:, :].unsqueeze(2)), ALU.is_equal))
                    if i + 1 < picks:
                        step(dve.scalar_tensor_tensor(out=left[:, :, :], in0=pick[i][:, :, :], scalar=-BIG, in1=source[:, :, :],
                                                      op0=ALU.mult, op1=ALU.add))
                        source = left
                if picks == 1:
                    step(dve.tensor_tensor(left[:, :, :], logits[:, :, :], bcast(best[:, 0, :].unsqueeze(2)), ALU.subtract))
                    dve.wait_ge(exps, 1)
                    step(dve.reduce_sum(col[:, :], tmp[:, :, :], AX.X))
                    step(dve.reciprocal(weight[:, 0, :], col[:, :]))
                else:
                    step(dve.tensor_tensor(col[:, :], best[:, 1, :], best[:, 0, :], ALU.subtract))
                    dve.wait_ge(exps, 1)
                    step(dve.tensor_scalar(col[:, :], best[:, 1, :], 1.0, None, ALU.add))
                    step(dve.reciprocal(weight[:, 0, :], col[:, :]))
                    step(dve.tensor_tensor(weight[:, 1, :], best[:, 1, :], weight[:, 0, :], ALU.mult))
                for i in range(picks):
                    step(dve.tensor_tensor(pick[i][:, :, :], pick[i][:, :, :], bcast(valid[:, :].unsqueeze(2)), ALU.mult))
                turned = lambda ap: ap.rearrange("p t e -> p e t")
                if picks == 1:
                    step(dve.tensor_copy(member[:, :, :], turned(pick[0][:, :, :])))
                else:
                    step(dve.tensor_tensor(member[:, :, :], turned(pick[0][:, :, :]), turned(pick[1][:, :, :]), ALU.add))
                for e in range(EXP):
                    step(dve.tensor_tensor_scan(rank[:, e, :], member[:, e, :], zeros[:, :], 0.0, ALU.add, ALU.add))
                step(dve.tensor_copy(count[:, :], rank[:, :, NT - 1]))
                dve.sem_inc(sloted, 1)
                dve.wait_ge(mm, 1)
                step(dve.tensor_scalar(total_i[:, :], ps_c[:, EXP:2 * EXP], float(P - 1), None, ALU.add))
                step(dve.tensor_scalar(total_i[:, :], total_i[:, :], 7, None, ALU.arith_shift_right))
                step(dve.tensor_copy(ntile[:, :], total_i[:, :]))
                step(dve.tensor_tensor_scan(end[:, :], ntile[:, :], zeros[:, 0:EXP], 0.0, ALU.add, ALU.add))
                step(dve.tensor_tensor(begin[:, 0, :], end[:, :], ntile[:, :], ALU.subtract))
                step(dve.scalar_tensor_tensor(out=begin[:, 0, :], in0=begin[:, 0, :], scalar=float(P), in1=ps_c[:, 0:EXP],
                                              op0=ALU.mult, op1=ALU.add))
                step(dve.tensor_tensor(slot[:, :, :], rank[:, :, :].rearrange("p e t -> p t e"), bcast(begin[:, :, :]), ALU.add))
                for i in range(picks):
                    step(dve.tensor_tensor(tmp[:, :, :], slot[:, :, :], pick[i][:, :, :], ALU.mult))
                    step(dve.reduce_sum(slots[:, i, :], tmp[:, :, :], AX.X))
                    step(dve.scalar_tensor_tensor(out=slot_i[:, i, :], in0=slots[:, i, :], scalar=-1.0, in1=missing[:, :],
                                                  op0=ALU.add, op1=ALU.add))
                    step(dve.tensor_scalar(slot_of[:, i, :], slots[:, i, :], -1.0, 0.0, ALU.add, ALU.max))
                dve.sem_inc(sloted, 1)
                step(dve.tensor_tensor(past[:, :, :], co.iota[0:1, 0:tiles].unsqueeze(2).to_broadcast([1, tiles, EXP]),
                                       end[0:1, :].unsqueeze(1).to_broadcast([1, tiles, EXP]), ALU.is_ge))
                step(dve.reduce_sum(exp_f[:, :], past[:, :, :], AX.X))
                step(dve.tensor_scalar(expert_of[:, :], exp_f[:, :], float(EXP - 1), None, ALU.min))
                dve.wait_ge(mm, 2)
                dve.tensor_copy(token_of[:, :], ps_b[:, 0:tiles]).then_inc(conv, 1)

            @block.scalar
            def _(act):
                act.preload_act_table(ACT.Exp)
                if picks == 1:
                    act.wait_ge(chain, 10)
                    act.activation(tmp[:, :, :], left[:, :, :], ACT.Exp).then_inc(exps, 1)
                else:
                    act.wait_ge(chain, 16)
                    act.activation(best[:, 1, :], col[:, :], ACT.Exp).then_inc(exps, 1)

            @block.tensor
            def _(pe):
                pe.wait_ge(sloted, 1)
                pe.matmul(ps_c[:, 0:EXP], co.before[:, :], count[:, :], start=True, stop=True)
                pe.matmul(ps_c[:, EXP:2 * EXP], co.ones[:, :], count[:, :], start=True, stop=True).then_inc(mm, 1)
                pe.wait_ge(loaded, 16)
                pe.transpose(ps_b[:, 0:tiles], back[:, :], co.ident[0:tiles, 0:tiles]).then_inc(mm, 1)

            @block.gpsimd
            def _(gp):
                gp.iota(token[:, :], pattern=[[P, NT]], base=0, channel_multiplier=1, allow_small_or_imprecise_dtypes=True)\
                  .then_inc(iot, 1)
                gp.memset(back[:, :], 0.0).then_inc(zeroed, 1)
                gp.wait_ge(iot, 1)
                gp.wait_ge(sloted, 2)
                gp.wait_ge(zeroed, 17)
                for i in range(picks):
                    with gp.Fori(0, NT // 5) as t:
                        gp.tensor_copy(ring_i[:, :], slot_i[:, i, bass.ds(t * 5, 5)]).then_inc(cols, 1)
                        gp.tensor_copy(ring_t[:, :], token[:, bass.ds(t * 5, 5)]).then_inc(cols, 1)
                        gp.wait_ge(cols, t * 2 + (2 + i * 2 * (NT // 5)))
                        gp.sem_inc(seen, 1)
                        for k in range(5):
                            gp.indirect_dma_start(ids.rearrange("(s a) -> s a", a=1),
                                                  bass.IndirectOffsetOnAxis(ap=ring_i[:, k:k + 1], axis=0),
                                                  ring_t[:, k:k + 1], None, bounds_check=tiles * P - 1,
                                                  oob_is_err=False).then_inc(placed, 16)
                        gp.wait_ge(placed, t * 80 + (80 + i * 80 * (NT // 5)))
                        gp.sem_inc(seen, 1)

            @block.sync
            def _(sp):
                sp.wait_ge(zeroed, 1)
                sp.dma_start(ids.rearrange("(s p) -> s p", p=P), back[:, :]).then_inc(zeroed, 16)
                sp.wait_ge(placed, picks * NT * 16)
                sp.dma_start(back[:, :], ids.rearrange("(s p) -> s p", p=P)).then_inc(loaded, 16)
                sp.wait_ge(loaded, 16)


def experts(nc, co, name, tiles, table, result, token_of, expert_of, a):
    shared = name == "exp0"
    HK = HID1 // P
    H2 = HK // 2
    HH = HID1 // 2
    with phase(co, name) as ph:
        w1 = ph.sb("w1", [P, 1 if shared else EXP, KD, HID1])
        w2 = ph.sb("w2", [P, EXP, HK, D])
        b2 = ph.sb("b2", [P, EXP, D])
        if shared:
            b1 = ph.sb("b1", [P, HK])
        else:
            b1 = ph.sb("b1", [3, EXP, HID1], BF16)
            ln_g, ln_b = ph.sb("ln_g", [P, KD, EXP]), ph.sb("ln_b", [P, KD, EXP])
            hid = [ph.sb(f"hid{i}", [P, HH]) for i in range(2)]
            ps_t = [ph.ps(f"ps_t{i}", [P, H2, P]) for i in range(2)]
        index, rows = ph.sb("index", [P, 1], U32), ph.sb("rows", [P, D])
        xt, ht, y = ph.sb("xt", [P, KD, P]), ph.sb("ht", [P, HK, P]), ph.sb("y", [P, 1, D])
        ps_x, ps_y = ph.ps("ps_x", [P, 512]), ph.ps("ps_y", [P, 512])
        ps_h = [ph.ps(f"ps_h{i}", [P, H2, P]) for i in range(2)]
        loaded, indexed, turned, out, done, stored, seen = (ph.sem(n) for n in (
            "loaded", "indexed", "turned", "out", "done", "stored", "seen"))
        got = ph.gp_dma_sem(0)
        made, bent, used, flipped, spread = ([ph.sem(f"{n}{i}") for i in range(2)] for n in
                                             ("made", "bent", "used", "flipped", "spread"))
        LOADS = 16 * (5 if shared else 2 * EXP + 6)
        with nc.Block() as block:
            @block.sync
            def _(sp):
                if shared:
                    sp.dma_start(w1[:, 0, :, :], a["L0_ffn_W1"].rearrange("(k p) d -> p k d", p=P)).then_inc(loaded, 16)
                    with nc.allow_non_contiguous_dma(reason="a bias with its features on partitions"):
                        sp.dma_start(b1[:, :], a["L0_ffn_b1"].rearrange("(k p) -> p k", p=P)).then_inc(loaded, 16)
                    for h in range(2):
                        sp.dma_start(w2[:, h * 4:h * 4 + 4, :, :], a["L0_ffn_Wd"][h * 4:h * 4 + 4].rearrange("e (k p) d -> p e k d", p=P))\
                          .then_inc(loaded, 16)
                    sp.dma_start(b2[:, :, :].rearrange("p e d -> p (e d)"), row_on_all(a["L0_ffn_bd"].rearrange("e d -> (e d)"), EXP * D))\
                      .then_inc(loaded, 16)
                else:
                    for e in range(EXP):
                        sp.dma_start(w1[:, e, :, :], a["L1_ffn_W1"][e].rearrange("(k p) d -> p k d", p=P)).then_inc(loaded, 16)
                        sp.dma_start(w2[:, e, :, :], a["L1_ffn_W2"][e].rearrange("(k p) d -> p k d", p=P)).then_inc(loaded, 16)
                    with nc.allow_non_contiguous_dma(reason="an affine map with its features on partitions"):
                        for k in range(KD):
                            sp.dma_start(ln_g[:, k, :], a["L1_ffn_ln_g"][:, k * P:(k + 1) * P].rearrange("e p -> p e")).then_inc(loaded, 16)
                            sp.dma_start(ln_b[:, k, :], a["L1_ffn_ln_b"][:, k * P:(k + 1) * P].rearrange("e p -> p e")).then_inc(loaded, 16)
                    sp.dma_start(b1[:, :, :].rearrange("q e d -> q (e d)"), a["b1_parts"]).then_inc(loaded, 16)
                    sp.dma_start(b2[:, :, :].rearrange("p e d -> p (e d)"), row_on_all(a["L1_ffn_b2"].rearrange("e d -> (e d)"), EXP * D))\
                      .then_inc(loaded, 16)

                def store(s):
                    sp.wait_ge(done, s + 1)
                    sp.dma_start(result[bass.ds(s * P, P), :], y[:, 0, :]).then_inc(stored, 16)

                over_tiles(sp, tiles, [(0, store)])
                sp.wait_ge(stored, 16 * tiles)

            @block.gpsimd
            def _(gp):
                def gather(s):
                    at_least(gp, turned, s)
                    gp.sem_inc(seen, 1)
                    gp.tensor_copy(index[:, :], token_of[:, bass.ds(s, 1)]).then_inc(indexed, 1)
                    gp.wait_ge(indexed, s + 1)
                    gp.sem_inc(seen, 1)
                    gp.indirect_dma_start(rows[:, :], None, table, bass.IndirectOffsetOnAxis(ap=index[:, 0:1], axis=0)).then_inc(got, 16)

                over_tiles(gp, tiles, [(0, gather)])

            def expert(eng, s):
                return eng.value_load(expert_of[0:1, bass.ds(s, 1)], min_val=0, max_val=EXP - 1)

            @block.tensor
            def _(pe):
                pe.wait_ge(loaded, LOADS)

                def turn(s):
                    pe.wait_ge(got, 16 * s + 16)
                    at_least(pe, out, s)
                    for k in range(KD):
                        last = pe.transpose(ps_x[:, k * P:(k + 1) * P], rows[:, k * P:(k + 1) * P], co.ident[:, :])
                    last.then_inc(turned, 1)

                def up(i):
                    def body(s):
                        e = None if shared else expert(pe, s)
                        pe.wait_ge(out, s + 1)
                        at_least(pe, bent[i], s)
                        if shared:
                            for m in range(H2):
                                for k in range(KD):
                                    last = pe.matmul(ps_h[i][:, m, :], w1[:, 0, k, (i * H2 + m) * P:(i * H2 + m + 1) * P],
                                                     xt[:, k, :], start=(k == 0), stop=(k == KD - 1))
                        else:
                            where = ps_h[i][:, :, :].rearrange("p m c -> p (m c)").unsqueeze(1)
                            pe.matmul(where, co.ones3[:, :], b1[:, bass.ds(e, 1), i * HH:(i + 1) * HH], start=True, stop=False)
                            for k in range(KD):
                                last = pe.matmul(where, xt[:, k, :], w1[:, bass.ds(e, 1), k, i * HH:(i + 1) * HH],
                                                 start=False, stop=(k == KD - 1))
                        last.then_inc(made[i], 1)
                    return body

                def flip(i):
                    def body(s):
                        pe.wait_ge(bent[i], s + 1)
                        at_least(pe, spread[i], s)
                        for m in range(H2):
                            last = pe.transpose(ps_t[i][:, m, :], hid[i][:, m * P:(m + 1) * P], co.ident[:, :])
                        last.then_inc(flipped[i], 1)
                    return body

                def down(i):
                    def body(s):
                        e = expert(pe, s)
                        pe.wait_ge(bent[i] if shared else spread[i], s + 1)
                        if i == 0:
                            at_least(pe, done, s)
                        for m in range(i * H2, (i + 1) * H2):
                            last = pe.matmul(ps_y[:, 0:D].unsqueeze(1), ht[:, m, :], w2[:, bass.ds(e, 1), m, :],
                                             start=(m == 0), stop=(m == HK - 1))
                        last.then_inc(used[i], 1)
                    return body

                if shared:
                    over_tiles(pe, tiles, [(1, up(0)), (2, down(1)), (1, up(1)), (1, down(0)), (0, turn)])
                else:
                    over_tiles(pe, tiles, [(1, up(0)), (2, down(0)), (1, up(1)), (2, down(1)), (0, turn), (1, flip(0)), (1, flip(1))])

            @block.scalar
            def _(act):
                act.preload_act_table(ACT.Gelu)
                act.wait_ge(loaded, LOADS)

                def bend(i):
                    def body(s):
                        act.wait_ge(made[i], s + 1)
                        if shared:
                            at_least(act, used[i], s)
                            for m in range(H2):
                                last = act.activation(ht[:, i * H2 + m, :], ps_h[i][:, m, :], ACT.Gelu,
                                                      bias=b1[:, i * H2 + m:i * H2 + m + 1])
                        else:
                            at_least(act, flipped[i], s)
                            last = act.activation(hid[i][:, :], ps_h[i][:, :, :].rearrange("p m c -> p (m c)"), ACT.Gelu)
                        last.then_inc(bent[i], 1)
                    return body

                over_tiles(act, tiles, [(1, bend(0)), (1, bend(1))])

            @block.vector
            def _(dve):
                dve.wait_ge(loaded, LOADS)

                def evacuate(s):
                    if not shared:
                        e = expert(dve, s)
                    dve.wait_ge(turned, s + 1)
                    at_least(dve, made[1], s)
                    if shared:
                        dve.tensor_copy(xt[:, :, :], ps_x[:, 0:D].rearrange("p (k c) -> p k c", k=KD)).then_inc(out, 1)
                    else:
                        for k in range(KD):
                            last = dve.tensor_scalar(xt[:, k, :], ps_x[:, k * P:(k + 1) * P], ln_g[:, k, bass.ds(e, 1)],
                                                     ln_b[:, k, bass.ds(e, 1)], ALU.mult, ALU.add)
                        last.then_inc(out, 1)

                def unflip(i):
                    def body(s):
                        dve.wait_ge(flipped[i], s + 1)
                        at_least(dve, used[i], s)
                        dve.tensor_copy(ht[:, i * H2:(i + 1) * H2, :], ps_t[i][:, :, :]).then_inc(spread[i], 1)
                    return body

                def rest(s):
                    e = expert(dve, s)
                    dve.wait_ge(used[1], s + 1)
                    at_least(dve, stored, 16 * s)
                    dve.tensor_tensor(y[:, :, :], ps_y[:, 0:D].unsqueeze(1), b2[:, bass.ds(e, 1), :], ALU.add).then_inc(done, 1)

                if shared:
                    over_tiles(dve, tiles, [(2, rest), (0, evacuate)])
                else:
                    over_tiles(dve, tiles, [(2, rest), (0, evacuate), (1, unflip(0)), (1, unflip(1))])


def combine(nc, co, name, picks, result, slot_of, weight):
    with phase(co, name) as ph:
        R = 5
        ring = ph.sb("ring", [P, R], U32)
        rows = [ph.sb(f"rows{k}", [P, 1, D]) for k in range(R)]
        got = [ph.gp_dma_sem(k) for k in range(R)]
        cols, seen, added = ph.sem("cols"), ph.sem("seen"), ph.sem("added")
        turns = NT // R
        with nc.Block() as block:
            @block.gpsimd
            def _(gp):
                for i in range(picks):
                    with gp.Fori(0, turns) as t:
                        gp.wait_ge(added, t * R + (i * NT + 1))
                        gp.sem_inc(seen, 1)
                        gp.tensor_copy(ring[:, :], slot_of[:, i, bass.ds(t * R, R)]).then_inc(cols, 1)
                        gp.wait_ge(cols, t + (i * turns + 1))
                        gp.sem_inc(seen, 1)
                        for k in range(R):
                            gp.indirect_dma_start(rows[k][:, 0, :], None, result,
                                                  bass.IndirectOffsetOnAxis(ap=ring[:, k:k + 1], axis=0)).then_inc(got[k], 16)

            @block.vector
            def _(dve):
                dve.sem_inc(added, 1)
                for i in range(picks):
                    with dve.Fori(0, turns) as t:
                        for k in range(R):
                            mine = co.x[:, bass.ds(t * R + k, 1), :]
                            dve.wait_ge(got[k], t * 16 + (i * turns * 16 + 16))
                            if i:
                                dve.wait_ge(added, t * R + k + ((i - 1) * NT + 2))
                            dve.scalar_tensor_tensor(out=mine, in0=rows[k][:, :, :], scalar=weight[:, i, bass.ds(t * R + k, 1)],
                                                     in1=mine, op0=ALU.mult, op1=ALU.add).then_inc(added, 1)
def split_bias(nc, co, bias, parts):
    n = bias.shape[0] // P
    with phase(co, "bias") as ph:
        whole, rest = ph.sb("whole", [P, n]), ph.sb("rest", [P, n])
        part = [ph.sb(f"part{i}", [P, n], BF16) for i in range(3)]
        loaded, made, stored = ph.sem("loaded"), ph.sem("made"), ph.sem("stored")
        with nc.Block() as block:
            @block.sync
            def _(sp):
                sp.dma_start(whole[:, :], bias.rearrange("(p n) -> p n", p=P)).then_inc(loaded, 16)
                sp.wait_ge(made, 5)
                for i in range(3):
                    sp.dma_start(parts[i, :].rearrange("(p n) -> p n", p=P), part[i][:, :]).then_inc(stored, 16)
                sp.wait_ge(stored, 48)

            @block.vector
            def _(dve):
                dve.wait_ge(loaded, 16)
                dve.tensor_copy(part[0][:, :], whole[:, :]).then_inc(made, 1)
                dve.wait_ge(made, 1)
                dve.tensor_tensor(rest[:, :], whole[:, :], part[0][:, :], ALU.subtract).then_inc(made, 1)
                dve.wait_ge(made, 2)
                dve.tensor_copy(part[1][:, :], rest[:, :]).then_inc(made, 1)
                dve.wait_ge(made, 3)
                dve.tensor_tensor(rest[:, :], rest[:, :], part[1][:, :], ALU.subtract).then_inc(made, 1)
                dve.wait_ge(made, 4)
                dve.tensor_copy(part[2][:, :], rest[:, :]).then_inc(made, 1)


def gat_inputs(nc, co, name, h, a, layer, heads, table, r_parts, att, acc, top):
    ch = D // heads
    W = D + heads
    junk = acc.shape[2] - heads * (ch + 1)
    with phase(co, name) as ph:
        w = {s: ph.sb("w" + s, [P, KD, W]) for s in "lr"}
        prod = ph.sb("prod", [P, KD, D])
        folded = {s: ph.sb("folded" + s, [P, KD, heads]) for s in "lr"}
        attb, att4 = ph.sb("attb", [P, 1, D]), ph.sb("att4", [P, 1, D])
        cur, xt = ph.sb("cur", [P, 1, D]), ph.sb("xt", [P, KD, P])
        xl = ph.sb("xl", [P, NT, W])
        arf, mags = ph.sb("arf", [P, NT, heads]), ph.sb("mags", [P, NT, heads])
        self_l, first, gap = (ph.sb(n, [P, NT, heads]) for n in ("self_l", "first", "gap"))
        weight = ph.sb("weight", [P, NT, heads])
        topb = ph.sb("topb", [P, NT, heads], BF16)
        rest = ph.sb("rest", [P, 1, W])
        both, size = ph.sb("both", [P, 1, D]), ph.sb("size", [P, 1, D])
        ps_x, ps_l, ps_r = (ph.ps(n, [P, 512]) for n in ("ps_x", "ps_l", "ps_r"))
        loaded, cleared, ready, chain, staged, turned, out, made, copied, split, summed, tabled, seen, self_, exped = (
            ph.sem(n) for n in ("loaded", "cleared", "ready", "chain", "staged", "turned", "out", "made", "copied", "split",
                                "summed", "tabled", "seen", "self", "exped"))
        with nc.Block() as block:
            @block.sync
            def _(sp):
                for s in "lr":
                    sp.dma_start(w[s][:, :, 0:D], a[f"L1_gnn_W{s}{layer}"].rearrange("(k p) d -> p k d", p=P)).then_inc(loaded, 16)
                flat = a[f"L1_gnn_att{layer}"].rearrange("h c -> (h c)")
                sp.dma_start(attb[:, 0, :], row_on_all(flat, D)).then_inc(loaded, 16)
                sp.wait_ge(cleared, 1)
                with nc.allow_non_contiguous_dma(reason="a vector with its features on partitions"):
                    if heads == 1:
                        sp.dma_start(att[:, :, 0], flat.rearrange("(k p) -> p k", p=P)).then_inc(loaded, 16)
                    else:
                        for i in range(heads):
                            at = i * ch % P
                            sp.dma_start(att[at:at + ch, i * ch // P, i:i + 1], flat[i * ch:(i + 1) * ch].rearrange("(p a) -> p a", a=1))\
                              .then_inc(loaded, 16)
                sp.wait_ge(copied, NT)
                sp.dma_start(table.rearrange("(t p) d -> p t d", p=P), xl[:, :, :]).then_inc(tabled, 16)
                sp.wait_ge(tabled, 16)

            @block.gpsimd
            def _(gp):
                def stage(t):
                    at_least(gp, turned, t)
                    gp.sem_inc(seen, 1)
                    gp.tensor_copy(cur[:, :, :], h[:, bass.ds(t, 1), :]).then_inc(staged, 1)

                over_tiles(gp, NT, [(0, stage)])

            @block.tensor
            def _(pe):
                pe.wait_ge(ready, 1)

                def turn(t):
                    pe.wait_ge(staged, t + 1)
                    at_least(pe, out, t)
                    for k in range(KD):
                        last = pe.transpose(ps_x[:, k * P:(k + 1) * P], cur[:, 0, k * P:(k + 1) * P], co.ident[:, :])
                    last.then_inc(turned, 1)

                def project(t):
                    pe.wait_ge(out, t + 1)
                    at_least(pe, copied, t)
                    at_least(pe, summed, t)
                    for s, where in (("l", ps_l), ("r", ps_r)):
                        for k in range(KD):
                            last = pe.matmul(where[:, 0:W], xt[:, k, :], w[s][:, k, :], start=(k == 0), stop=(k == KD - 1))
                    last.then_inc(made, 1)

                over_tiles(pe, NT, [(0, turn), (1, project)])

            @block.scalar
            def _(act):
                act.preload_act_table(ACT.Exp)

                def evacuate(t):
                    act.wait_ge(turned, t + 1)
                    at_least(act, made, t)
                    act.copy(xt[:, :, :], ps_x[:, 0:D].rearrange("p (k c) -> p k c", k=KD)).then_inc(out, 1)

                def copy(t):
                    act.wait_ge(made, t + 1)
                    act.copy(r_parts[:, bass.ds(t, 1), 0, :], ps_r[:, 0:W].unsqueeze(1))
                    act.copy(arf[:, bass.ds(t, 1), :], ps_r[:, D:W].unsqueeze(1))
                    act.copy(xl[:, bass.ds(t, 1), :], ps_l[:, 0:W].unsqueeze(1)).then_inc(copied, 1)

                over_tiles(act, NT, [(1, copy), (0, evacuate)])
                act.wait_ge(self_, 4)
                act.activation(weight[:, :, :], gap[:, :, :], ACT.Exp).then_inc(exped, 1)

            @block.vector
            def _(dve):
                n = [0]

                def step(ins):
                    n[0] += 1
                    ins.then_inc(chain, 1)
                    dve.wait_ge(chain, n[0])

                dve.memset(att[:, :, :], 0.0).then_inc(cleared, 1)
                if junk:
                    dve.memset(acc[:, :, D:D + junk], 0.0)
                dve.wait_ge(loaded, 16 * (3 + heads))
                step(dve.tensor_scalar(att[:, :, :], att[:, :, :], 0.4, None, ALU.mult))
                step(dve.tensor_scalar(att4[:, :, :], attb[:, :, :], 0.4, None, ALU.mult))
                for s in "lr":
                    step(dve.tensor_tensor(prod[:, :, :], w[s][:, :, 0:D], attb[:, :, :].to_broadcast([P, KD, D]), ALU.mult))
                    step(dve.tensor_reduce(folded[s][:, :, :], prod[:, :, :].rearrange("p k (h c) -> p k h c", h=heads), AX.X, ALU.add))
                    step(dve.tensor_scalar(w[s][:, :, D:W], folded[s][:, :, :], 0.6, None, ALU.mult))
                dve.sem_inc(ready, 1)
                base = n[0]

                def sums(t):
                    dve.wait_ge(copied, t + 1)
                    dve.tensor_tensor(both[:, :, :], xl[:, bass.ds(t, 1), 0:D], ps_r[:, 0:D].unsqueeze(1), ALU.add).then_inc(split, 1)
                    part = lambda i: r_parts[:, bass.ds(t, 1), i, :]
                    dve.tensor_tensor(rest[:, :, :], ps_r[:, 0:W].unsqueeze(1), part(0), ALU.subtract).then_inc(summed, 1)
                    dve.wait_ge(split, 4 * t + 1)
                    dve.scalar_tensor_tensor(out=size[:, :, :], in0=both[:, :, :], scalar=-1.0, in1=both[:, :, :],
                                             op0=ALU.mult, op1=ALU.max).then_inc(split, 1)
                    dve.wait_ge(summed, t + 1)
                    dve.tensor_scalar(part(1), rest[:, :, :], 1.0, None, ALU.mult).then_inc(chain, 1)
                    dve.wait_ge(split, 4 * t + 2)
                    dve.tensor_tensor(size[:, :, :], size[:, :, :], att4[:, :, :], ALU.mult).then_inc(split, 1)
                    dve.wait_ge(split, 4 * t + 3)
                    dve.tensor_reduce(mags[:, bass.ds(t, 1), :], size[:, :, :].rearrange("p a (h c) -> p a h c", h=heads), AX.X, ALU.add)\
                       .then_inc(split, 1)
                    dve.wait_ge(chain, t * 2 + (base + 1))
                    dve.tensor_tensor(part(2), rest[:, :, :], part(1), ALU.subtract).then_inc(chain, 1)
                    dve.wait_ge(split, 4 * t + 4)
                    dve.wait_ge(chain, t * 2 + (base + 2))

                over_tiles(dve, NT, [(1, sums)])
                dve.tensor_tensor(self_l[:, :, :], xl[:, :, D:W], arf[:, :, :], ALU.add).then_inc(self_, 1)
                dve.wait_ge(self_, 1)
                dve.tensor_tensor(first[:, :, :], self_l[:, :, :], mags[:, :, :], ALU.add).then_inc(self_, 1)
                dve.wait_ge(self_, 2)
                dve.tensor_copy(topb[:, :, :], first[:, :, :]).then_inc(self_, 1)
                dve.wait_ge(self_, 3)
                dve.tensor_copy(top[:, :, :], topb[:, :, :])
                dve.tensor_tensor(gap[:, :, :], first[:, :, :], topb[:, :, :], ALU.subtract).then_inc(self_, 1)
                dve.wait_ge(exped, 1)
                for i in range(heads):
                    at = i * (ch + 1)
                    dve.tensor_tensor(acc[:, :, at:at + ch], xl[:, :, i * ch:(i + 1) * ch],
                                      weight[:, :, i:i + 1].to_broadcast([P, NT, ch]), ALU.mult)
                    dve.tensor_copy(acc[:, :, at + ch + junk:at + ch + junk + 1], weight[:, :, i:i + 1])


def gat_output(nc, co, name, acc, bias, heads, there, elu):
    ch = D // heads
    junk = acc.shape[2] - heads * (ch + 1)
    C = 5
    with phase(co, name) as ph:
        b = ph.sb("b", [P, 1, D])
        inv = ph.sb("inv", [P, NT, heads])
        o, low, high = ph.sb("o", [P, C, D]), ph.sb("low", [P, C, D]), ph.sb("high", [P, C, D])
        loaded, inverse, scaled, biased, lowered, exped, done = (ph.sem(n) for n in (
            "loaded", "inverse", "scaled", "biased", "lowered", "exped", "done"))
        with nc.Block() as block:
            @block.sync
            def _(sp):
                sp.dma_start(b[:, 0, :], row_on_all(bias, D)).then_inc(loaded, 16)

            @block.vector
            def _(dve):
                wide = acc[:, :, 0:heads * (ch + 1)].rearrange("p t (h c) -> p t h c", h=heads)
                sums = acc[:, :, D + junk:D + junk + 1] if heads == 1 else wide[:, :, :, ch]
                dve.reciprocal(inv[:, :, :], sums).then_inc(inverse, 1)
                dve.wait_ge(inverse, 1)
                dve.wait_ge(loaded, 16)

                def scale(t):
                    at_least(dve, done, t)
                    for i in range(heads):
                        last = dve.tensor_tensor(o[:, :, i * ch:(i + 1) * ch], acc[:, bass.ds(t * C, C), i * (ch + 1):i * (ch + 1) + ch],
                                                 inv[:, bass.ds(t * C, C), i:i + 1].to_broadcast([P, C, ch]), ALU.mult)
                    last.then_inc(scaled, 1)
                    dve.wait_ge(scaled, t + 1)
                    dve.tensor_tensor(o[:, :, :], o[:, :, :], b[:, :, :].to_broadcast([P, C, D]), ALU.add).then_inc(biased, 1)
                    dve.wait_ge(biased, t + 1)
                    if elu:
                        at_least(dve, exped, t)
                        dve.tensor_scalar(low[:, :, :], o[:, :, :], 0.0, None, ALU.min).then_inc(lowered, 1)
                        dve.tensor_scalar(high[:, :, :], o[:, :, :], 0.0, -1.0, ALU.max, ALU.add).then_inc(lowered, 1)
                        dve.wait_ge(exped, t + 1)
                        dve.wait_ge(lowered, 2 * t + 2)
                        dve.tensor_tensor(there[:, bass.ds(t * C, C), :], low[:, :, :], high[:, :, :], ALU.add).then_inc(done, 1)
                    else:
                        at = there[:, bass.ds(t * C, C), :]
                        dve.tensor_tensor(at, at, o[:, :, :], ALU.add).then_inc(done, 1)

                over_tiles(dve, NT // C, [(0, scale)])

            if elu:
                @block.scalar
                def _(act):
                    act.preload_act_table(ACT.Exp)

                    def exp(t):
                        act.wait_ge(lowered, 2 * t + 2)
                        act.activation(low[:, :, :], low[:, :, :], ACT.Exp).then_inc(exped, 1)

                    over_tiles(act, NT // C, [(0, exp)])


def store_x(nc, co, out):
    with phase(co, "store") as ph:
        stored = ph.sem("stored")
        with nc.Block() as block:
            @block.sync
            def _(sp):
                sp.dma_start(out[0:(NT - 1) * P, :].rearrange("(t p) d -> p t d", p=P), co.x[:, 0:NT - 1, :]).then_inc(stored, 16)
                sp.dma_start(out[(NT - 1) * P:N, :], co.x[0:LAST, NT - 1, :]).then_inc(stored, 16)
                sp.wait_ge(stored, 32)


def gat_layer(nc, co, name, h, a, layer, heads, there, elu):
    width = D + 2 if heads == 1 else D + heads
    table = nc.dram_tensor(name + "_table", [NPAD, D + heads], F32, kind="Internal").ap()
    with co.scope():
        acc = co.sbuf(name + "_acc", [P, NT, width])
        top = co.sbuf(name + "_top", [P, NT, heads])
        att = co.sbuf(name + "_att", [P, KD, heads])
        r_parts = co.sbuf(name + "_r_parts", [P, NT, 3, D + heads], BF16)
        gat_inputs(nc, co, name + "_in", h, a, layer, heads, table, r_parts, att, acc, top)
        edge_pass(nc, co, name + "_edges", table, acc, top, heads, r_parts=r_parts, att=att)
        gat_output(nc, co, name + "_out", acc, a[f"L1_gnn_b{layer}"], heads, there, elu)


def routed_ffn(nc, co, which, a, picks, tiles):
    table = nc.dram_tensor(f"ffn{which}_table", [NPAD, D], F32, kind="Internal").ap()
    result = nc.dram_tensor(f"ffn{which}_result", [tiles * P, D], F32, kind="Internal").ap()
    ids = nc.dram_tensor(f"ffn{which}_ids", [tiles * P], F32, kind="Internal").ap()
    with co.scope():
        slot = co.sbuf(f"slot{which}", [P, picks, NT], U32)
        weight = co.sbuf(f"weight{which}", [P, picks, NT])
        token = co.sbuf(f"token{which}", [P, tiles], U32)
        expert = co.sbuf(f"expert{which}", [1, tiles], I32)
        with co.scope():
            h = co.sbuf(f"ffn_h{which}", [P, NT, D])
            logits = co.sbuf(f"logits{which}", [P, NT, EXP])
            layer_norm(nc, co, f"ffn_norm{which}", co.x, h)
            if which == 0:
                top1_logits(nc, co, h, a, logits, table)
            else:
                xn = co.sbuf("ffn_xn", [P, NT, D])
                layer_norm(nc, co, "expert_norm", h, xn)
                top2_logits(nc, co, h, xn, a, logits, table)
            route(nc, co, f"route{which}", logits, picks, tiles, ids, weight, slot, token, expert)
        experts(nc, co, f"exp{which}", tiles, table, result, token, expert, a)
        combine(nc, co, f"combine{which}", picks, result, slot, weight)


def attention_block(nc, co, a):
    table = nc.dram_tensor("attention_table", [NPAD, D], F32, kind="Internal").ap()
    with co.scope():
        xn = co.sbuf("xn", [P, NT, D])
        base = co.sbuf("base", [P, NT, D])
        with co.scope():
            q_parts = co.sbuf("q_parts", [P, NT, 3, D + 1], BF16)
            acc = co.sbuf("acc", [P, NT, D + 1])
            top = co.sbuf("top", [P, NT, 1])
            layer_norm(nc, co, "attention_norm", co.x, xn)
            attention_inputs(nc, co, xn, a, q_parts, base, table, acc, top)
            edge_pass(nc, co, "dot_edges", table, acc, top, 1, q_parts=q_parts)
            attention_output(nc, co, acc, base, a)
        layer_norm(nc, co, "inner_norm1", base, xn)
        attention_ffn(nc, co, xn, base, a)
        layer_norm(nc, co, "inner_norm2", base, xn)
        add_affine(nc, co, xn, a["L0_gnn_g2"], a["L0_gnn_b2"])


def build(nc, a, out):
    co = Core(nc)
    dram = lambda n, shape, dt=F32: nc.dram_tensor(n, shape, dt, kind="Internal").ap()
    sdst, ssrc, sweight = dram("sorted_dst", [EPAD], I32), dram("sorted_src", [EPAD], U32), dram("sorted_weight", [EPAD])
    a["b1_parts"] = dram("b1_parts", [3, EXP * HID1], BF16)
    with co.keep:
        constants(nc, co)
        split_bias(nc, co, a["L1_ffn_b1"].rearrange("e d -> (e d)"), a["b1_parts"])
        load_x(nc, co, a["x"])
        with co.scope():
            sort_edges(nc, co, a["dst"], a["src"], a["edge_weight"], sdst, ssrc, sweight)
            plan_steps(nc, co, sdst, ssrc, sweight, a["L0_gnn_we"], a["L0_gnn_be"])
            attention_block(nc, co, a)
            routed_ffn(nc, co, 0, a, 1, TOP1_TILES)
            with co.scope():
                h = co.sbuf("gat_h", [P, NT, D])
                layer_norm(nc, co, "gat_norm", co.x, h)
                gat_layer(nc, co, "gat1", h, a, 1, 4, h, True)
                gat_layer(nc, co, "gat2", h, a, 2, 1, co.x, False)
        routed_ffn(nc, co, 1, a, 2, TOP2_TILES)
        store_x(nc, co, out)


def kernel(**inputs):
    import concourse.bacc as bacc
    from concourse.bass_utils import run_bass_kernel_spmd as run

    nc = bacc.Bacc("TRN2", target_bir_lowering=False, num_devices=1)
    arrays = {k: np.ascontiguousarray(v) for k, v in inputs.items()}
    arrays["src"] = arrays["src"].view(np.uint32)
    arrays["L0_gnn_wk"] = np.ascontiguousarray(arrays["L0_gnn_wk"].T)
    args = {k: nc.dram_tensor(k, v.shape, mybir.dt.from_np(v.dtype), kind="ExternalInput").ap() for k, v in arrays.items()}
    out = nc.dram_tensor("out", (N, D), F32, kind="ExternalOutput").ap()
    build(nc, args, out)
    got = run(nc, [arrays], core_ids=[0])
    return got.results[0]["out"]
```

```python
from contextlib import ExitStack, contextmanager

import numpy as np

import concourse.bass as bass
from concourse import mybir

ALU = mybir.AluOpType
ACT = mybir.ActivationFunctionType
AX = mybir.AxisListType
F32 = mybir.dt.float32
BF16 = mybir.dt.bfloat16
U32 = mybir.dt.uint32
I32 = mybir.dt.int32

P = 128
N = 3125
D = 256
KD = D // P
NT = -(-N // P)
NPAD = NT * P
LAST = N - (NT - 1) * P
E = 50000
EP, EJ = 125, 400
EB = 256
NB = -(-E // EB)
STEPS = NB + NT - 1
EPAD = NB * EB
HB = NB // 2
BIG = float(2 ** 100)
NOWHERE = float(2 ** 20)
TILE_BITS, FIELDS = 5, 6
ROUNDS = 4
UNROLL = 5
EPS = 1e-5
HID0, HID1, EXP = 1024, 1024, 8
TOP1_TILES = (N + EXP * (P - 1)) // P
TOP2_TILES = (2 * N + EXP * (P - 1)) // P


class Core:

    def __init__(self, nc):
        self.nc = nc
        self.keep = ExitStack()
        self.fetched = [self.keep.enter_context(nc.semaphore(f"fetched{k}")) for k in range(2)]
        self.gp_dma = [self.keep.enter_context(nc.semaphore(f"gp_dma{k}")) for k in range(5)]

    @contextmanager
    def scope(self):
        outer, self.keep = self.keep, ExitStack()
        with self.keep:
            yield
        self.keep = outer

    def sbuf(self, name, shape, dt=F32):
        return self.keep.enter_context(self.nc.sbuf_tensor("kept_" + name, shape, dt))


@contextmanager
def phase(co, name):
    nc = co.nc
    sems, gp_dma = [], []
    with ExitStack() as ctx:
        class Ph:
            def sb(self, n, shape, dt=F32):
                return ctx.enter_context(nc.sbuf_tensor(f"{name}_{n}", shape, dt))

            def ps(self, n, shape, dt=F32):
                return ctx.enter_context(nc.psum_tensor(f"{name}_{n}", shape, dt))

            def sem(self, n):
                s = ctx.enter_context(nc.semaphore(f"{name}_{n}"))
                sems.append(s)
                return s

            def gp_dma_sem(self, k):
                gp_dma.append(co.gp_dma[k])
                return co.gp_dma[k]

        yield Ph()
        for s in sems:
            nc.sync.sem_clear(s)
        if gp_dma:
            nc.gpsimd.dma_reset()
        for s in gp_dma:
            nc.gpsimd.sem_clear(s)
        nc.all_engine_barrier()


def constants(nc, co):
    co.ident = co.sbuf("ident", [P, P])
    co.identb = co.sbuf("identb", [P, P], BF16)
    co.bigident = co.sbuf("bigident", [P, P], BF16)
    co.before = co.sbuf("before", [P, P])
    co.ones = co.sbuf("ones", [P, P])
    co.iota = co.sbuf("iota", [P, STEPS])
    co.iotab = co.sbuf("iotab", [P, P], BF16)
    co.rowno = co.sbuf("rowno", [P, 1])
    co.ones3 = co.sbuf("ones3", [3, P], BF16)
    with phase(co, "const") as ph:
        done = ph.sem("done")
        base = ph.sem("base")
        with nc.Block() as block:
            @block.gpsimd
            def _(gp):
                gp.memset(co.ident[:, :], 0.0).then_inc(base, 1)
                gp.memset(co.ones[:, :], 1.0).then_inc(base, 1)
                gp.iota(co.iota[:, :], pattern=[[1, STEPS]], base=0, channel_multiplier=0,
                        allow_small_or_imprecise_dtypes=True).then_inc(base, 1)
                gp.iota(co.rowno[:, :], pattern=[[0, 1]], base=0, channel_multiplier=1,
                        allow_small_or_imprecise_dtypes=True).then_inc(base, 1)
                gp.wait_ge(base, 4)
                gp.affine_select(out=co.before[:, :], in_=co.ones[:, :], compare_op=ALU.is_gt, fill=0.0,
                                 base=0, pattern=[[1, P]], channel_multiplier=-1).then_inc(base, 1)
                gp.affine_select(out=co.ident[:, :], in_=co.ident[:, :], compare_op=ALU.not_equal, fill=1.0,
                                 base=0, pattern=[[-1, P]], channel_multiplier=1).then_inc(base, 1)

            @block.vector
            def _(dve):
                dve.wait_ge(base, 6)
                dve.tensor_copy(co.identb[:, :], co.ident[:, :]).then_inc(done, 1)
                dve.tensor_scalar(co.bigident[:, :], co.ident[:, :], BIG, None, ALU.mult).then_inc(done, 1)
                dve.tensor_copy(co.iotab[:, :], co.iota[:, 0:P]).then_inc(done, 1)
                dve.memset(co.ones3[:, :], 1.0).then_inc(done, 1)
                dve.wait_ge(done, 4)


def pack(dve, step, words, numbers, moved, n, back):
    step(dve.memset(words[:, :], 0))
    for i in range(FIELDS):
        lo, hi = max(back - i, 0), n + back - i
        step(dve.tensor_scalar(moved[:, :], numbers[:, :], TILE_BITS * i, None, ALU.logical_shift_left))
        step(dve.tensor_tensor(words[:, lo:hi], words[:, lo:hi], moved[:, lo + i - back:n], ALU.bitwise_or))


def number_in(word, field, limit):
    return ((word >> TILE_BITS * field) & (2 ** TILE_BITS - 1)).with_bounds(min_val=0, max_val=limit - 1)


def sort_edges(nc, co, dst, src, weight, sdst, ssrc, sweight):
    co.count = co.sbuf("count", [NT, 1])
    co.first = co.sbuf("first", [NT, 1])
    with phase(co, "sort") as ph:
        d = ph.sb("d", [EP, EJ], I32)
        s = ph.sb("s", [EP, EJ], U32)
        w = ph.sb("w", [EP, EJ])
        bucket_i = ph.sb("bucket_i", [EP, EJ], I32)
        bucket = ph.sb("bucket", [EP, EJ + 1])
        next_i = ph.sb("next_i", [EP, 2], I32)
        member = ph.sb("member", [EP, EJ])
        rank = ph.sb("rank", [EP, EJ])
        slot = ph.sb("slot", [EP, EJ])
        slot_u = ph.sb("slot_u", [EP, EJ], U32)
        cnt = ph.sb("cnt", [EP, NT])
        excl = ph.sb("excl", [EP, NT])
        zero = ph.sb("zero", [EP, NT])
        offset = ph.sb("offset", [EP, NT])
        falls = ph.sb("falls", [EP, EJ])
        bad = ph.sb("bad", [EP, 1])
        flag = ph.sb("flag", [1, 1], I32)
        stage_i = ph.sb("stage_i", [EP, 1], U32)
        stage_d = ph.sb("stage_d", [EP, 1], I32)
        stage_s = ph.sb("stage_s", [EP, 1], U32)
        stage_w = ph.sb("stage_w", [EP, 1])
        pad = ph.sb("pad", [1, EPAD - E], I32)
        padz = ph.sb("padz", [1, EPAD - E], I32)
        psum = ph.ps("psum", [P, 512])
        loaded, chain, mm, copied, flagged = (ph.sem(n) for n in ("loaded", "chain", "mm", "copied", "flagged"))
        slots, staged, tick, padded = (ph.sem(n) for n in ("slots", "staged", "tick", "padded"))
        placed = ph.gp_dma_sem(0)
        with nc.Block() as block:
            @block.sync
            def _(sp):
                sp.dma_start(d[:, :], dst.rearrange("(p j) -> p j", j=EJ)).then_inc(loaded, 16)
                with nc.allow_non_contiguous_dma(reason="one edge of each row"):
                    sp.dma_start(next_i[0:EP - 1, 0:1], dst[EJ:E].rearrange("(p j) -> p j", j=EJ)[:, 0:1]).then_inc(loaded, 16)
                    sp.dma_start(next_i[EP - 1:EP, 0:1], dst[E - 1:E].rearrange("(p j) -> p j", j=1)).then_inc(loaded, 16)
                sp.dma_start(s[:, :], src.rearrange("(p j) -> p j", j=EJ)).then_inc(loaded, 16)
                sp.dma_start(w[:, :], weight.rearrange("(p j) -> p j", j=EJ)).then_inc(loaded, 16)
                sp.wait_ge(copied, 2)
                sp.dma_start(sdst[E:EPAD].rearrange("(a b) -> a b", a=1), pad[:, :]).then_inc(padded, 16)
                sp.dma_start(ssrc[E:EPAD].rearrange("(a b) -> a b", a=1), padz[:, :].bitcast(U32)).then_inc(padded, 16)
                sp.dma_start(sweight[E:EPAD].rearrange("(a b) -> a b", a=1), padz[:, :].bitcast(F32)).then_inc(padded, 16)
                sp.wait_ge(padded, 48)

            @block.vector
            def _(dve):
                dve.memset(pad[:, :], int(NOWHERE)).then_inc(copied, 1)
                dve.memset(padz[:, :], 0).then_inc(copied, 1)
                dve.memset(zero[:, :], 0.0).then_inc(chain, 1)
                dve.wait_ge(loaded, 80)
                dve.tensor_scalar(bucket_i[:, :], d[:, :], 7, None, ALU.arith_shift_right).then_inc(chain, 1)
                dve.tensor_scalar(next_i[:, 1:2], next_i[:, 0:1], 7, None, ALU.arith_shift_right).then_inc(chain, 1)
                dve.wait_ge(chain, 3)
                dve.tensor_copy(bucket[:, 0:EJ], bucket_i[:, :]).then_inc(chain, 1)
                dve.tensor_copy(bucket[:, EJ:EJ + 1], next_i[:, 1:2]).then_inc(chain, 1)
                dve.wait_ge(chain, 5)
                dve.tensor_tensor(falls[:, :], bucket[:, 0:EJ], bucket[:, 1:EJ + 1], ALU.is_gt).then_inc(chain, 1)
                for b in range(NT):
                    dve.wait_ge(chain, 6 + b)
                    dve.tensor_scalar(member[:, :], bucket[:, 0:EJ], float(b), None, ALU.is_equal, ALU.add,
                                      accum_out=cnt[:, b:b + 1]).then_inc(chain, 1)
                dve.wait_ge(chain, 6 + NT)
                dve.reduce_max(bad[:, :], falls[:, :], AX.X).then_inc(chain, 1)
                dve.tensor_tensor_scan(excl[:, :], cnt[:, :], zero[:, :], 0.0, ALU.add, ALU.add).then_inc(chain, 1)
                dve.wait_ge(chain, 8 + NT)
                dve.tensor_tensor(excl[:, :], excl[:, :], cnt[:, :], ALU.subtract).then_inc(chain, 1)
                dve.wait_ge(mm, 1)
                dve.tensor_copy(co.count[:, :], psum[0:NT, 0:1]).then_inc(copied, 1)
                dve.wait_ge(mm, 2)
                dve.tensor_copy(offset[:, :], psum[0:EP, 64:64 + NT]).then_inc(copied, 1)
                dve.tensor_copy(co.first[:, :], psum[0:NT, 128:129]).then_inc(copied, 1)
                dve.tensor_copy(flag[:, :], psum[0:1, 192:193]).then_inc(flagged, 1)
                dve.wait_ge(flagged, 1)
                unsorted = dve.value_load(flag[0:1, 0:1], min_val=0, max_val=EP)
                with dve.If(unsorted > 0):
                    dve.memset(slot[:, :], 0.0).then_inc(slots, 1)
                    dve.wait_ge(copied, 5)
                    for b in range(NT):
                        dve.tensor_scalar(member[:, :], bucket[:, 0:EJ], float(b), None, ALU.is_equal).then_inc(slots, 1)
                        dve.wait_ge(slots, 4 * b + 2)
                        dve.tensor_tensor_scan(rank[:, :], member[:, :], member[:, :], 0.0, ALU.add, ALU.bypass).then_inc(slots, 1)
                        dve.wait_ge(slots, 4 * b + 3)
                        dve.scalar_tensor_tensor(out=rank[:, :], in0=rank[:, :], scalar=offset[:, b:b + 1],
                                                 in1=member[:, :], op0=ALU.add, op1=ALU.mult).then_inc(slots, 1)
                        dve.wait_ge(slots, 4 * b + 4)
                        dve.tensor_tensor(slot[:, :], slot[:, :], rank[:, :], ALU.add).then_inc(slots, 1)
                        dve.wait_ge(slots, 4 * b + 5)
                    dve.tensor_scalar(slot_u[:, :], slot[:, :], -1.0, None, ALU.add).then_inc(slots, 1)
                with dve.Else():
                    dve.memset(slot[:, 0:1], 0.0).then_inc(slots, 1)

            @block.tensor
            def _(pe):
                pe.wait_ge(chain, 6 + NT)
                pe.matmul(psum[0:NT, 0:1], cnt[:, :], co.ones[0:EP, 0:1], start=True, stop=True).then_inc(mm, 1)
                pe.wait_ge(chain, 9 + NT)
                pe.wait_ge(copied, 3)
                pe.matmul(psum[0:EP, 64:64 + NT], co.before[0:EP, 0:EP], cnt[:, :], start=True, stop=False)
                pe.matmul(psum[0:EP, 64:64 + NT], co.ones[0:EP, 0:EP], excl[:, :], start=False, stop=True)
                pe.matmul(psum[0:NT, 128:129], co.before[0:NT, 0:NT], co.count[:, :], start=True, stop=True)
                pe.matmul(psum[0:1, 192:193], bad[:, :], co.ones[0:EP, 0:1], start=True, stop=True).then_inc(mm, 1)

            @block.gpsimd
            def _(gp):
                gp.wait_ge(flagged, 1)
                unsorted = gp.value_load(flag[0:1, 0:1], min_val=0, max_val=EP)
                with gp.If(unsorted > 0):
                    gp.wait_ge(slots, 4 * NT + 2)
                    gp.sem_inc(tick, 1)
                    with gp.Fori(0, EJ) as j:
                        gp.tensor_copy(stage_i[:, :], slot_u[:, bass.ds(j, 1)]).then_inc(staged, 1)
                        gp.tensor_copy(stage_d[:, :], d[:, bass.ds(j, 1)]).then_inc(staged, 1)
                        gp.tensor_copy(stage_s[:, :], s[:, bass.ds(j, 1)]).then_inc(staged, 1)
                        gp.tensor_copy(stage_w[:, :], w[:, bass.ds(j, 1)]).then_inc(staged, 1)
                        gp.wait_ge(staged, 4 * j + 4)
                        gp.sem_inc(tick, 1)
                        for there, value in ((sdst, stage_d), (ssrc, stage_s), (sweight, stage_w)):
                            gp.indirect_dma_start(there[0:E].rearrange("(a b) -> a b", b=1),
                                                  bass.IndirectOffsetOnAxis(ap=stage_i[:, 0:1], axis=0),
                                                  value[:, :], None).then_inc(placed, 16)
                        gp.wait_ge(placed, 48 * j + 48)
                        gp.sem_inc(tick, 1)
                with gp.Else():
                    for there, value in ((sdst, d), (ssrc, s), (sweight, w)):
                        gp.dma_start(there[0:E].rearrange("(p j) -> p j", j=EJ), value[:, :]).then_inc(placed, 16)
                    gp.wait_ge(placed, 48)


def plan_steps(nc, co, sdst, ssrc, sweight, we, be):
    co.tiles = co.sbuf("tiles", [1, STEPS + UNROLL], I32)
    co.local = co.sbuf("local", [P, 2, STEPS])
    co.edge_src = co.sbuf("edge_src", [P, 2, STEPS], U32)
    co.edge_term = co.sbuf("edge_term", [P, 2, STEPS])
    with phase(co, "plan") as ph:
        raw = [ph.sb(f"raw{i}", [HB, 2, EB], I32) for i in range(3)]
        val = [ph.sb(f"val{i}", [HB, 2, EB]) for i in range(2)]
        wev = ph.sb("wev", [P, 2])
        lim_i, lim = ph.sb("lim_i", [NT, 4], I32), ph.sb("lim", [NT, 9])
        meets = ph.sb("meets", [NT, STEPS])
        row = ph.sb("row", [1, 5, STEPS])
        tile_of, moved = ph.sb("tile_of", [1, STEPS], I32), ph.sb("moved", [1, STEPS], I32)
        number = ph.sb("number", [HB, 2])
        chosen = ph.sb("chosen", [HB, 2, STEPS])
        shift = ph.sb("shift", [P, 1, STEPS])
        psum, psum2, psum3, psum4 = (ph.ps(f"psum{i}", [P, 512]) for i in range(4))
        psb = [ph.ps(f"psb{i}", [P, 2, 256]) for i in range(3)]
        loaded, chain, mm, brought, conv = (ph.sem(n) for n in ("loaded", "chain", "mm", "brought", "conv"))
        with nc.Block() as block:
            @block.sync
            def _(sp):
                for i, a in enumerate((sdst, ssrc, sweight)):
                    a = a if i == 0 else a.bitcast(I32)
                    sp.dma_start(raw[i][:, :, :], a[0:NB * EB].rearrange("(h t e) -> t h e", h=2, e=EB)).then_inc(loaded, 16)
                sp.dma_start(wev[:, 0:1], we.to_broadcast([P, 1])).then_inc(loaded, 16)
                sp.dma_start(wev[:, 1:2], be.rearrange("(a b) -> a b", b=1).to_broadcast([P, 1])).then_inc(loaded, 16)

            @block.vector
            def _(dve):
                n = [0]

                def step(ins):
                    n[0] += 1
                    ins.then_inc(chain, 1)
                    dve.wait_ge(chain, n[0])

                c = lambda k: lim[:, k:k + 1]
                step(dve.tensor_copy(lim_i[:, 0:1], co.first[:, :]))
                step(dve.scalar_tensor_tensor(out=c(0), in0=co.first[:, :], scalar=-1.0, in1=co.count[:, :],
                                              op0=ALU.add, op1=ALU.add))
                step(dve.tensor_copy(lim_i[:, 1:2], c(0)))
                step(dve.tensor_scalar(lim_i[:, 2:4], lim_i[:, 0:2], 8, None, ALU.arith_shift_right))
                step(dve.tensor_copy(lim[:, 1:3], lim_i[:, 2:4]))
                step(dve.scalar_tensor_tensor(out=c(3), in0=c(2), scalar=1.0, in1=c(1), op0=ALU.add, op1=ALU.subtract))
                step(dve.tensor_scalar(c(4), co.count[:, :], 0.5, None, ALU.is_gt))
                step(dve.tensor_tensor(c(5), c(3), c(4), ALU.mult))
                dve.wait_ge(mm, 1)
                step(dve.tensor_copy(c(6), psum[0:NT, 0:1]))
                step(dve.tensor_tensor(c(7), c(6), c(5), ALU.add))
                step(dve.scalar_tensor_tensor(out=c(8), in0=c(1), scalar=-float(NB), in1=c(6), op0=ALU.add, op1=ALU.subtract))
                step(dve.tensor_scalar(meets[:, :], co.iota[0:NT, :], c(6), None, ALU.is_ge))
                step(dve.scalar_tensor_tensor(out=meets[:, :], in0=co.iota[0:NT, :], scalar=c(7), in1=meets[:, :],
                                              op0=ALU.is_lt, op1=ALU.mult))
                dve.wait_ge(mm, 2)
                step(dve.tensor_copy(row[:, 0, :], psum[0:1, 16:16 + STEPS]))
                step(dve.tensor_copy(row[:, 1, :], psum[0:1, 256:256 + STEPS]))
                step(dve.tensor_tensor(row[:, 2, :], co.iota[0:1, :], psum2[0:1, 0:STEPS], ALU.mult))
                step(dve.scalar_tensor_tensor(out=row[:, 3, :], in0=row[:, 1, :], scalar=float(NB), in1=row[:, 2, :],
                                              op0=ALU.add, op1=ALU.add))
                step(dve.tensor_scalar(row[:, 4, :], psum2[0:1, 0:STEPS], -NOWHERE, NOWHERE, ALU.mult, ALU.add))
                step(dve.scalar_tensor_tensor(out=row[:, 4, :], in0=row[:, 0, :], scalar=-float(P), in1=row[:, 4, :],
                                              op0=ALU.mult, op1=ALU.add))
                dve.tensor_scalar(number[:, 0:1], co.rowno[0:HB, :], 0.0, None, ALU.add)
                step(dve.tensor_scalar(number[:, 1:2], co.rowno[0:HB, :], float(HB), None, ALU.add))
                dve.wait_ge(mm, 3)
                dve.tensor_copy(shift[:, 0, :], psum3[:, 0:STEPS])
                for h in range(2):
                    last = dve.tensor_scalar(chosen[:, h, :], psum4[0:HB, 0:STEPS], number[:, h:h + 1], None, ALU.is_equal)
                step(last)
                dve.wait_ge(loaded, 80)
                for i in range(2):
                    dve.tensor_copy(val[i][:, :, :], raw[i][:, :, :]).then_inc(conv, 1)
                step(dve.tensor_copy(tile_of[:, :], row[:, 0, :]))
                pack(dve, step, co.tiles, tile_of, moved, STEPS, UNROLL)
                dve.wait_ge(brought, 1)
                dve.tensor_tensor(co.local[:, :, :], psb[0][:, :, 0:STEPS], shift[:, :, :].to_broadcast([P, 2, STEPS]), ALU.add)
                dve.wait_ge(brought, 2)
                dve.tensor_copy(co.edge_src[:, :, :], psb[1][:, :, 0:STEPS])

            @block.tensor
            def _(pe):
                pe.wait_ge(chain, 8)
                pe.matmul(psum[0:NT, 0:1], co.before[0:NT, 0:NT], lim[:, 5:6], start=True, stop=True).then_inc(mm, 1)
                pe.wait_ge(chain, 13)
                pe.matmul(psum[0:1, 16:16 + STEPS], co.rowno[0:NT, :], meets[:, :], start=True, stop=True)
                pe.matmul(psum[0:1, 256:256 + STEPS], lim[:, 8:9], meets[:, :], start=True, stop=True)
                pe.matmul(psum2[0:1, 0:STEPS], co.ones[0:NT, 0:1], meets[:, :], start=True, stop=True).then_inc(mm, 1)
                pe.wait_ge(chain, 19)
                pe.matmul(psum3[:, 0:STEPS], co.ones[0:1, :], row[:, 4, :], start=True, stop=True)
                pe.matmul(psum4[:, 0:STEPS], co.ones[0:1, :], row[:, 3, :], start=True, stop=True).then_inc(mm, 1)
                pe.wait_ge(conv, 2)
                pe.wait_ge(chain, 21)
                for i in range(3):
                    for j in range(2):
                        for h in range(2):
                            a = val[i][:, h, :] if i < 2 else raw[i][:, h, :].bitcast(F32)
                            last = pe.matmul(psb[i][:, j, 0:STEPS], a[:, j * P:(j + 1) * P], chosen[:, h, :],
                                             start=(h == 0), stop=(h == 1))
                    last.then_inc(brought, 1)

            @block.scalar
            def _(act):
                act.preload_act_table(ACT.Exp)
                act.wait_ge(brought, 3)
                act.activation(co.edge_term[:, :, :], psb[2][:, :, 0:STEPS], ACT.Identity, bias=wev[:, 1:2], scale=wev[:, 0:1])


def load_x(nc, co, x):
    co.x = co.sbuf("x", [P, NT, D])
    with phase(co, "loadx") as ph:
        cleared, loaded = ph.sem("cleared"), ph.sem("loaded")
        with nc.Block() as block:
            @block.vector
            def _(dve):
                dve.memset(co.x[:, NT - 1, :], 0.0).then_inc(cleared, 1)

            @block.sync
            def _(sp):
                sp.dma_start(co.x[:, 0:NT - 1, :], x[0:(NT - 1) * P, :].rearrange("(t p) d -> p t d", p=P)).then_inc(loaded, 16)
                sp.wait_ge(cleared, 1)
                sp.dma_start(co.x[0:LAST, NT - 1, :], x[(NT - 1) * P:N, :]).then_inc(loaded, 16)
                sp.wait_ge(loaded, 32)


def layer_norm(nc, co, name, src, dst):
    with phase(co, name) as ph:
        stats = ph.sb("stats", [P, NT, 6])
        mv = ph.sb("mv", [P, NT, 2])
        var = ph.sb("var", [P, NT])
        std = ph.sb("std", [P, NT])
        rstd = ph.sb("rstd", [P, NT])
        shift = ph.sb("shift", [P, NT])
        stat, agg, eps, root, inv, neg = (ph.sem(n) for n in ("stat", "agg", "eps", "root", "inv", "neg"))
        C = 5
        half = 15
        with nc.Block() as block:
            @block.vector
            def _(dve):
                with dve.Fori(0, NT // C) as q:
                    for c in range(C):
                        dve.bn_stats(stats[:, bass.ds(C * q + c, 1), :], src[:, bass.ds(C * q + c, 1), :]).then_inc(stat, 1)
                dve.wait_ge(stat, NT)
                for t in range(NT):
                    dve.bn_aggr(mv[:, t, :], stats[:, t, :]).then_inc(agg, 1)
                dve.wait_ge(agg, NT)
                dve.tensor_scalar(var[:, :], mv[:, :, 1], EPS, None, ALU.add).then_inc(eps, 1)
                dve.wait_ge(root, 1)
                dve.reciprocal(rstd[:, :], std[:, :]).then_inc(inv, 1)
                dve.wait_ge(inv, 1)
                dve.scalar_tensor_tensor(out=shift[:, :], in0=mv[:, :, 0], scalar=-1.0, in1=rstd[:, :],
                                         op0=ALU.mult, op1=ALU.mult).then_inc(neg, 1)
                dve.wait_ge(neg, 1)
                with dve.Fori(0, half // C) as q:
                    for c in range(C):
                        t = bass.ds(C * q + c, 1)
                        dve.tensor_scalar(dst[:, t, :], src[:, t, :], rstd[:, t], shift[:, t], ALU.mult, ALU.add)

            @block.scalar
            def _(act):
                act.preload_act_table(ACT.Sqrt)
                act.wait_ge(eps, 1)
                act.activation(std[:, :], var[:, :], ACT.Sqrt).then_inc(root, 1)
                act.wait_ge(neg, 1)
                with act.Fori(half // C, NT // C) as q:
                    for c in range(C):
                        t = bass.ds(C * q + c, 1)
                        act.activation(dst[:, t, :], src[:, t, :], ACT.Identity, bias=shift[:, t], scale=rstd[:, t])


def at_least(eng, sem, value):
    if not isinstance(value, int) or value > 0:
        eng.wait_ge(sem, value)


def over_tiles(eng, n, stages, words=None):
    most = max(lag for lag, _ in stages)
    lead = -(-(most + 2) // ROUNDS)

    def round_(q, c, static):
        r = ROUNDS * q + c
        if words is not None and c == 0:
            word[0] = eng.value_load(words[0:1, bass.ds(r + ROUNDS - 2, 1)])
        for lag, body in stages:
            if not static or 0 <= r - lag < n:
                body(r - lag, (c - lag) % 2, *([] if words is None else [number_in(word[0], c - lag + 2, EXP)]))

    word = [None]

    turns = max(lead, n // ROUNDS)
    for r in range(min(ROUNDS * lead, n + most)):
        round_(r // ROUNDS, r % ROUNDS, True)
    if lead < turns:
        with eng.Fori(lead, turns) as q:
            for c in range(ROUNDS):
                round_(q, c, False)
    for r in range(ROUNDS * turns, n + most):
        round_(r // ROUNDS, r % ROUNDS, True)


def split3(dve, parts, t, rest, whole, sem, count):
    part = lambda i: parts[:, bass.ds(t, 1), i, :]
    dve.tensor_tensor(rest, whole, part(0), ALU.subtract).then_inc(sem, 1)
    dve.wait_ge(sem, count + 1)
    dve.tensor_scalar(part(1), rest, 1.0, None, ALU.mult).then_inc(sem, 1)
    dve.wait_ge(sem, count + 2)
    dve.tensor_tensor(part(2), rest, part(1), ALU.subtract).then_inc(sem, 1)


def attention_inputs(nc, co, xn, a, q_parts, base, table, acc, top):
    with phase(co, "attin") as ph:
        wq, wk, ws = ph.sb("wq", [P, KD, D]), ph.sb("wk", [P, KD, D + 1]), ph.sb("ws", [P, KD, D])
        bq, bs = ph.sb("bq", [P, KD]), ph.sb("bs", [P, 1, D])
        cur, xt, qt = ([ph.sb(f"{n}{u}", shape) for u in range(2)] for n, shape in (
            ("cur", [P, D]), ("xt", [P, KD, P]), ("qt", [P, KD, P])))
        qf, rest = ph.sb("qf", [P, 1, D + 1]), ph.sb("rest", [P, 1, D + 1])
        ps_x, ps_q, ps_k, ps_s = ([ph.ps(f"{n}{u}", [P, 512]) for u in range(2)] for n in ("ps_x", "ps_q", "ps_k", "ps_s"))
        loaded, tabled, biased, staged = (ph.sem(n) for n in ("loaded", "tabled", "biased", "staged"))
        x_turned, x_out, q_made, q_out, k_made, k_out, s_made, s_out, split = (ph.sem(n) for n in (
            "x_turned", "x_out", "q_made", "q_out", "k_made", "k_out", "s_made", "s_out", "split"))
        seen = ph.sem("seen")
        with nc.Block() as block:
            @block.sync
            def _(sp):
                for there, w in ((wq[:, :, :], "L0_gnn_wq"), (wk[:, :, 0:D], "L0_gnn_wk"), (ws[:, :, :], "L0_gnn_ws")):
                    sp.dma_start(there, a[w].rearrange("(k p) d -> p k d", p=P)).then_inc(loaded, 16)
                with nc.allow_non_contiguous_dma(reason="a bias with its features on partitions"):
                    sp.dma_start(bq[:, :], a["L0_gnn_bq"].rearrange("(k p) -> p k", p=P)).then_inc(loaded, 16)
                    sp.dma_start(wk[:, :, D:D + 1], a["L0_gnn_bk"].rearrange("(k p a) -> p k a", p=P, a=1)).then_inc(loaded, 16)
                sp.dma_start(bs[:, 0, :], a["L0_gnn_bs"].rearrange("(a d) -> a d", a=1).to_broadcast([P, D])).then_inc(loaded, 16)
                sp.dma_start(table.rearrange("(t p) d -> p t d", p=P), xn[:, :, :]).then_inc(tabled, 16)
                sp.wait_ge(tabled, 16)

            @block.gpsimd
            def _(gp):
                gp.wait_ge(loaded, 96)

                def stage(t, u):
                    gp.tensor_tensor(base[:, bass.ds(t, 1), :], xn[:, bass.ds(t, 1), :], bs[:, :, :], ALU.add).then_inc(biased, 1)
                    at_least(gp, x_turned, t - 1)
                    gp.sem_inc(seen, 1)
                    gp.tensor_copy(cur[u][:, :].unsqueeze(1), xn[:, bass.ds(t, 1), :]).then_inc(staged, 1)

                over_tiles(gp, NT, [(0, stage)])

            @block.tensor
            def _(pe):
                pe.wait_ge(loaded, 96)

                def turn(t, u):
                    pe.wait_ge(staged, t + 1)
                    at_least(pe, x_out, t - 1)
                    for k in range(KD):
                        last = pe.transpose(ps_x[u][:, k * P:(k + 1) * P], cur[u][:, k * P:(k + 1) * P], co.ident[:, :])
                    last.then_inc(x_turned, 1)

                def project(t, u):
                    pe.wait_ge(x_out, t + 1)
                    at_least(pe, q_out, t - 1)
                    for m in range(KD):
                        for k in range(KD):
                            last = pe.matmul(ps_q[u][:, m * P:(m + 1) * P], wq[:, k, m * P:(m + 1) * P], xt[u][:, k, :],
                                             start=(k == 0), stop=(k == KD - 1))
                    last.then_inc(q_made, 1)
                    at_least(pe, s_out, t - 1)
                    for k in range(KD):
                        last = pe.matmul(ps_s[u][:, 0:D], xt[u][:, k, :], ws[:, k, :], start=(k == 0), stop=(k == KD - 1))
                    last.then_inc(s_made, 1)

                def keys(t, u):
                    pe.wait_ge(q_out, t + 1)
                    at_least(pe, k_out, t - 1)
                    for k in range(KD):
                        last = pe.matmul(ps_k[u][:, 0:D + 1], qt[u][:, k, :], wk[:, k, :], start=(k == 0), stop=(k == KD - 1))
                    last.then_inc(k_made, 1)

                over_tiles(pe, NT, [(0, turn), (1, project), (2, keys)])

            @block.scalar
            def _(act):
                act.preload_act_table(ACT.Exp)

                def turned(t, u):
                    act.wait_ge(x_turned, t + 1)
                    at_least(act, s_made, t - 1)
                    act.copy(xt[u][:, :, :], ps_x[u][:, 0:D].rearrange("p (k c) -> p k c", k=KD)).then_inc(x_out, 1)

                def scaled(t, u):
                    act.wait_ge(k_made, t + 1)
                    at_least(act, split, 3 * t)
                    act.mul(qf[:, 0, :], ps_k[u][:, 0:D + 1], D ** -0.5)
                    act.mul(q_parts[:, bass.ds(t, 1), 0, :], ps_k[u][:, 0:D + 1].unsqueeze(1), D ** -0.5).then_inc(k_out, 1)

                over_tiles(act, NT, [(0, turned), (2, scaled)])

            @block.vector
            def _(dve):
                dve.memset(acc[:, :, :], 0.0)
                dve.memset(top[:, :, :], -BIG)
                dve.wait_ge(loaded, 96)

                def biases(t, u):
                    dve.wait_ge(q_made, t + 1)
                    at_least(dve, k_made, t - 1)
                    for m in range(KD):
                        last = dve.tensor_scalar(qt[u][:, m, :], ps_q[u][:, m * P:(m + 1) * P], bq[:, m:m + 1], None, ALU.add)
                    last.then_inc(q_out, 1)
                    dve.wait_ge(s_made, t + 1)
                    dve.wait_ge(biased, t + 1)
                    dve.tensor_tensor(base[:, bass.ds(t, 1), :], ps_s[u][:, 0:D].unsqueeze(1), base[:, bass.ds(t, 1), :], ALU.add)\
                       .then_inc(s_out, 1)

                def parts(t, u):
                    dve.wait_ge(k_out, t + 1)
                    split3(dve, q_parts, t, rest[:, :, :], qf[:, :, :], split, 3 * t)

                over_tiles(dve, NT, [(1, biases), (3, parts)])


def over_steps(eng, n, tiles, stages):
    most = max(lag for lag, *_ in stages)
    turns = n // UNROLL
    assert n % UNROLL == 0 and most <= UNROLL

    def turn(q, steps, static):
        words = {first: eng.value_load(tiles[0:1, bass.ds(UNROLL * q + first + UNROLL, 1)])
                 for first in sorted({first for _, _, first in stages if first is not None})}
        for r in steps:
            for lag, body, first in stages:
                if not static or 0 <= UNROLL * q + r - lag < n:
                    body(q + (r - lag) // UNROLL, (r - lag) % UNROLL,
                         None if first is None else number_in(words[first], r - lag - first, NT))

    turn(0, range(UNROLL), True)
    turn(1, range(UNROLL), True)
    with eng.Fori(2, turns) as q:
        turn(q, range(UNROLL), False)
    turn(turns, range(most), True)


def edge_pass(nc, co, name, table, acc, top, heads, q_parts=None, r_parts=None, att=None):
    gat = att is not None
    row_width = table.shape[1]
    ch = D // heads
    one = row_width if heads == 1 else None
    sum_width = row_width + 1 if heads == 1 else heads * (ch + 1)
    room = max(sum_width, row_width)
    with phase(co, name) as ph:
        rows = [ph.sb(f"rows{k}", [P, 2, room]) for k in range(UNROLL)]
        index = [ph.sb(f"index{k}", [P, 2], U32) for k in range(UNROLL)]
        inside = [ph.sb(f"inside{k}", [P, 2, P]) for k in range(UNROLL)]
        outside = [ph.sb(f"outside{k}", [P, 2, P], BF16) for k in range(UNROLL)]
        turned = [ph.sb(f"turned{k}", [P, 2, P], BF16) for k in range(UNROLL)]
        score = [ph.sb(f"score{k}", [P, 2, heads]) for k in range(UNROLL)]
        rough = [ph.sb(f"rough{k}", [P, 2, heads], BF16) for k in range(UNROLL)]
        old, gmax = ph.sb("old", [P, heads]), ph.sb("gmax", [P, heads])
        peak = [ph.sb(f"peak{k}", [P, heads + 1], BF16) for k in range(UNROLL)]
        fall = [ph.sb(f"fall{k}", [P, heads]) for k in range(UNROLL)]
        keep = [ph.sb(f"keep{k}", [P, heads]) for k in range(UNROLL)]
        gap = ph.sb("gap", [P, 2, heads])
        exponent = [ph.sb(f"exponent{k}", [P, 2, heads]) for k in range(UNROLL)]
        weight = [ph.sb(f"weight{k}", [P, 2, heads]) for k in range(UNROLL)]
        if heads == 1:
            weighted = [ph.sb(f"weighted{k}", [P, 2, P]) for k in range(UNROLL)]
        else:
            scaled = [ph.sb(f"scaled{k}", [P, 2, heads, ch + 1]) for k in range(UNROLL)]
        if gat:
            size = [ph.sb(f"size{k}", [P, KD, 2 * P]) for k in range(UNROLL)]
            ps_mixed = ph.ps("ps_mixed", [P, KD, 2 * P])
            ps_logits = ph.ps("ps_logits", [P, 512])
        else:
            dots, constant = ph.sb("dots", [P, 2, 1]), ph.sb("constant", [P, 2, 1])
            junk = ph.sb("junk", [P, 2, D])
            ps_query = ph.ps("ps_query", [P, 2, 512])
        ps_turned = ph.ps("ps_turned", [P, 1024], BF16)
        ps_masked = ph.ps("ps_masked", [P, 1 if heads == 1 else 2, 512])
        ps_tops = ph.ps("ps_tops", [P, 512])
        ps_sums = ph.ps("ps_sums", [P, 512])
        masked_view = (lambda: ps_masked[:, 0, 0:2 * P].rearrange("p (j h e) -> p j h e", j=2, h=1)) if heads == 1 else \
                (lambda: ps_masked[:, :, :].rearrange("p j (h e) -> p j h e", h=heads))
        tops_view = lambda: ps_tops[:, 0:2 * (heads + 1)].rearrange("p (j h) -> p j h", j=2)
        got = [ph.gp_dma_sem(k) for k in range(UNROLL)]
        indexed, seen, primed = ph.sem("indexed"), ph.sem("seen"), ph.sem("primed")
        dotted, maxed, peaked, fell, gapped, summed = (ph.sem(n) for n in (
            "dotted", "maxed", "peaked", "fell", "gapped", "summed"))
        members, turned_made, turned_ready, expanded, sized, logits_made, scored, masked_made = (ph.sem(n) for n in (
            "members", "turned_made", "turned_ready", "expanded", "sized", "logits_made", "scored", "masked_made"))
        kept, tops_made, exponents_ready, weighed, scaled_by_vector, scaled_by_scalar, sums_made = (ph.sem(n) for n in (
            "kept", "tops_made", "exponents_ready", "weighed", "scaled_by_vector", "scaled_by_scalar", "sums_made"))
        constants = UNROLL * (2 if heads == 1 else 1)
        num = lambda q, k: UNROLL * q + k

        with nc.Block() as block:
            @block.gpsimd
            def _(gp):
                gp.wait_ge(primed, constants)

                def gather(q, k, _):
                    g = num(q, k)
                    at_least(gp, sums_made, g - (UNROLL - 1))
                    gp.sem_inc(seen, 1)
                    gp.tensor_copy(index[k][:, :].unsqueeze(2), co.edge_src[:, :, bass.ds(g, 1)]).then_inc(indexed, 1)
                    gp.wait_ge(indexed, g + 1)
                    gp.sem_inc(seen, 1)
                    for j in range(2):
                        gp.indirect_dma_start(rows[k][:, j, 0:row_width], None, table,
                                              bass.IndirectOffsetOnAxis(ap=index[k][:, j:j + 1], axis=0)).then_inc(got[k], 16)

                over_steps(gp, STEPS, co.tiles, [(0, gather, None)])

            @block.vector
            def _(dve):
                for k in range(UNROLL):
                    if heads == 1:
                        dve.memset(rows[k][:, :, one:one + 1], 1.0).then_inc(primed, 1)
                    dve.memset(peak[k][:, heads:heads + 1], BIG).then_inc(primed, 1)
                dve.wait_ge(primed, constants)

                def outsider(j):
                    def body(q, k, _):
                        dve.tensor_scalar(outside[k][:, j, :], co.iotab[:, :], co.local[:, j, bass.ds(num(q, k), 1)], -1.0,
                                          ALU.is_equal, ALU.add)
                    return body

                def member(j):
                    def body(q, k, _):
                        g = num(q, k)
                        last = dve.tensor_scalar(inside[k][:, j, :], co.iota[:, 0:P], co.local[:, j, bass.ds(g, 1)], None, ALU.is_equal)
                        if j == 1:
                            last.then_inc(members, 1)
                    return body

                def dot_products(q, k, _):
                    g = num(q, k)
                    dve.wait_ge(expanded, g + 1)
                    dve.tensor_tensor(constant[:, :, :], co.edge_term[:, :, bass.ds(g, 1)], ps_query[:, :, D:D + 1], ALU.add)
                    for j in range(2):
                        last = dve.tensor_tensor_reduce(junk[:, j, :], rows[k][:, j, 0:D], ps_query[:, j, 0:D], 1.0, 0.0, ALU.mult,
                                                        ALU.add, dots[:, j, :])
                    last.then_inc(dotted, 1)

                def scores(q, k, _):
                    g = num(q, k)
                    if gat:
                        dve.wait_ge(logits_made, g + 1)
                        parts = ps_logits[:, 0:2 * heads].rearrange("p (j h) -> p j h", j=2), rows[k][:, :, D:D + heads]
                    else:
                        dve.wait_ge(dotted, g + 1)
                        parts = dots[:, :, :], constant[:, :, :]
                    dve.tensor_tensor(score[k][:, :, :], *parts, ALU.add)
                    dve.tensor_tensor(rough[k][:, :, :], *parts, ALU.add).then_inc(scored, 1)

                def old_tops(q, k, tile):
                    dve.tensor_copy(old[:, :].unsqueeze(1), top[:, bass.ds(tile, 1), :])

                def maxima(q, k, _):
                    g = num(q, k)
                    dve.wait_ge(masked_made, g + 1)
                    dve.tensor_reduce(gmax[:, :], masked_view().rearrange("p j h e -> p h j e"), AX.XY, ALU.max).then_inc(maxed, 1)

                def peaks(q, k, _):
                    g = num(q, k)
                    dve.wait_ge(maxed, g + 1)
                    dve.tensor_tensor(peak[k][:, 0:heads], old[:, :], gmax[:, :], ALU.max).then_inc(peaked, 1)

                def new_tops(q, k, tile):
                    g = num(q, k)
                    dve.wait_ge(peaked, g + 1)
                    dve.tensor_tensor(fall[k][:, :], old[:, :], peak[k][:, 0:heads], ALU.subtract).then_inc(fell, 1)
                    dve.tensor_scalar(top[:, bass.ds(tile, 1), :], peak[k][:, 0:heads].unsqueeze(1), 1.0, None, ALU.mult)

                def differences(q, k, _):
                    g = num(q, k)
                    dve.wait_ge(tops_made, g + 1)
                    dve.tensor_tensor(gap[:, :, :], score[k][:, :, :], tops_view()[:, :, 0:heads], ALU.subtract).then_inc(gapped, 1)

                def arguments(q, k, _):
                    g = num(q, k)
                    dve.wait_ge(gapped, g + 1)
                    dve.scalar_tensor_tensor(out=exponent[k][:, :, :], in0=tops_view()[:, :, heads:heads + 1].to_broadcast([P, 2, heads]),
                                             scalar=-BIG, in1=gap[:, :, :], op0=ALU.add, op1=ALU.add).then_inc(exponents_ready, 1)

                def weights(q, k, _):
                    dve.wait_ge(weighed, num(q, k) + 1)
                    dve.tensor_tensor(scaled[k][:, 0, :, 0:ch], rows[k][:, 0, 0:D].rearrange("p (h c) -> p h c", h=heads),
                                      weight[k][:, 0, :].unsqueeze(2).to_broadcast([P, heads, ch]), ALU.mult)
                    dve.tensor_copy(scaled[k][:, :, :, ch], weight[k][:, :, :]).then_inc(scaled_by_vector, 1)

                def sums(q, k, tile):
                    g = num(q, k)
                    dve.wait_ge(sums_made, g + 1)
                    w = sum_width // heads
                    for h in range(heads):
                        mine = acc[:, bass.ds(tile, 1), h * w:(h + 1) * w]
                        last = dve.scalar_tensor_tensor(out=mine, in0=mine, scalar=keep[k][:, h:h + 1],
                                                        in1=ps_sums[:, h * w:(h + 1) * w].unsqueeze(1), op0=ALU.mult, op1=ALU.add)
                    last.then_inc(summed, 1)

                ends = [(3, maxima, None), (0, member(0), None), (3, peaks, None), (0, member(1), None), (3, new_tops, -3)]
                if gat and heads > 1:
                    over_steps(dve, STEPS, co.tiles,
                               [(3, scores, None), (4, differences, None), (0, outsider(0), None), (4, arguments, None),
                                (5, sums, -5), (3, old_tops, -3), (0, outsider(1), None), (4, weights, None)] + ends)
                elif gat:
                    over_steps(dve, STEPS, co.tiles,
                               [(4, differences, None), (0, outsider(0), None), (4, arguments, None), (3, scores, None),
                                (5, sums, -5), (3, old_tops, -3), (0, outsider(1), None)] + ends)
                else:
                    over_steps(dve, STEPS, co.tiles,
                               [(3, dot_products, None), (4, differences, None), (3, scores, None), (4, arguments, None),
                                (0, outsider(0), None), (5, sums, -5), (3, old_tops, -3), (0, outsider(1), None)] + ends)

            @block.scalar
            def _(act):
                act.preload_act_table(ACT.Exp)

                def turn(q, k, _):
                    g = num(q, k)
                    act.wait_ge(turned_made, g + 1)
                    act.activation(turned[k][:, :, :], ps_turned[:, 0:2 * P].rearrange("p (j e) -> p j e", j=2), ACT.Identity,
                                   bias=co.ones[:, 0:1]).then_inc(turned_ready, 1)

                def magnitudes(q, k, _):
                    g = num(q, k)
                    act.wait_ge(expanded, g + 1)
                    act.activation(size[k][:, :, :], ps_mixed[:, :, :], ACT.Abs).then_inc(sized, 1)

                def keeps(q, k, _):
                    g = num(q, k)
                    act.wait_ge(fell, g + 1)
                    act.activation(keep[k][:, :], fall[k][:, :], ACT.Exp).then_inc(kept, 1)

                def exps(q, k, _):
                    g = num(q, k)
                    act.wait_ge(exponents_ready, g + 1)
                    act.activation(weight[k][:, :, :], exponent[k][:, :, :], ACT.Exp).then_inc(weighed, 1)

                def weights(q, k, _):
                    act.wait_ge(weighed, num(q, k) + 1)
                    if heads == 1:
                        for j in range(2):
                            last = act.activation(weighted[k][:, j, :], inside[k][:, j, :], ACT.Copy, scale=weight[k][:, j, :])
                    else:
                        for h in range(heads):
                            last = act.activation(scaled[k][:, 1, h, 0:ch], rows[k][:, 1, h * ch:(h + 1) * ch],
                                                  ACT.Copy, scale=weight[k][:, 1, h:h + 1])
                    last.then_inc(scaled_by_scalar, 1)

                of_dst = [(2, magnitudes, None)] if gat else []
                spreading = [(4, weights, None)]
                over_steps(act, STEPS, co.tiles, [(4, exps, None)] + (spreading + of_dst if heads == 1 else of_dst + spreading) +
                           [(1, turn, None), (3, keeps, None)])

            @block.tensor
            def _(pe):
                pe.wait_ge(primed, constants)

                def turns(q, k, tile):
                    g = num(q, k)
                    pe.wait_ge(members, g + 1)
                    for j in range(2):
                        last = pe.transpose(ps_turned[:, j * P:(j + 1) * P], outside[k][:, j, :], co.identb[:, :])
                    last.then_inc(turned_made, 1)

                def expand(q, k, tile):
                    g = num(q, k)
                    if not gat:
                        pe.wait_ge(turned_ready, g + 1)
                        pe.wait_ge(got[k], 32 * q + 32)
                        for j in range(2):
                            for i in range(3):
                                last = pe.matmul(ps_query[:, j, 0:D + 1], turned[k][:, j, :], q_parts[:, bass.ds(tile, 1), i, :],
                                                 start=(i == 0), stop=(i == 2))
                        last.then_inc(expanded, 1)
                        return
                    pe.wait_ge(turned_ready, g + 1)
                    pe.wait_ge(got[k], 32 * q + 32)
                    at_least(pe, sized, g)
                    for c in range(KD):
                        for j in range(2):
                            pe.matmul(ps_mixed[:, c, j * P:(j + 1) * P], rows[k][:, j, c * P:(c + 1) * P], co.ident[:, :],
                                      is_transpose=True, start=(c == 0 and j == 0), stop=False, skip_group_check=True)
                        for i in range(3):
                            last = pe.matmul(ps_mixed[:, c, :], r_parts[:, bass.ds(tile, 1), i, c * P:(c + 1) * P],
                                             turned[k][:, :, :], start=False, stop=(c == KD - 1 and i == 2),
                                             skip_group_check=True)
                    last.then_inc(expanded, 1)

                def logits(q, k, tile):
                    g = num(q, k)
                    pe.wait_ge(sized, g + 1)
                    for j in range(2):
                        for c in range(KD):
                            pe.matmul(ps_logits[:, j * heads:(j + 1) * heads], size[k][:, c, j * P:(j + 1) * P],
                                      att[:, c, :], start=(c == 0), stop=False)
                        for i in range(3):
                            last = pe.matmul(ps_logits[:, j * heads:(j + 1) * heads], turned[k][:, j, :],
                                             r_parts[:, bass.ds(tile, 1), i, D:D + heads], start=False, stop=(i == 2))
                    last.then_inc(logits_made, 1)

                def spread_scores(q, k, tile):
                    g = num(q, k)
                    pe.wait_ge(scored, g + 1)
                    for j in range(2):
                        where = ps_masked[:, 0, j * P:(j + 1) * P] if heads == 1 else ps_masked[:, j, :]
                        pe.matmul(where, outside[k][:, j, :], co.bigident[:, :] if heads == 1 else
                                  co.bigident[:, :].unsqueeze(1).to_broadcast([P, heads, P]), start=(heads > 1 or j == 0),
                                  stop=False, skip_group_check=True)
                        for h in range(heads):
                            last = pe.matmul(where[:, h * P:(h + 1) * P], rough[k][:, j, h:h + 1].to_broadcast([P, P]),
                                             co.identb[:, :], start=False, stop=(h == heads - 1), skip_group_check=True)
                    last.then_inc(masked_made, 1)

                def tops_of(q, k, tile):
                    g = num(q, k)
                    pe.wait_ge(peaked, g + 1)
                    w = heads + 1
                    for j in range(2):
                        last = pe.matmul(ps_tops[:, j * w:(j + 1) * w], turned[k][:, j, :], peak[k][:, :], start=True, stop=True)
                    last.then_inc(tops_made, 1)

                def add_up(q, k, tile):
                    g = num(q, k)
                    pe.wait_ge(scaled_by_scalar, g + 1)
                    if heads > 1:
                        pe.wait_ge(scaled_by_vector, g + 1)
                    else:
                        at_least(pe, summed, g)
                    for j in range(2):
                        if heads == 1:
                            last = pe.matmul(ps_sums[:, 0:sum_width], weighted[k][:, j, :], rows[k][:, j, 0:sum_width], start=(j == 0), stop=(j == 1))
                        else:
                            last = pe.matmul(ps_sums[:, 0:sum_width], inside[k][:, j, :], scaled[k][:, j, :, :].rearrange("p h c -> p (h c)"),
                                             start=(j == 0), stop=(j == 1))
                    last.then_inc(sums_made, 1)

                if gat:
                    over_steps(pe, STEPS, co.tiles, [(2, expand, -2), (3, spread_scores, None), (1, turns, None)] +
                               ([(4, add_up, None), (2, logits, -2)] if heads == 1 else [(2, logits, -2), (4, add_up, None)]) +
                               [(3, tops_of, None)])
                else:
                    over_steps(pe, STEPS, co.tiles, [(3, spread_scores, None), (2, expand, -2), (3, tops_of, None),
                                                     (4, add_up, None), (1, turns, None)])


def row_on_all(ap, n):
    return ap.rearrange("(a n) -> a n", a=1).to_broadcast([P, n])


def attention_output(nc, co, acc, base, a):
    with phase(co, "attout") as ph:
        wv = ph.sb("wv", [P, KD, D])
        bv = ph.sb("bv", [P, 1, D])
        most, inv, share = ph.sb("most", [P, NT]), ph.sb("inv", [P, NT]), ph.sb("share", [P, NT])
        cur, xt, biased = ([ph.sb(f"{n}{u}", shape) for u in range(2)] for n, shape in (
            ("cur", [P, 1, D]), ("xt", [P, KD, P]), ("biased", [P, 1, D])))
        ps_x, ps_v = ([ph.ps(f"{n}{u}", [P, 512]) for u in range(2)] for n in ("ps_x", "ps_v"))
        loaded, chain, staged, turned, out, made, mixed, used = (ph.sem(n) for n in (
            "loaded", "chain", "staged", "turned", "out", "made", "mixed", "used"))
        with nc.Block() as block:
            @block.sync
            def _(sp):
                sp.dma_start(wv[:, :, :], a["L0_gnn_wv"].rearrange("(k p) d -> p k d", p=P)).then_inc(loaded, 16)
                sp.dma_start(bv[:, 0, :], row_on_all(a["L0_gnn_bv"], D)).then_inc(loaded, 16)

            @block.scalar
            def _(act):
                act.preload_act_table(ACT.Exp)
                act.wait_ge(chain, 3)

                def stage(t, u):
                    at_least(act, turned, t - 1)
                    act.activation(cur[u][:, :, :], acc[:, bass.ds(t, 1), 0:D], ACT.Copy, scale=inv[:, bass.ds(t, 1)]).then_inc(staged, 1)

                def evacuate(t, u):
                    act.wait_ge(turned, t + 1)
                    at_least(act, made, t - 1)
                    act.copy(xt[u][:, :, :], ps_x[u][:, 0:D].rearrange("p (k c) -> p k c", k=KD)).then_inc(out, 1)

                over_tiles(act, NT, [(1, evacuate), (0, stage)])

            @block.tensor
            def _(pe):
                pe.wait_ge(loaded, 32)

                def turn(t, u):
                    pe.wait_ge(staged, t + 1)
                    at_least(pe, out, t - 1)
                    for k in range(KD):
                        last = pe.transpose(ps_x[u][:, k * P:(k + 1) * P], cur[u][:, 0, k * P:(k + 1) * P], co.ident[:, :])
                    last.then_inc(turned, 1)

                def project(t, u):
                    pe.wait_ge(out, t + 1)
                    at_least(pe, mixed, t - 1)
                    for k in range(KD):
                        last = pe.matmul(ps_v[u][:, 0:D], xt[u][:, k, :], wv[:, k, :], start=(k == 0), stop=(k == KD - 1))
                    last.then_inc(made, 1)

                over_tiles(pe, NT, [(0, turn), (1, project)])

            @block.vector
            def _(dve):
                dve.tensor_scalar(most[:, :], acc[:, :, D], 1e-12, None, ALU.max).then_inc(chain, 1)
                dve.wait_ge(chain, 1)
                dve.reciprocal(inv[:, :], most[:, :]).then_inc(chain, 1)
                dve.wait_ge(chain, 2)
                dve.tensor_tensor(share[:, :], acc[:, :, D], inv[:, :], ALU.mult).then_inc(chain, 1)
                dve.wait_ge(chain, 3)
                dve.wait_ge(loaded, 32)

                def mix(t, u):
                    dve.wait_ge(made, t + 1)
                    at_least(dve, used, t - 1)
                    dve.scalar_tensor_tensor(out=biased[u][:, :, :], in0=bv[:, :, :], scalar=share[:, bass.ds(t, 1)],
                                             in1=ps_v[u][:, 0:D].unsqueeze(1), op0=ALU.mult, op1=ALU.add).then_inc(mixed, 1)
                    dve.wait_ge(mixed, t + 1)
                    dve.tensor_tensor(base[:, bass.ds(t, 1), :], biased[u][:, :, :], base[:, bass.ds(t, 1), :], ALU.add).then_inc(used, 1)

                over_tiles(dve, NT, [(1, mix)])


def attention_ffn(nc, co, y, base, a):
    K2 = 2 * KD
    with phase(co, "attffn") as ph:
        w1, w2 = ph.sb("w1", [P, KD, 2 * D]), ph.sb("w2", [P, K2, D])
        b1 = ph.sb("b1", [P, K2])
        g, b, b2, both = (ph.sb(n, [P, 1, D]) for n in ("g", "b", "b2", "both"))
        cur, xt, ht = ([ph.sb(f"{n}{u}", shape) for u in range(2)] for n, shape in (
            ("cur", [P, 1, D]), ("xt", [P, KD, P]), ("ht", [P, K2, P])))
        ps_x, ps_h, ps_f = ([ph.ps(f"{n}{u}", shape) for u in range(2)] for n, shape in (
            ("ps_x", [P, 512]), ("ps_h", [P, K2, P]), ("ps_f", [P, 512])))
        loaded, added, scaled, staged, rested, turned, out, made, bent, mixed, done, seen = (ph.sem(n) for n in (
            "loaded", "added", "scaled", "staged", "rested", "turned", "out", "made", "bent", "mixed", "done", "seen"))
        with nc.Block() as block:
            @block.sync
            def _(sp):
                sp.dma_start(w1[:, :, :], a["L0_gnn_w_ff1"].rearrange("(k p) d -> p k d", p=P)).then_inc(loaded, 16)
                sp.dma_start(w2[:, :, :], a["L0_gnn_w_ff2"].rearrange("(k p) d -> p k d", p=P)).then_inc(loaded, 16)
                with nc.allow_non_contiguous_dma(reason="a bias with its features on partitions"):
                    sp.dma_start(b1[:, :], a["L0_gnn_b_ff1"].rearrange("(k p) -> p k", p=P)).then_inc(loaded, 16)
                for there, v in ((g, "L0_gnn_g1"), (b, "L0_gnn_b1"), (b2, "L0_gnn_b_ff2")):
                    sp.dma_start(there[:, 0, :], row_on_all(a[v], D)).then_inc(loaded, 16)

            @block.gpsimd
            def _(gp):
                gp.wait_ge(loaded, 96)
                gp.tensor_tensor(both[:, :, :], b[:, :, :], b2[:, :, :], ALU.add).then_inc(added, 1)
                gp.wait_ge(added, 1)

                def stage(t, u):
                    at = y[:, bass.ds(t, 1), :]
                    gp.tensor_tensor(at, at, g[:, :, :], ALU.mult).then_inc(scaled, 1)
                    gp.wait_ge(scaled, t + 1)
                    at_least(gp, turned, t - 1)
                    gp.sem_inc(seen, 1)
                    gp.tensor_tensor(cur[u][:, :, :], at, b[:, :, :], ALU.add).then_inc(staged, 1)
                    gp.wait_ge(staged, t + 1)
                    gp.sem_inc(seen, 1)
                    gp.tensor_tensor(at, at, both[:, :, :], ALU.add).then_inc(rested, 1)

                over_tiles(gp, NT, [(0, stage)])

            @block.tensor
            def _(pe):
                pe.wait_ge(loaded, 96)

                def turn(t, u):
                    pe.wait_ge(staged, t + 1)
                    at_least(pe, out, t - 1)
                    for k in range(KD):
                        last = pe.transpose(ps_x[u][:, k * P:(k + 1) * P], cur[u][:, 0, k * P:(k + 1) * P], co.ident[:, :])
                    last.then_inc(turned, 1)

                def up(t, u):
                    pe.wait_ge(out, t + 1)
                    at_least(pe, bent, t - 1)
                    for m in range(K2):
                        for k in range(KD):
                            last = pe.matmul(ps_h[u][:, m, :], w1[:, k, m * P:(m + 1) * P], xt[u][:, k, :],
                                             start=(k == 0), stop=(k == KD - 1))
                    last.then_inc(made, 1)

                def down(t, u):
                    pe.wait_ge(bent, t + 1)
                    at_least(pe, done, t - 1)
                    for k in range(K2):
                        last = pe.matmul(ps_f[u][:, 0:D], ht[u][:, k, :], w2[:, k, :], start=(k == 0), stop=(k == K2 - 1))
                    last.then_inc(mixed, 1)

                over_tiles(pe, NT, [(0, turn), (1, up), (2, down)])

            @block.scalar
            def _(act):
                act.preload_act_table(ACT.Gelu_apprx_tanh)
                act.wait_ge(loaded, 96)

                def bend(t, u):
                    act.wait_ge(made, t + 1)
                    at_least(act, mixed, t - 1)
                    for m in range(K2):
                        last = act.activation(ht[u][:, m, :], ps_h[u][:, m, :], ACT.Gelu_apprx_tanh, bias=b1[:, m:m + 1])
                    last.then_inc(bent, 1)

                over_tiles(act, NT, [(1, bend)])

            @block.vector
            def _(dve):
                def evacuate(t, u):
                    dve.wait_ge(turned, t + 1)
                    at_least(dve, made, t - 1)
                    dve.tensor_copy(xt[u][:, :, :], ps_x[u][:, 0:D].rearrange("p (k c) -> p k c", k=KD)).then_inc(out, 1)

                def rest(t, u):
                    dve.wait_ge(mixed, t + 1)
                    dve.wait_ge(rested, t + 1)
                    dve.tensor_tensor(base[:, bass.ds(t, 1), :], ps_f[u][:, 0:D].unsqueeze(1), y[:, bass.ds(t, 1), :], ALU.add)\
                       .then_inc(done, 1)

                over_tiles(dve, NT, [(0, evacuate), (2, rest)])


def add_affine(nc, co, z, g_ap, b_ap):
    half = 17
    with phase(co, "affine") as ph:
        g, b = ph.sb("g", [P, 1, D]), ph.sb("b", [P, 1, D])
        loaded, v, w = ph.sem("loaded"), ph.sem("v"), ph.sem("w")
        with nc.Block() as block:
            @block.sync
            def _(sp):
                sp.dma_start(g[:, 0, :], row_on_all(g_ap, D)).then_inc(loaded, 16)
                sp.dma_start(b[:, 0, :], row_on_all(b_ap, D)).then_inc(loaded, 16)

            def steps(eng, lo, hi, sem):
                eng.wait_ge(loaded, 32)
                n = hi - lo
                zz, xx = z[:, lo:hi, :], co.x[:, lo:hi, :]
                eng.tensor_tensor(zz, zz, g[:, :, :].to_broadcast([P, n, D]), ALU.mult).then_inc(sem, 1)
                eng.wait_ge(sem, 1)
                eng.tensor_tensor(xx, xx, zz, ALU.add).then_inc(sem, 1)
                eng.wait_ge(sem, 2)
                eng.tensor_tensor(xx, xx, b[:, :, :].to_broadcast([P, n, D]), ALU.add)

            @block.vector
            def _(dve):
                steps(dve, 0, half, v)

            @block.gpsimd
            def _(gp):
                steps(gp, half, NT, w)
def top1_logits(nc, co, h, a, logits, table):
    HK = HID0 // P
    H2 = HK // 2
    with phase(co, "top1") as ph:
        w1, wg = ph.sb("w1", [P, KD, HID0]), ph.sb("wg", [P, HK, EXP])
        b1, bg = ph.sb("b1", [P, HK]), ph.sb("bg", [P, 1, EXP])
        cur, xt, ht = ([ph.sb(f"{n}{u}", shape) for u in range(2)] for n, shape in (
            ("cur", [P, 1, D]), ("xt", [P, KD, P]), ("ht", [P, HK, P])))
        ps_x, ps_g = ([ph.ps(f"{n}{u}", [P, 512]) for u in range(2)] for n in ("ps_x", "ps_g"))
        ps_h = [[ph.ps(f"ps_h{i}{u}", [P, H2, P]) for u in range(2)] for i in range(2)]
        loaded, tabled, staged, turned, out, done, seen = (ph.sem(n) for n in (
            "loaded", "tabled", "staged", "turned", "out", "done", "seen"))
        made, bent, used = ([ph.sem(f"{n}{i}") for i in range(2)] for n in ("made", "bent", "used"))
        with nc.Block() as block:
            @block.sync
            def _(sp):
                sp.dma_start(w1[:, :, :], a["L0_ffn_W1"].rearrange("(k p) d -> p k d", p=P)).then_inc(loaded, 16)
                sp.dma_start(wg[:, :, :], a["L0_ffn_Wg"].rearrange("(k p) e -> p k e", p=P)).then_inc(loaded, 16)
                with nc.allow_non_contiguous_dma(reason="a bias with its features on partitions"):
                    sp.dma_start(b1[:, :], a["L0_ffn_b1"].rearrange("(k p) -> p k", p=P)).then_inc(loaded, 16)
                sp.dma_start(bg[:, 0, :], row_on_all(a["L0_ffn_bg"], EXP)).then_inc(loaded, 16)
                sp.dma_start(table.rearrange("(t p) d -> p t d", p=P), h[:, :, :]).then_inc(tabled, 16)
                sp.wait_ge(tabled, 16)

            @block.gpsimd
            def _(gp):
                def stage(t, u):
                    at_least(gp, turned, t - 1)
                    gp.sem_inc(seen, 1)
                    gp.tensor_copy(cur[u][:, :, :], h[:, bass.ds(t, 1), :]).then_inc(staged, 1)

                over_tiles(gp, NT, [(0, stage)])

            @block.tensor
            def _(pe):
                pe.wait_ge(loaded, 64)

                def turn(t, u):
                    pe.wait_ge(staged, t + 1)
                    at_least(pe, out, t - 1)
                    for k in range(KD):
                        last = pe.transpose(ps_x[u][:, k * P:(k + 1) * P], cur[u][:, 0, k * P:(k + 1) * P], co.ident[:, :])
                    last.then_inc(turned, 1)

                def up(i):
                    def body(t, u):
                        pe.wait_ge(out, t + 1)
                        at_least(pe, bent[i], t - 1)
                        for m in range(H2):
                            for k in range(KD):
                                last = pe.matmul(ps_h[i][u][:, m, :], w1[:, k, (i * H2 + m) * P:(i * H2 + m + 1) * P], xt[u][:, k, :],
                                                 start=(k == 0), stop=(k == KD - 1))
                        last.then_inc(made[i], 1)
                    return body

                def gate(i):
                    def body(t, u):
                        pe.wait_ge(bent[i], t + 1)
                        if i == 0:
                            at_least(pe, done, t - 1)
                        for m in range(i * H2, (i + 1) * H2):
                            last = pe.matmul(ps_g[u][:, 0:EXP], ht[u][:, m, :], wg[:, m, :], start=(m == 0), stop=(m == HK - 1))
                        last.then_inc(used[i], 1)
                    return body

                over_tiles(pe, NT, [(0, turn), (1, up(0)), (1, up(1)), (2, gate(0)), (2, gate(1))])

            @block.scalar
            def _(act):
                act.preload_act_table(ACT.Gelu)
                act.wait_ge(loaded, 64)

                def bend(i):
                    def body(t, u):
                        act.wait_ge(made[i], t + 1)
                        at_least(act, used[i], t - 1)
                        for m in range(H2):
                            last = act.activation(ht[u][:, i * H2 + m, :], ps_h[i][u][:, m, :], ACT.Gelu, bias=b1[:, i * H2 + m:i * H2 + m + 1])
                        last.then_inc(bent[i], 1)
                    return body

                over_tiles(act, NT, [(1, bend(0)), (1, bend(1))])

            @block.vector
            def _(dve):
                dve.wait_ge(loaded, 64)

                def evacuate(t, u):
                    dve.wait_ge(turned, t + 1)
                    at_least(dve, made[1], t - 1)
                    dve.tensor_copy(xt[u][:, :, :], ps_x[u][:, 0:D].rearrange("p (k c) -> p k c", k=KD)).then_inc(out, 1)

                def rest(t, u):
                    dve.wait_ge(used[1], t + 1)
                    dve.tensor_tensor(logits[:, bass.ds(t, 1), :], ps_g[u][:, 0:EXP].unsqueeze(1), bg[:, :, :], ALU.add)\
                       .then_inc(done, 1)

                over_tiles(dve, NT, [(0, evacuate), (2, rest)])


def top2_logits(nc, co, h, a, logits):
    with phase(co, "top2") as ph:
        wr, br = ph.sb("wr", [P, KD, EXP]), ph.sb("br", [P, 1, EXP])
        cur, xt = ([ph.sb(f"{n}{u}", shape) for u in range(2)] for n, shape in (("cur", [P, 1, D]), ("xt", [P, KD, P])))
        ps_x, ps_g = ([ph.ps(f"{n}{u}", [P, 512]) for u in range(2)] for n in ("ps_x", "ps_g"))
        loaded, staged, turned, out, made, done, seen = (ph.sem(n) for n in (
            "loaded", "staged", "turned", "out", "made", "done", "seen"))
        with nc.Block() as block:
            @block.sync
            def _(sp):
                sp.dma_start(wr[:, :, :], a["L1_ffn_Wr"].rearrange("(k p) e -> p k e", p=P)).then_inc(loaded, 16)
                sp.dma_start(br[:, 0, :], row_on_all(a["L1_ffn_br"], EXP)).then_inc(loaded, 16)

            @block.gpsimd
            def _(gp):
                def stage(t, u):
                    at_least(gp, turned, t - 1)
                    gp.sem_inc(seen, 1)
                    gp.tensor_copy(cur[u][:, :, :], h[:, bass.ds(t, 1), :]).then_inc(staged, 1)

                over_tiles(gp, NT, [(0, stage)])

            @block.tensor
            def _(pe):
                pe.wait_ge(loaded, 32)

                def turn(t, u):
                    pe.wait_ge(staged, t + 1)
                    at_least(pe, out, t - 1)
                    for k in range(KD):
                        last = pe.transpose(ps_x[u][:, k * P:(k + 1) * P], cur[u][:, 0, k * P:(k + 1) * P], co.ident[:, :])
                    last.then_inc(turned, 1)

                def gate(t, u):
                    pe.wait_ge(out, t + 1)
                    at_least(pe, done, t - 1)
                    for k in range(KD):
                        last = pe.matmul(ps_g[u][:, 0:EXP], xt[u][:, k, :], wr[:, k, :], start=(k == 0), stop=(k == KD - 1))
                    last.then_inc(made, 1)

                over_tiles(pe, NT, [(0, turn), (1, gate)])

            @block.scalar
            def _(act):
                act.preload_act_table(ACT.Exp)

                def evacuate(t, u):
                    act.wait_ge(turned, t + 1)
                    at_least(act, made, t - 1)
                    act.copy(xt[u][:, :, :], ps_x[u][:, 0:D].rearrange("p (k c) -> p k c", k=KD)).then_inc(out, 1)

                over_tiles(act, NT, [(0, evacuate)])

            @block.vector
            def _(dve):
                dve.wait_ge(loaded, 32)

                def rest(t, u):
                    dve.wait_ge(made, t + 1)
                    dve.tensor_tensor(logits[:, bass.ds(t, 1), :], ps_g[u][:, 0:EXP].unsqueeze(1), br[:, :, :], ALU.add)\
                       .then_inc(done, 1)

                over_tiles(dve, NT, [(1, rest)])


def expert_buffers(co, which):
    HK = HID1 // P
    w1 = co.sbuf(f"expert_w1_{which}", [P, 1 if which == 0 else EXP, KD, HID1])
    w2 = co.sbuf(f"expert_w2_{which}", [P, EXP, HK, D])
    b2 = co.sbuf(f"expert_b2_{which}", [P, EXP, D])
    small = [co.sbuf("expert_b1_0", [P, HK])] if which == 0 else [co.sbuf(n, [P, KD, EXP]) for n in ("expert_g", "expert_b")]
    return w1, w2, b2, *small


def fetch_experts(nc, co, which, a, buffers):
    w1, w2, b2, *small = buffers
    fetched = co.fetched[which]
    with nc.Block() as block:
        @block.sync
        def _(sp):
            if which == 0:
                sp.dma_start(w1[:, 0, :, :], a["L0_ffn_W1"].rearrange("(k p) d -> p k d", p=P)).then_inc(fetched, 16)
                for h in range(2):
                    sp.dma_start(w2[:, h * 4:h * 4 + 4, :, :], a["L0_ffn_Wd"][h * 4:h * 4 + 4].rearrange("e (k p) d -> p e k d", p=P))\
                      .then_inc(fetched, 16)
                with nc.allow_non_contiguous_dma(reason="a bias with its features on partitions"):
                    sp.dma_start(small[0][:, :], a["L0_ffn_b1"].rearrange("(k p) -> p k", p=P)).then_inc(fetched, 16)
            else:
                with nc.allow_non_contiguous_dma(reason="an affine map with its features on partitions"):
                    for there, v in zip(small, ("L1_ffn_ln_g", "L1_ffn_ln_b")):
                        for k in range(KD):
                            sp.dma_start(there[:, k, :], a[v][:, k * P:(k + 1) * P].rearrange("e p -> p e")).then_inc(fetched, 16)
                for e in range(EXP):
                    sp.dma_start(w1[:, e, :, :], a["L1_ffn_W1"][e].rearrange("(k p) d -> p k d", p=P)).then_inc(fetched, 16)
                    sp.dma_start(w2[:, e, :, :], a["L1_ffn_W2"][e].rearrange("(k p) d -> p k d", p=P)).then_inc(fetched, 16)
            bias = a["L0_ffn_bd" if which == 0 else "L1_ffn_b2"].rearrange("e d -> (e d)")
            sp.dma_start(b2[:, :, :].rearrange("p e d -> p (e d)"), row_on_all(bias, EXP * D)).then_inc(fetched, 16)


def route(nc, co, name, logits, picks, tiles, ids, weight, slot_of, token_of, expert_of, rows=None, table=None):
    with phase(co, name) as ph:
        left = ph.sb("left", [P, NT, EXP])
        best = ph.sb("best", [P, picks, NT])
        pick = [ph.sb(f"pick{i}", [P, NT, EXP]) for i in range(picks)]
        member = ph.sb("member", [P, EXP, NT])
        rank, slot, tmp = ph.sb("rank", [P, EXP, NT]), ph.sb("slot", [P, NT, EXP]), ph.sb("tmp", [P, NT, EXP])
        order = ph.sb("order", [P, 1, EXP])
        col = ph.sb("col", [P, NT])
        valid, missing = ph.sb("valid", [P, NT]), ph.sb("missing", [P, NT])
        token = ph.sb("token", [P, NT])
        count, ntile, end = (ph.sb(n, [P, EXP]) for n in ("count", "ntile", "end"))
        total_i = ph.sb("total_i", [P, EXP], I32)
        begin = ph.sb("begin", [P, 1, EXP])
        zeros = ph.sb("zeros", [P, NT])
        slots, slot_i = ph.sb("slots", [P, picks, NT]), ph.sb("slot_i", [P, picks, NT], U32)
        ring = ph.sb("ring", [P, NT], U32)
        past = ph.sb("past", [1, tiles, EXP])
        exp_f, exp_i, moved = ph.sb("exp_f", [1, tiles]), ph.sb("exp_i", [1, tiles], I32), ph.sb("moved", [1, tiles], I32)
        back = ph.sb("back", [tiles, P])
        ps_c, ps_b = ph.ps("ps_c", [P, 512]), ph.ps("ps_b", [P, 512])
        iot, chain, mm, zeroed, exps, sloted, cols, loaded, seen, conv = (ph.sem(n) for n in (
            "iot", "chain", "mm", "zeroed", "exps", "sloted", "cols", "loaded", "seen", "conv"))
        placed = ph.gp_dma_sem(0)
        tabled = ph.sem("tabled")
        bcast = lambda ap: ap.to_broadcast([P, NT, EXP])
        with nc.Block() as block:
            @block.vector
            def _(dve):
                n = [0]

                def step(ins):
                    n[0] += 1
                    ins.then_inc(chain, 1)
                    dve.wait_ge(chain, n[0])

                dve.memset(zeros[:, :], 0.0)
                step(dve.memset(valid[:, :], 1.0))
                step(dve.tensor_scalar(valid[:, NT - 1:NT], co.rowno[:, :], float(LAST), None, ALU.is_lt))
                step(dve.tensor_scalar(missing[:, :], valid[:, :], -1e5, 1e5, ALU.mult, ALU.add))
                step(dve.tensor_scalar(order[:, 0, :], co.iota[:, 0:EXP], -1.0, float(EXP), ALU.mult, ALU.add))
                dve.wait_ge(iot, 1)
                source = logits
                for i in range(picks):
                    step(dve.tensor_reduce(best[:, i, :], source[:, :, :], AX.X, ALU.max))
                    step(dve.tensor_tensor(tmp[:, :, :], source[:, :, :], bcast(best[:, i, :].unsqueeze(2)), ALU.is_equal))
                    step(dve.tensor_tensor(tmp[:, :, :], tmp[:, :, :], bcast(order[:, :, :]), ALU.mult))
                    step(dve.tensor_reduce(col[:, :], tmp[:, :, :], AX.X, ALU.max))
                    step(dve.tensor_tensor(pick[i][:, :, :], tmp[:, :, :], bcast(col[:, :].unsqueeze(2)), ALU.is_equal))
                    if i + 1 < picks:
                        step(dve.scalar_tensor_tensor(out=left[:, :, :], in0=pick[i][:, :, :], scalar=-BIG, in1=source[:, :, :],
                                                      op0=ALU.mult, op1=ALU.add))
                        source = left
                if picks == 1:
                    step(dve.tensor_tensor(left[:, :, :], logits[:, :, :], bcast(best[:, 0, :].unsqueeze(2)), ALU.subtract))
                    dve.wait_ge(exps, 1)
                    step(dve.reduce_sum(col[:, :], tmp[:, :, :], AX.X))
                    step(dve.reciprocal(weight[:, 0, :], col[:, :]))
                else:
                    step(dve.tensor_tensor(col[:, :], best[:, 1, :], best[:, 0, :], ALU.subtract))
                    dve.wait_ge(exps, 1)
                    step(dve.tensor_scalar(col[:, :], best[:, 1, :], 1.0, None, ALU.add))
                    step(dve.reciprocal(weight[:, 0, :], col[:, :]))
                    step(dve.tensor_tensor(weight[:, 1, :], best[:, 1, :], weight[:, 0, :], ALU.mult))
                for i in range(picks):
                    step(dve.tensor_tensor(pick[i][:, :, :], pick[i][:, :, :], bcast(valid[:, :].unsqueeze(2)), ALU.mult))
                turned = lambda ap: ap.rearrange("p t e -> p e t")
                if picks == 1:
                    step(dve.tensor_copy(member[:, :, :], turned(pick[0][:, :, :])))
                else:
                    step(dve.tensor_tensor(member[:, :, :], turned(pick[0][:, :, :]), turned(pick[1][:, :, :]), ALU.add))
                for e in range(EXP):
                    step(dve.tensor_tensor_scan(rank[:, e, :], member[:, e, :], zeros[:, :], 0.0, ALU.add, ALU.add))
                step(dve.tensor_copy(count[:, :], rank[:, :, NT - 1]))
                dve.sem_inc(sloted, 1)
                dve.wait_ge(mm, 1)
                step(dve.tensor_scalar(total_i[:, :], ps_c[:, EXP:2 * EXP], float(P - 1), None, ALU.add))
                step(dve.tensor_scalar(total_i[:, :], total_i[:, :], 7, None, ALU.arith_shift_right))
                step(dve.tensor_copy(ntile[:, :], total_i[:, :]))
                step(dve.tensor_tensor_scan(end[:, :], ntile[:, :], zeros[:, 0:EXP], 0.0, ALU.add, ALU.add))
                step(dve.tensor_tensor(begin[:, 0, :], end[:, :], ntile[:, :], ALU.subtract))
                step(dve.scalar_tensor_tensor(out=begin[:, 0, :], in0=begin[:, 0, :], scalar=float(P), in1=ps_c[:, 0:EXP],
                                              op0=ALU.mult, op1=ALU.add))
                step(dve.tensor_tensor(slot[:, :, :], rank[:, :, :].rearrange("p e t -> p t e"), bcast(begin[:, :, :]), ALU.add))
                for i in range(picks):
                    step(dve.tensor_tensor(tmp[:, :, :], slot[:, :, :], pick[i][:, :, :], ALU.mult))
                    step(dve.reduce_sum(slots[:, i, :], tmp[:, :, :], AX.X))
                    step(dve.scalar_tensor_tensor(out=slot_i[:, i, :], in0=slots[:, i, :], scalar=-1.0, in1=missing[:, :],
                                                  op0=ALU.add, op1=ALU.add))
                    step(dve.tensor_scalar(slot_of[:, i, :], slots[:, i, :], -1.0, 0.0, ALU.add, ALU.max))
                dve.sem_inc(sloted, 1)
                step(dve.tensor_tensor(past[:, :, :], co.iota[0:1, 0:tiles].unsqueeze(2).to_broadcast([1, tiles, EXP]),
                                       end[0:1, :].unsqueeze(1).to_broadcast([1, tiles, EXP]), ALU.is_ge))
                step(dve.reduce_sum(exp_f[:, :], past[:, :, :], AX.X))
                step(dve.tensor_scalar(exp_i[:, :], exp_f[:, :], float(EXP - 1), None, ALU.min))
                pack(dve, step, expert_of, exp_i, moved, tiles, ROUNDS)
                dve.wait_ge(mm, 2)
                dve.tensor_copy(token_of[:, :], ps_b[:, 0:tiles]).then_inc(conv, 1)

            @block.scalar
            def _(act):
                act.preload_act_table(ACT.Exp)
                if picks == 1:
                    act.wait_ge(chain, 10)
                    act.activation(tmp[:, :, :], left[:, :, :], ACT.Exp).then_inc(exps, 1)
                else:
                    act.wait_ge(chain, 16)
                    act.activation(best[:, 1, :], col[:, :], ACT.Exp).then_inc(exps, 1)

            @block.tensor
            def _(pe):
                pe.wait_ge(sloted, 1)
                pe.matmul(ps_c[:, 0:EXP], co.before[:, :], count[:, :], start=True, stop=True)
                pe.matmul(ps_c[:, EXP:2 * EXP], co.ones[:, :], count[:, :], start=True, stop=True).then_inc(mm, 1)
                pe.wait_ge(loaded, 16)
                pe.transpose(ps_b[:, 0:tiles], back[:, :], co.ident[0:tiles, 0:tiles]).then_inc(mm, 1)

            @block.gpsimd
            def _(gp):
                gp.iota(token[:, :], pattern=[[P, NT]], base=0, channel_multiplier=1, allow_small_or_imprecise_dtypes=True)\
                  .then_inc(iot, 1)
                gp.memset(back[:, :], 0.0).then_inc(zeroed, 1)
                gp.wait_ge(iot, 1)
                gp.wait_ge(sloted, 2)
                gp.wait_ge(zeroed, 17)
                with gp.Fori(0, picks) as i:
                    gp.tensor_copy(ring[:, :].unsqueeze(1), slot_i[:, bass.ds(i, 1), :]).then_inc(cols, 1)
                    gp.wait_ge(cols, i + 1)
                    gp.sem_inc(seen, 1)
                    for t in range(NT):
                        gp.indirect_dma_start(ids.rearrange("(s a) -> s a", a=1),
                                              bass.IndirectOffsetOnAxis(ap=ring[:, t:t + 1], axis=0),
                                              token[:, t:t + 1], None, bounds_check=tiles * P - 1,
                                              oob_is_err=False).then_inc(placed, 16)
                    gp.wait_ge(placed, i * (16 * NT) + 16 * NT)
                    gp.sem_inc(seen, 1)

            @block.sync
            def _(sp):
                if rows is not None:
                    sp.dma_start(table.rearrange("(t p) d -> p t d", p=P), rows[:, :, :]).then_inc(tabled, 16)
                    sp.wait_ge(tabled, 16)
                sp.wait_ge(zeroed, 1)
                sp.dma_start(ids.rearrange("(s p) -> s p", p=P), back[:, :]).then_inc(zeroed, 16)
                sp.wait_ge(placed, picks * NT * 16)
                sp.dma_start(back[:, :], ids.rearrange("(s p) -> s p", p=P)).then_inc(loaded, 16)
                sp.wait_ge(loaded, 16)


def experts(nc, co, name, tiles, table, result, token_of, expert_of, buffers, a):
    shared = name == "exp0"
    HK = HID1 // P
    H2 = HK // 2
    HH = HID1 // 2
    with phase(co, name) as ph:
        if shared:
            w1, w2, b2, b1 = buffers
        else:
            w1, w2, b2, ln_g, ln_b = buffers
            b1 = ph.sb("b1", [3, EXP, HID1], BF16)
            hid = [ph.sb(f"hid{i}", [P, HH]) for i in range(2)]
            ps_t = [ph.ps(f"ps_t{i}", [P, H2, P]) for i in range(2)]
        index, rows = ([ph.sb(f"{n}{u}", shape, dt) for u in range(2)] for n, shape, dt in (
            ("index", [P, 1], U32), ("rows", [P, D], F32)))
        xt, y = ([ph.sb(f"{n}{u}", shape) for u in range(2)] for n, shape in (("xt", [P, KD, P]), ("y", [P, 1, D])))
        ht = ph.sb("ht", [P, HK, P])
        ps_x, ps_y = ([ph.ps(f"{n}{u}", [P, 512]) for u in range(2)] for n in ("ps_x", "ps_y"))
        ps_h = [ph.ps(f"ps_h{i}", [P, H2, P]) for i in range(2)]
        loaded, indexed, turned, out, done, seen = (ph.sem(n) for n in (
            "loaded", "indexed", "turned", "out", "done", "seen"))
        arrived = co.fetched[0 if shared else 1]
        stored = [ph.sem(f"stored{u}") for u in range(2)]
        got = [ph.gp_dma_sem(u) for u in range(2)]
        made, bent, used, flipped, spread = ([ph.sem(f"{n}{i}") for i in range(2)] for n in
                                             ("made", "bent", "used", "flipped", "spread"))
        fetches = 16 * (5 if shared else 2 * EXP + 5)
        with nc.Block() as block:
            @block.sync
            def _(sp):
                if not shared:
                    sp.dma_start(b1[:, :, :].rearrange("q e d -> q (e d)"), a["b1_parts"]).then_inc(loaded, 16)

                def store(s, u):
                    sp.wait_ge(done, s + 1)
                    sp.dma_start(result[bass.ds(s * P, P), :], y[u][:, 0, :]).then_inc(stored[u], 16)

                over_tiles(sp, tiles, [(0, store)])
                for u in range(2):
                    sp.wait_ge(stored[u], 8 * tiles)

            @block.gpsimd
            def _(gp):
                def gather(s, u):
                    at_least(gp, turned, s - 1)
                    gp.sem_inc(seen, 1)
                    gp.tensor_copy(index[u][:, :], token_of[:, bass.ds(s, 1)]).then_inc(indexed, 1)
                    gp.wait_ge(indexed, s + 1)
                    gp.sem_inc(seen, 1)
                    gp.indirect_dma_start(rows[u][:, :], None, table, bass.IndirectOffsetOnAxis(ap=index[u][:, 0:1], axis=0)).then_inc(got[u], 16)

                over_tiles(gp, tiles, [(0, gather)])

            @block.tensor
            def _(pe):
                pe.wait_ge(arrived, fetches)
                if not shared:
                    pe.wait_ge(loaded, 16)

                def turn(s, u, e):
                    pe.wait_ge(got[u], (s - u) * 8 + 16)
                    at_least(pe, out, s - 1)
                    for k in range(KD):
                        last = pe.transpose(ps_x[u][:, k * P:(k + 1) * P], rows[u][:, k * P:(k + 1) * P], co.ident[:, :])
                    last.then_inc(turned, 1)

                def up(i):
                    def body(s, u, e):
                        pe.wait_ge(out, s + 1)
                        at_least(pe, bent[i], s)
                        if shared:
                            for m in range(H2):
                                for k in range(KD):
                                    last = pe.matmul(ps_h[i][:, m, :], w1[:, 0, k, (i * H2 + m) * P:(i * H2 + m + 1) * P],
                                                     xt[u][:, k, :], start=(k == 0), stop=(k == KD - 1))
                        else:
                            where = ps_h[i][:, :, :].rearrange("p m c -> p (m c)").unsqueeze(1)
                            pe.matmul(where, co.ones3[:, :], b1[:, bass.ds(e, 1), i * HH:(i + 1) * HH], start=True, stop=False)
                            for k in range(KD):
                                last = pe.matmul(where, xt[u][:, k, :], w1[:, bass.ds(e, 1), k, i * HH:(i + 1) * HH],
                                                 start=False, stop=(k == KD - 1))
                        last.then_inc(made[i], 1)
                    return body

                def flip(i):
                    def body(s, u, e):
                        pe.wait_ge(bent[i], s + 1)
                        at_least(pe, spread[i], s)
                        for m in range(H2):
                            last = pe.transpose(ps_t[i][:, m, :], hid[i][:, m * P:(m + 1) * P], co.ident[:, :])
                        last.then_inc(flipped[i], 1)
                    return body

                def down(i):
                    def body(s, u, e):
                        pe.wait_ge(bent[i] if shared else spread[i], s + 1)
                        if i == 0:
                            at_least(pe, done, s - 1)
                        for m in range(i * H2, (i + 1) * H2):
                            last = pe.matmul(ps_y[u][:, 0:D].unsqueeze(1), ht[:, m, :], w2[:, bass.ds(e, 1), m, :],
                                             start=(m == 0), stop=(m == HK - 1))
                        last.then_inc(used[i], 1)
                    return body

                if shared:
                    over_tiles(pe, tiles, [(1, up(0)), (2, down(1)), (0, turn), (1, up(1)), (1, down(0))], expert_of)
                else:
                    over_tiles(pe, tiles, [(1, up(0)), (2, down(0)), (0, turn), (1, up(1)), (2, down(1)), (1, flip(0)), (1, flip(1))], expert_of)

            @block.scalar
            def _(act):
                act.preload_act_table(ACT.Gelu)
                act.wait_ge(arrived, fetches)

                def bend(i):
                    def body(s, u):
                        act.wait_ge(made[i], s + 1)
                        if shared:
                            at_least(act, used[i], s)
                            for m in range(H2):
                                last = act.activation(ht[:, i * H2 + m, :], ps_h[i][:, m, :], ACT.Gelu,
                                                      bias=b1[:, i * H2 + m:i * H2 + m + 1])
                        else:
                            at_least(act, flipped[i], s)
                            last = act.activation(hid[i][:, :], ps_h[i][:, :, :].rearrange("p m c -> p (m c)"), ACT.Gelu)
                        last.then_inc(bent[i], 1)
                    return body

                over_tiles(act, tiles, [(1, bend(0)), (1, bend(1))])

            @block.vector
            def _(dve):
                dve.wait_ge(arrived, fetches)

                def evacuate(s, u, e):
                    dve.wait_ge(turned, s + 1)
                    at_least(dve, made[1], s - 1)
                    if shared:
                        dve.tensor_copy(xt[u][:, :, :], ps_x[u][:, 0:D].rearrange("p (k c) -> p k c", k=KD)).then_inc(out, 1)
                    else:
                        for k in range(KD):
                            last = dve.tensor_scalar(xt[u][:, k, :], ps_x[u][:, k * P:(k + 1) * P], ln_g[:, k, bass.ds(e, 1)],
                                                     ln_b[:, k, bass.ds(e, 1)], ALU.mult, ALU.add)
                        last.then_inc(out, 1)

                def unflip(i):
                    def body(s, u, e):
                        dve.wait_ge(flipped[i], s + 1)
                        at_least(dve, used[i], s)
                        dve.tensor_copy(ht[:, i * H2:(i + 1) * H2, :], ps_t[i][:, :, :]).then_inc(spread[i], 1)
                    return body

                def rest(s, u, e):
                    dve.wait_ge(used[1], s + 1)
                    at_least(dve, stored[u], (s - u) * 8)
                    dve.tensor_tensor(y[u][:, :, :], ps_y[u][:, 0:D].unsqueeze(1), b2[:, bass.ds(e, 1), :], ALU.add).then_inc(done, 1)

                if shared:
                    over_tiles(dve, tiles, [(2, rest), (0, evacuate)], expert_of)
                else:
                    over_tiles(dve, tiles, [(0, evacuate), (2, rest), (1, unflip(0)), (1, unflip(1))], expert_of)


def combine(nc, co, name, picks, result, slot_of, weight):
    with phase(co, name) as ph:
        R = 5
        ring = ph.sb("ring", [P, NT], U32)
        rows = [ph.sb(f"rows{k}", [P, 1, D]) for k in range(R)]
        got = [ph.gp_dma_sem(k) for k in range(R)]
        cols, seen, added = ph.sem("cols"), ph.sem("seen"), ph.sem("added")
        turns = NT // R
        with nc.Block() as block:
            @block.gpsimd
            def _(gp):
                with gp.Fori(0, picks) as i:
                    gp.wait_ge(added, i * NT + R)
                    gp.sem_inc(seen, 1)
                    gp.tensor_copy(ring[:, :].unsqueeze(1), slot_of[:, bass.ds(i, 1), :]).then_inc(cols, 1)
                    gp.wait_ge(cols, i + 1)
                    gp.sem_inc(seen, 1)
                    for t in range(NT):
                        gp.wait_ge(added, i * NT + (t + 1))
                        gp.sem_inc(seen, 1)
                        gp.indirect_dma_start(rows[t % R][:, 0, :], None, result,
                                              bass.IndirectOffsetOnAxis(ap=ring[:, t:t + 1], axis=0)).then_inc(got[t % R], 16)

            @block.vector
            def _(dve):
                dve.sem_inc(added, R)
                for i in range(picks):
                    with dve.Fori(0, turns) as t:
                        for k in range(R):
                            mine = co.x[:, bass.ds(t * R + k, 1), :]
                            dve.wait_ge(got[k], t * 16 + (i * turns * 16 + 16))
                            if i:
                                dve.wait_ge(added, t * R + k + ((i - 1) * NT + R + 1))
                            dve.scalar_tensor_tensor(out=mine, in0=rows[k][:, :, :], scalar=weight[:, i, bass.ds(t * R + k, 1)],
                                                     in1=mine, op0=ALU.mult, op1=ALU.add).then_inc(added, 1)
def split_bias(nc, co, bias, parts):
    n = bias.shape[0] // P
    with phase(co, "bias") as ph:
        whole, rest = ph.sb("whole", [P, n]), ph.sb("rest", [P, n])
        part = [ph.sb(f"part{i}", [P, n], BF16) for i in range(3)]
        loaded, made, stored = ph.sem("loaded"), ph.sem("made"), ph.sem("stored")
        with nc.Block() as block:
            @block.sync
            def _(sp):
                sp.dma_start(whole[:, :], bias.rearrange("(p n) -> p n", p=P)).then_inc(loaded, 16)
                sp.wait_ge(made, 5)
                for i in range(3):
                    sp.dma_start(parts[i, :].rearrange("(p n) -> p n", p=P), part[i][:, :]).then_inc(stored, 16)
                sp.wait_ge(stored, 48)

            @block.vector
            def _(dve):
                dve.wait_ge(loaded, 16)
                dve.tensor_copy(part[0][:, :], whole[:, :]).then_inc(made, 1)
                dve.wait_ge(made, 1)
                dve.tensor_tensor(rest[:, :], whole[:, :], part[0][:, :], ALU.subtract).then_inc(made, 1)
                dve.wait_ge(made, 2)
                dve.tensor_copy(part[1][:, :], rest[:, :]).then_inc(made, 1)
                dve.wait_ge(made, 3)
                dve.tensor_tensor(rest[:, :], rest[:, :], part[1][:, :], ALU.subtract).then_inc(made, 1)
                dve.wait_ge(made, 4)
                dve.tensor_copy(part[2][:, :], rest[:, :]).then_inc(made, 1)


def gat_inputs(nc, co, name, h, a, layer, heads, table, r_parts, att, acc, top):
    ch = D // heads
    W = D + heads
    junk = acc.shape[2] - heads * (ch + 1)
    with phase(co, name) as ph:
        w = {s: ph.sb("w" + s, [P, KD, W]) for s in "lr"}
        prod = ph.sb("prod", [P, KD, D])
        folded = {s: ph.sb("folded" + s, [P, KD, heads]) for s in "lr"}
        attb, att4 = ph.sb("attb", [P, 1, D]), ph.sb("att4", [P, 1, D])
        cur, xt = ([ph.sb(f"{n}{u}", shape) for u in range(2)] for n, shape in (("cur", [P, 1, D]), ("xt", [P, KD, P])))
        xl = ph.sb("xl", [P, NT, W])
        arf, mags = ph.sb("arf", [P, NT, heads]), ph.sb("mags", [P, NT, heads])
        self_l, first, gap = (ph.sb(n, [P, NT, heads]) for n in ("self_l", "first", "gap"))
        weight = ph.sb("weight", [P, NT, heads])
        topb = ph.sb("topb", [P, NT, heads], BF16)
        rest, both, size = ([ph.sb(f"{n}{u}", shape) for u in range(2)] for n, shape in (
            ("rest", [P, 1, W]), ("both", [P, 1, D]), ("size", [P, 1, D])))
        ps_x, ps_l, ps_r = ([ph.ps(f"{n}{u}", [P, 512]) for u in range(2)] for n in ("ps_x", "ps_l", "ps_r"))
        loaded, cleared, ready, chain, staged, turned, out, made, copied, summed, sized, scaled, finished = (
            ph.sem(n) for n in ("loaded", "cleared", "ready", "chain", "staged", "turned", "out", "made", "copied", "summed",
                                "sized", "scaled", "finished"))
        tabled, seen, self_, exped = (ph.sem(n) for n in ("tabled", "seen", "self", "exped"))
        with nc.Block() as block:
            @block.sync
            def _(sp):
                for s in "lr":
                    sp.dma_start(w[s][:, :, 0:D], a[f"L1_gnn_W{s}{layer}"].rearrange("(k p) d -> p k d", p=P)).then_inc(loaded, 16)
                flat = a[f"L1_gnn_att{layer}"].rearrange("h c -> (h c)")
                sp.dma_start(attb[:, 0, :], row_on_all(flat, D)).then_inc(loaded, 16)
                sp.wait_ge(cleared, 1)
                with nc.allow_non_contiguous_dma(reason="a vector with its features on partitions"):
                    if heads == 1:
                        sp.dma_start(att[:, :, 0], flat.rearrange("(k p) -> p k", p=P)).then_inc(loaded, 16)
                    else:
                        for i in range(heads):
                            at = i * ch % P
                            sp.dma_start(att[at:at + ch, i * ch // P, i:i + 1], flat[i * ch:(i + 1) * ch].rearrange("(p a) -> p a", a=1))\
                              .then_inc(loaded, 16)
                sp.wait_ge(copied, NT)
                sp.dma_start(table.rearrange("(t p) d -> p t d", p=P), xl[:, :, :]).then_inc(tabled, 16)
                sp.wait_ge(tabled, 16)

            @block.gpsimd
            def _(gp):
                def stage(t, u):
                    at_least(gp, turned, t - 1)
                    gp.sem_inc(seen, 1)
                    gp.tensor_copy(cur[u][:, :, :], h[:, bass.ds(t, 1), :]).then_inc(staged, 1)

                over_tiles(gp, NT, [(0, stage)])

            @block.tensor
            def _(pe):
                pe.wait_ge(ready, 1)

                def turn(t, u):
                    pe.wait_ge(staged, t + 1)
                    at_least(pe, out, t - 1)
                    for k in range(KD):
                        last = pe.transpose(ps_x[u][:, k * P:(k + 1) * P], cur[u][:, 0, k * P:(k + 1) * P], co.ident[:, :])
                    last.then_inc(turned, 1)

                def project(t, u):
                    pe.wait_ge(out, t + 1)
                    at_least(pe, copied, t - 1)
                    at_least(pe, summed, t - 1)
                    for s, where in (("l", ps_l[u]), ("r", ps_r[u])):
                        for k in range(KD):
                            last = pe.matmul(where[:, 0:W], xt[u][:, k, :], w[s][:, k, :], start=(k == 0), stop=(k == KD - 1))
                    last.then_inc(made, 1)

                over_tiles(pe, NT, [(0, turn), (1, project)])

            @block.scalar
            def _(act):
                act.preload_act_table(ACT.Exp)

                def evacuate(t, u):
                    act.wait_ge(turned, t + 1)
                    at_least(act, made, t - 1)
                    act.copy(xt[u][:, :, :], ps_x[u][:, 0:D].rearrange("p (k c) -> p k c", k=KD)).then_inc(out, 1)

                def copy(t, u):
                    act.wait_ge(made, t + 1)
                    act.copy(r_parts[:, bass.ds(t, 1), 0, :], ps_r[u][:, 0:W].unsqueeze(1))
                    act.copy(arf[:, bass.ds(t, 1), :], ps_r[u][:, D:W].unsqueeze(1))
                    act.copy(xl[:, bass.ds(t, 1), :], ps_l[u][:, 0:W].unsqueeze(1)).then_inc(copied, 1)

                def sizes(t, u):
                    act.wait_ge(summed, t + 1)
                    at_least(act, finished, t - 1)
                    act.activation(size[u][:, :, :], both[u][:, :, :], ACT.Abs)
                    act.copy(r_parts[:, bass.ds(t, 1), 1, :], rest[u][:, :, :]).then_inc(sized, 1)

                over_tiles(act, NT, [(0, evacuate), (2, sizes), (1, copy)])
                act.wait_ge(self_, 4)
                act.activation(weight[:, :, :], gap[:, :, :], ACT.Exp).then_inc(exped, 1)

            @block.vector
            def _(dve):
                n = [0]

                def step(ins):
                    n[0] += 1
                    ins.then_inc(chain, 1)
                    dve.wait_ge(chain, n[0])

                dve.memset(att[:, :, :], 0.0).then_inc(cleared, 1)
                if junk:
                    dve.memset(acc[:, :, D:D + junk], 0.0)
                dve.wait_ge(loaded, 16 * (3 + heads))
                step(dve.tensor_scalar(att[:, :, :], att[:, :, :], 0.4, None, ALU.mult))
                step(dve.tensor_scalar(att4[:, :, :], attb[:, :, :], 0.4, None, ALU.mult))
                for s in "lr":
                    step(dve.tensor_tensor(prod[:, :, :], w[s][:, :, 0:D], attb[:, :, :].to_broadcast([P, KD, D]), ALU.mult))
                    step(dve.tensor_reduce(folded[s][:, :, :], prod[:, :, :].rearrange("p k (h c) -> p k h c", h=heads), AX.X, ALU.add))
                    step(dve.tensor_scalar(w[s][:, :, D:W], folded[s][:, :, :], 0.6, None, ALU.mult))
                dve.sem_inc(ready, 1)

                def sums(t, u):
                    dve.wait_ge(copied, t + 1)
                    at_least(dve, finished, t - 1)
                    dve.tensor_tensor(both[u][:, :, :], xl[:, bass.ds(t, 1), 0:D], ps_r[u][:, 0:D].unsqueeze(1), ALU.add)
                    dve.tensor_tensor(rest[u][:, :, :], ps_r[u][:, 0:W].unsqueeze(1), r_parts[:, bass.ds(t, 1), 0, :], ALU.subtract)\
                       .then_inc(summed, 1)

                def finish(t, u):
                    dve.wait_ge(sized, t + 1)
                    dve.tensor_tensor(size[u][:, :, :], size[u][:, :, :], att4[:, :, :], ALU.mult).then_inc(scaled, 1)
                    dve.tensor_tensor(r_parts[:, bass.ds(t, 1), 2, :], rest[u][:, :, :], r_parts[:, bass.ds(t, 1), 1, :], ALU.subtract)
                    dve.wait_ge(scaled, t + 1)
                    dve.tensor_reduce(mags[:, bass.ds(t, 1), :], size[u][:, :, :].rearrange("p a (h c) -> p a h c", h=heads), AX.X, ALU.add)\
                       .then_inc(finished, 1)

                over_tiles(dve, NT, [(1, sums), (2, finish)])
                dve.wait_ge(finished, NT)
                dve.tensor_tensor(self_l[:, :, :], xl[:, :, D:W], arf[:, :, :], ALU.add).then_inc(self_, 1)
                dve.wait_ge(self_, 1)
                dve.tensor_tensor(first[:, :, :], self_l[:, :, :], mags[:, :, :], ALU.add).then_inc(self_, 1)
                dve.wait_ge(self_, 2)
                dve.tensor_copy(topb[:, :, :], first[:, :, :]).then_inc(self_, 1)
                dve.wait_ge(self_, 3)
                dve.tensor_copy(top[:, :, :], topb[:, :, :])
                dve.tensor_tensor(gap[:, :, :], first[:, :, :], topb[:, :, :], ALU.subtract).then_inc(self_, 1)
                dve.wait_ge(exped, 1)
                for i in range(heads):
                    at = i * (ch + 1)
                    dve.tensor_tensor(acc[:, :, at:at + ch], xl[:, :, i * ch:(i + 1) * ch],
                                      weight[:, :, i:i + 1].to_broadcast([P, NT, ch]), ALU.mult)
                    dve.tensor_copy(acc[:, :, at + ch + junk:at + ch + junk + 1], weight[:, :, i:i + 1])


def gat_output(nc, co, name, acc, bias, heads, there, elu):
    ch = D // heads
    junk = acc.shape[2] - heads * (ch + 1)
    C = 5
    with phase(co, name) as ph:
        b = ph.sb("b", [P, 1, D])
        inv = ph.sb("inv", [P, NT, heads])
        o, low, high = ph.sb("o", [P, C, D]), ph.sb("low", [P, C, D]), ph.sb("high", [P, C, D])
        loaded, inverse, scaled, biased, lowered, exped, done = (ph.sem(n) for n in (
            "loaded", "inverse", "scaled", "biased", "lowered", "exped", "done"))
        with nc.Block() as block:
            @block.sync
            def _(sp):
                sp.dma_start(b[:, 0, :], row_on_all(bias, D)).then_inc(loaded, 16)

            @block.vector
            def _(dve):
                wide = acc[:, :, 0:heads * (ch + 1)].rearrange("p t (h c) -> p t h c", h=heads)
                sums = acc[:, :, D + junk:D + junk + 1] if heads == 1 else wide[:, :, :, ch]
                dve.reciprocal(inv[:, :, :], sums).then_inc(inverse, 1)
                dve.wait_ge(inverse, 1)
                dve.wait_ge(loaded, 16)

                def scale(t, _):
                    at_least(dve, done, t)
                    for i in range(heads):
                        last = dve.tensor_tensor(o[:, :, i * ch:(i + 1) * ch], acc[:, bass.ds(t * C, C), i * (ch + 1):i * (ch + 1) + ch],
                                                 inv[:, bass.ds(t * C, C), i:i + 1].to_broadcast([P, C, ch]), ALU.mult)
                    last.then_inc(scaled, 1)
                    dve.wait_ge(scaled, t + 1)
                    dve.tensor_tensor(o[:, :, :], o[:, :, :], b[:, :, :].to_broadcast([P, C, D]), ALU.add).then_inc(biased, 1)
                    dve.wait_ge(biased, t + 1)
                    if elu:
                        at_least(dve, exped, t)
                        dve.tensor_scalar(low[:, :, :], o[:, :, :], 0.0, None, ALU.min).then_inc(lowered, 1)
                        dve.tensor_scalar(high[:, :, :], o[:, :, :], 0.0, -1.0, ALU.max, ALU.add).then_inc(lowered, 1)
                        dve.wait_ge(exped, t + 1)
                        dve.wait_ge(lowered, 2 * t + 2)
                        dve.tensor_tensor(there[:, bass.ds(t * C, C), :], low[:, :, :], high[:, :, :], ALU.add).then_inc(done, 1)
                    else:
                        at = there[:, bass.ds(t * C, C), :]
                        dve.tensor_tensor(at, at, o[:, :, :], ALU.add).then_inc(done, 1)

                over_tiles(dve, NT // C, [(0, scale)])

            if elu:
                @block.scalar
                def _(act):
                    act.preload_act_table(ACT.Exp)

                    def exp(t, _):
                        act.wait_ge(lowered, 2 * t + 2)
                        act.activation(low[:, :, :], low[:, :, :], ACT.Exp).then_inc(exped, 1)

                    over_tiles(act, NT // C, [(0, exp)])


def store_x(nc, co, out):
    with phase(co, "store") as ph:
        stored = ph.sem("stored")
        with nc.Block() as block:
            @block.sync
            def _(sp):
                sp.dma_start(out[0:(NT - 1) * P, :].rearrange("(t p) d -> p t d", p=P), co.x[:, 0:NT - 1, :]).then_inc(stored, 16)
                sp.dma_start(out[(NT - 1) * P:N, :], co.x[0:LAST, NT - 1, :]).then_inc(stored, 16)
                sp.wait_ge(stored, 32)


def gat_layer(nc, co, name, h, a, layer, heads, there, elu):
    width = D + 2 if heads == 1 else D + heads
    table = nc.dram_tensor(name + "_table", [NPAD, D + heads], F32, kind="Internal").ap()
    with co.scope():
        acc = co.sbuf(name + "_acc", [P, NT, width])
        top = co.sbuf(name + "_top", [P, NT, heads])
        att = co.sbuf(name + "_att", [P, KD, heads])
        r_parts = co.sbuf(name + "_r_parts", [P, NT, 3, D + heads], BF16)
        gat_inputs(nc, co, name + "_in", h, a, layer, heads, table, r_parts, att, acc, top)
        edge_pass(nc, co, name + "_edges", table, acc, top, heads, r_parts=r_parts, att=att)
        gat_output(nc, co, name + "_out", acc, a[f"L1_gnn_b{layer}"], heads, there, elu)


def routed_ffn(nc, co, which, a, picks, tiles, h, buffers):
    table = nc.dram_tensor(f"ffn{which}_table", [NPAD, D], F32, kind="Internal").ap()
    result = nc.dram_tensor(f"ffn{which}_result", [tiles * P, D], F32, kind="Internal").ap()
    ids = nc.dram_tensor(f"ffn{which}_ids", [tiles * P], F32, kind="Internal").ap()
    with co.scope():
        slot = co.sbuf(f"slot{which}", [P, picks, NT], U32)
        weight = co.sbuf(f"weight{which}", [P, picks, NT])
        token = co.sbuf(f"token{which}", [P, tiles], U32)
        expert = co.sbuf(f"expert{which}", [1, tiles + ROUNDS], I32)
        with co.scope():
            logits = co.sbuf(f"logits{which}", [P, NT, EXP])
            h = co.sbuf("ffn_h", [P, NT, D]) if h is None else h
            layer_norm(nc, co, f"ffn_norm{which}", co.x, h)
            if which == 0:
                top1_logits(nc, co, h, a, logits, table)
                route(nc, co, "route0", logits, picks, tiles, ids, weight, slot, token, expert)
            else:
                top2_logits(nc, co, h, a, logits)
                fetch_experts(nc, co, 1, a, buffers)
                layer_norm(nc, co, "expert_norm", h, h)
                route(nc, co, "route1", logits, picks, tiles, ids, weight, slot, token, expert, h, table)
        experts(nc, co, f"exp{which}", tiles, table, result, token, expert, buffers, a)
        combine(nc, co, f"combine{which}", picks, result, slot, weight)


def attention_block(nc, co, a, xn, base):
    table = nc.dram_tensor("attention_table", [NPAD, D], F32, kind="Internal").ap()
    with co.scope():
        q_parts = co.sbuf("q_parts", [P, NT, 3, D + 1], BF16)
        acc = co.sbuf("acc", [P, NT, D + 1])
        top = co.sbuf("top", [P, NT, 1])
        layer_norm(nc, co, "attention_norm", co.x, xn)
        attention_inputs(nc, co, xn, a, q_parts, base, table, acc, top)
        edge_pass(nc, co, "dot_edges", table, acc, top, 1, q_parts=q_parts)
        attention_output(nc, co, acc, base, a)


def attention_rest(nc, co, a, xn, base):
    layer_norm(nc, co, "inner_norm1", base, xn)
    attention_ffn(nc, co, xn, base, a)
    layer_norm(nc, co, "inner_norm2", base, xn)
    add_affine(nc, co, xn, a["L0_gnn_g2"], a["L0_gnn_b2"])


def build(nc, a, out):
    co = Core(nc)
    dram = lambda n, shape, dt=F32: nc.dram_tensor(n, shape, dt, kind="Internal").ap()
    sdst, ssrc, sweight = dram("sorted_dst", [EPAD], I32), dram("sorted_src", [EPAD], U32), dram("sorted_weight", [EPAD])
    a["b1_parts"] = dram("b1_parts", [3, EXP * HID1], BF16)
    with co.keep:
        constants(nc, co)
        split_bias(nc, co, a["L1_ffn_b1"].rearrange("e d -> (e d)"), a["b1_parts"])
        load_x(nc, co, a["x"])
        with co.scope():
            sort_edges(nc, co, a["dst"], a["src"], a["edge_weight"], sdst, ssrc, sweight)
            plan_steps(nc, co, sdst, ssrc, sweight, a["L0_gnn_we"], a["L0_gnn_be"])
            with co.scope():
                xn = co.sbuf("xn", [P, NT, D])
                base = co.sbuf("base", [P, NT, D])
                attention_block(nc, co, a, xn, base)
                buffers = expert_buffers(co, 0)
                fetch_experts(nc, co, 0, a, buffers)
                attention_rest(nc, co, a, xn, base)
                routed_ffn(nc, co, 0, a, 1, TOP1_TILES, xn, buffers)
            with co.scope():
                h = co.sbuf("gat_h", [P, NT, D])
                layer_norm(nc, co, "gat_norm", co.x, h)
                gat_layer(nc, co, "gat1", h, a, 1, 4, h, True)
                gat_layer(nc, co, "gat2", h, a, 2, 1, co.x, False)
        routed_ffn(nc, co, 1, a, 2, TOP2_TILES, None, expert_buffers(co, 1))
        store_x(nc, co, out)


def kernel(**inputs):
    import concourse.bacc as bacc
    from concourse.bass_utils import run_bass_kernel_spmd as run

    nc = bacc.Bacc("TRN2", target_bir_lowering=False, num_devices=1)
    arrays = {k: np.ascontiguousarray(v) for k, v in inputs.items()}
    arrays["src"] = arrays["src"].view(np.uint32)
    arrays["L0_gnn_wk"] = np.ascontiguousarray(arrays["L0_gnn_wk"].T)
    args = {k: nc.dram_tensor(k, v.shape, mybir.dt.from_np(v.dtype), kind="ExternalInput").ap() for k, v in arrays.items()}
    out = nc.dram_tensor("out", (N, D), F32, kind="ExternalOutput").ap()
    build(nc, args, out)
    got = run(nc, [arrays], core_ids=[0])
    return got.results[0]["out"]
```
